# Optimizing a Trainium2 kernel written in Bass

```python
import numpy as np
import jax
import jax.numpy as jnp

def _softmax(x, axis=-1):
    return jax.nn.softmax(x, axis=axis)

def _gelu(x):
    return jax.nn.gelu(x, approximate=True)

def _silu(x):
    return jax.nn.silu(x)

def _sigmoid(x):
    return jax.nn.sigmoid(x)

def _layernorm(x, axis=-1, eps=1e-05):
    m = jnp.mean(x, axis=axis, keepdims=True)
    v = jnp.var(x, axis=axis, keepdims=True)
    return (x - m) / jnp.sqrt(v + eps)

def _scatter_add(tgt, idx, src, axis=0):
    return tgt.at[idx].add(src)

def _segment_sum(src, seg, n):
    return jax.ops.segment_sum(src, seg, n)
kernel_name = 'mk_adaln_d1_jaxref_r8_6dfbe1'

def setup_inputs(seed: int=0):
    np.random.seed(seed)
    _w = jnp.asarray

    def _L0_attn_setup():
        import jax, jax.numpy as jnp
        import numpy as np
        DIM = 128
        NUM_HEAD = 16
        DIM_HEAD = DIM // NUM_HEAD
        RMS_EPS = 1.1920929e-07
        EPS_LIN = 1e-06
        THETA = 10000.0

        def rmsnorm(x, g, eps=RMS_EPS):
            return x * jax.lax.rsqrt(jnp.mean(x * x, axis=-1, keepdims=True) + eps) * g

        def rope_cos_sin(seq_len, dim_head, dtype=jnp.float32):
            inv_freq = 1.0 / THETA ** (jnp.arange(0, dim_head, 2, dtype=dtype) / dim_head)
            t = jnp.arange(seq_len, dtype=dtype)
            freqs = jnp.outer(t, inv_freq)
            return (jnp.cos(freqs), jnp.sin(freqs))

        def apply_rope(t, cos, sin):
            tr = t[..., 0::2]
            ti = t[..., 1::2]
            out_r = tr * cos - ti * sin
            out_i = tr * sin + ti * cos
            return jnp.stack([out_r, out_i], axis=-1).reshape(t.shape)
        key = jax.random.key(seed)
        ks = jax.random.split(key, 5)
        B, L = (4, 512)
        x = jax.random.normal(ks[0], (B, L, DIM), dtype=jnp.float32)
        Wqkv = jax.random.normal(ks[1], (3 * DIM, DIM), dtype=jnp.float32) * 0.02
        bqkv = jax.random.normal(ks[2], (3 * DIM,), dtype=jnp.float32) * 0.02
        gq = jnp.ones((DIM,), dtype=jnp.float32)
        gk = jnp.ones((DIM,), dtype=jnp.float32)
        Wout = jax.random.normal(ks[3], (DIM, DIM), dtype=jnp.float32) * 0.02
        bout = jax.random.normal(ks[4], (DIM,), dtype=jnp.float32) * 0.02
        gout = jnp.ones((DIM,), dtype=jnp.float32)
        return {'x': x, 'Wqkv': Wqkv, 'bqkv': bqkv, 'gq': gq, 'gk': gk, 'Wout': Wout, 'bout': bout, 'gout': gout}
    _L0_attn_in = _L0_attn_setup()

    def _L0_ffn_setup():
        import jax, jax.numpy as jnp
        import numpy as np
        D_MODEL = 128
        D_FFN = 256
        N_EXPERTS = 8
        TOP_K = 2
        B, S = (2, 256)
        LN_EPS = 1e-05
        key = jax.random.key(seed)
        ks = jax.random.split(key, 6)
        scale = 0.02
        x = jax.random.normal(ks[0], (B, S, D_MODEL), dtype=jnp.float32)
        w_router = jax.random.normal(ks[1], (N_EXPERTS, D_MODEL), dtype=jnp.float32) * scale
        w_gate = jax.random.normal(ks[2], (N_EXPERTS, D_FFN, D_MODEL), dtype=jnp.float32) * scale
        w_up = jax.random.normal(ks[3], (N_EXPERTS, D_FFN, D_MODEL), dtype=jnp.float32) * scale
        w_down = jax.random.normal(ks[4], (N_EXPERTS, D_MODEL, D_FFN), dtype=jnp.float32) * scale
        ln_gamma = jnp.ones((D_MODEL,), dtype=jnp.float32)
        ln_beta = jnp.zeros((D_MODEL,), dtype=jnp.float32)
        return {'x': x, 'w_router': w_router, 'w_gate': w_gate, 'w_up': w_up, 'w_down': w_down, 'ln_gamma': ln_gamma, 'ln_beta': ln_beta}
    _L0_ffn_in = _L0_ffn_setup()
    _L0_c = _w((lambda *s: np.random.randn(*s).astype(np.float32) * 0.05)(4, 128))
    _L0_wmod = _w((lambda *s: np.random.randn(*s).astype(np.float32) * 0.05)(128, 6 * 128) * 128 ** (-0.5))
    _d = {'L0_attn_x': _L0_attn_in['x'], 'L0_attn_Wqkv': _L0_attn_in['Wqkv'], 'L0_attn_bqkv': _L0_attn_in['bqkv'], 'L0_attn_gq': _L0_attn_in['gq'], 'L0_attn_gk': _L0_attn_in['gk'], 'L0_attn_Wout': _L0_attn_in['Wout'], 'L0_attn_bout': _L0_attn_in['bout'], 'L0_attn_gout': _L0_attn_in['gout'], 'L0_ffn_w_router': _L0_ffn_in['w_router'], 'L0_ffn_w_gate': _L0_ffn_in['w_gate'], 'L0_ffn_w_up': _L0_ffn_in['w_up'], 'L0_ffn_w_down': _L0_ffn_in['w_down'], 'L0_ffn_ln_gamma': _L0_ffn_in['ln_gamma'], 'L0_ffn_ln_beta': _L0_ffn_in['ln_beta'], 'L0_c': _L0_c, 'L0_wmod': _L0_wmod}
    _x0 = _d['L0_attn_x']
    _d['L0_attn_x'] = jax.random.normal(jax.random.fold_in(jax.random.key(seed), 1), (4, 512, 128), dtype=_x0.dtype)
    del _x0
    return _d

def reference(L0_attn_x, L0_attn_Wqkv, L0_attn_bqkv, L0_attn_gq, L0_attn_gk, L0_attn_Wout, L0_attn_bout, L0_attn_gout, L0_ffn_w_router, L0_ffn_w_gate, L0_ffn_w_up, L0_ffn_w_down, L0_ffn_ln_gamma, L0_ffn_ln_beta, L0_c, L0_wmod):

    def _L0_attn_ref(x, Wqkv, bqkv, gq, gk, Wout, bout, gout):
        import jax, jax.numpy as jnp
        import numpy as np
        DIM = 128
        NUM_HEAD = 16
        DIM_HEAD = DIM // NUM_HEAD
        RMS_EPS = 1.1920929e-07
        EPS_LIN = 1e-06
        THETA = 10000.0

        def rmsnorm(x, g, eps=RMS_EPS):
            return x * jax.lax.rsqrt(jnp.mean(x * x, axis=-1, keepdims=True) + eps) * g

        def rope_cos_sin(seq_len, dim_head, dtype=jnp.float32):
            inv_freq = 1.0 / THETA ** (jnp.arange(0, dim_head, 2, dtype=dtype) / dim_head)
            t = jnp.arange(seq_len, dtype=dtype)
            freqs = jnp.outer(t, inv_freq)
            return (jnp.cos(freqs), jnp.sin(freqs))

        def apply_rope(t, cos, sin):
            tr = t[..., 0::2]
            ti = t[..., 1::2]
            out_r = tr * cos - ti * sin
            out_i = tr * sin + ti * cos
            return jnp.stack([out_r, out_i], axis=-1).reshape(t.shape)
        B, L, D = x.shape
        qkv = x @ Wqkv.T + bqkv
        q, k, v = jnp.split(qkv, 3, axis=-1)
        q = rmsnorm(q, gq)
        k = rmsnorm(k, gk)
        split = lambda t: t.reshape(B, L, NUM_HEAD, DIM_HEAD).transpose(0, 2, 1, 3)
        q, k, v = (split(q), split(k), split(v))
        cos, sin = rope_cos_sin(L, DIM_HEAD)
        cos = cos[None, None]
        sin = sin[None, None]
        q = apply_rope(q, cos, sin)
        k = apply_rope(k, cos, sin)
        qf = jax.nn.relu(q)
        kf = jax.nn.relu(k)
        vpad = jnp.concatenate([v, jnp.ones_like(v[..., :1])], axis=-1)
        vk = jnp.einsum('bhlp,bhld->bhpd', vpad, kf)
        res = jnp.einsum('bhpd,bhld->bhlp', vk, qf)
        attn = res[..., :-1] / (res[..., -1:] + EPS_LIN)
        attn = attn.transpose(0, 2, 1, 3).reshape(B, L, D)
        out = rmsnorm(attn @ Wout.T + bout, gout)
        return out

    def _L0_ffn_ref(x, w_router, w_gate, w_up, w_down, ln_gamma, ln_beta):
        import jax, jax.numpy as jnp
        import numpy as np
        D_MODEL = 128
        D_FFN = 256
        N_EXPERTS = 8
        TOP_K = 2
        B, S = (2, 256)
        LN_EPS = 1e-05
        logits = jnp.einsum('bsd,ed->bse', x, w_router)
        top_vals, top_idx = jax.lax.top_k(logits, TOP_K)
        rw = jax.nn.softmax(top_vals, axis=-1)
        gate = jnp.einsum('bsd,efd->ebsf', x, w_gate)
        up = jnp.einsum('bsd,efd->ebsf', x, w_up)
        h = jax.nn.silu(gate) * up
        y = jnp.einsum('ebsf,edf->bsed', h, w_down)
        sel = jnp.take_along_axis(y, top_idx[..., None], axis=2)
        out = jnp.sum(rw[..., None] * sel, axis=2)
        mu = jnp.mean(out, axis=-1, keepdims=True)
        var = jnp.mean(jnp.square(out - mu), axis=-1, keepdims=True)
        out = (out - mu) * jax.lax.rsqrt(var + LN_EPS)
        return out * ln_gamma + ln_beta
    x = L0_attn_x
    mod = (_silu(L0_c) @ L0_wmod).reshape(L0_c.shape[0], 6, 1, -1)
    sa, ca, ga, sb, cb, gb = (mod[:, 0], mod[:, 1], mod[:, 2], mod[:, 3], mod[:, 4], mod[:, 5])
    ga = (2 * (ga >= 0) - 1) * jnp.maximum(jnp.abs(ga), 0.25)
    gb = (2 * (gb >= 0) - 1) * jnp.maximum(jnp.abs(gb), 0.25)
    h = _layernorm(x, axis=-1) * (1 + ca) + sa
    x = x + ga * _L0_attn_ref(h, L0_attn_Wqkv, L0_attn_bqkv, L0_attn_gq, L0_attn_gk, L0_attn_Wout, L0_attn_bout, L0_attn_gout)
    h = _layernorm(x, axis=-1) * (1 + cb) + sb
    x = x + gb * _L0_ffn_ref(h, L0_ffn_w_router, L0_ffn_w_gate, L0_ffn_w_up, L0_ffn_w_down, L0_ffn_ln_gamma, L0_ffn_ln_beta)
    return x

_drawn_inputs = setup_inputs


def setup_inputs(seed=0):
    import zlib

    import numpy as np

    out = dict(_drawn_inputs(seed))
    spreads = {'L0_attn_gq': (1.0, 0.6),
     'L0_attn_gk': (1.0, 0.6),
     'L0_attn_gout': (1.0, 0.2),
     'L0_ffn_ln_gamma': (1.0, 0.2),
     'L0_ffn_ln_beta': (0.0, 0.334)}
    factors = {}
    for name, (base, spread) in spreads.items():
        noise = np.random.default_rng([zlib.crc32(name.encode()), seed]).standard_normal(out[name].shape)
        drawn = base * np.exp(spread * noise) if base else spread * noise
        out[name] = jnp.asarray(drawn.astype(out[name].dtype))
    for name, factor in factors.items():
        out[name] = (out[name] * factor).astype(out[name].dtype)
    return out
```

```python
import concourse.bass as bass
from concourse import mybir
from contextlib import ExitStack

P = 128
B, L, D = 4, 512, 128
NT = L // P
TOKENS = B * L
TT = TOKENS // P
H, DH = 16, 8
NE, FF, TOPK = 8, 256, 2
FB = FF // P
RMS_EPS = 1.1920929e-07
LIN_EPS = 1e-06
LN_EPS = 1e-05
THETA = 10000.0

REGION = TOKENS + P
DEAD_ROW = NE * REGION
TILES = TOPK * TT + NE - 1
STAGES = 4
RING = 4
TURNS = (TILES - STAGES + 1) // RING
assert TURNS * RING == TILES - STAGES + 1
REC = D + 2
SKIP = 1 << 20

C_ID = 0
C_BLK = C_ID + P
C_HEAD = C_BLK + D
C_UP = C_HEAD + H
C_EXP = C_UP + P
C_BASE = C_EXP + NE
C_COS = C_BASE + NE
C_SIN = C_COS + NT * D
C_SEL = C_SIN + NT * D
C_TILE = C_SEL + B * P
C_ALL = C_TILE + TILES * NE

V_BQKV, V_BOUT, V_GQ, V_GK, V_GOUT, V_GAMMA, V_BETA = 0, 384, 512, 640, 768, 896, 1024
V_ALL = 1152


def adaln_block(nc, x, wqkv, wout, wrouter, wgu, wdown, wmod, cond, vecs, consts, dests, out):
    F32 = mybir.dt.float32
    BF16 = mybir.dt.bfloat16
    I32 = mybir.dt.int32
    U32 = mybir.dt.uint32
    ALU = mybir.AluOpType
    ACT = mybir.ActivationFunctionType
    AX = mybir.AxisListType

    sorted_rows = nc.dram_tensor("sorted_rows", [DEAD_ROW + P, REC], F32).ap()
    expert_rows = nc.dram_tensor("expert_rows", [TOPK * TOKENS, D], F32).ap()
    x_v = x.rearrange("(t p) d -> p t d", p=P)
    out_v = out.rearrange("(t p) d -> p t d", p=P)
    rows_v = expert_rows.rearrange("(k t p) d -> p k t d", k=TOPK, p=P)

    ctx = ExitStack()
    with ctx:
        def sb(name, shape, dt=F32):
            return ctx.enter_context(nc.sbuf_tensor(name, shape, dt))

        def pb(name):
            return ctx.enter_context(nc.psum_tensor(name, [P, 512], F32))

        def sem(name):
            return ctx.enter_context(nc.semaphore(name))

        x_sb = sb("x_sb", [P, TT, D])
        x2 = sb("x2", [P, TT, D])
        cst = sb("cst", [P, C_ALL])
        dest_sb = sb("dest_sb", [P, TT, TOPK])
        vec_row = sb("vec_row", [P, V_ALL])
        wqkv_sb = sb("wqkv_sb", [P, 3 * D])
        wout_sb = sb("wout_sb", [P, D])
        wr_sb = sb("wr_sb", [P, NE])
        wgu_sb = sb("wgu_sb", [P, NE, 2 * FF])
        wd_sb = sb("wd_sb", [P, NE, FB, D])
        wmod_sb = sb("wmod_sb", [P, 6 * D])
        cond_sb = sb("cond_sb", [P, B])
        scond = sb("scond", [P, B])
        ones = sb("ones", [P, P])
        ones16 = sb("ones16", [P, P], BF16)
        up16 = sb("up16", [P, P], BF16)
        neg_half = sb("neg_half", [P, 8])
        gswap = sb("gswap", [P, 2, D])
        rope_c = sb("rope_c", [P, NT, 2, D])
        rope_s = sb("rope_s", [P, NT, 2, D])
        sa_col = sb("sa_col", [P, B])
        ca_col = sb("ca_col", [P, B])
        mod4 = sb("mod4", [B, 6 * D])
        mod_sgn = sb("mod_sgn", [B, 2, D])
        mod_mag = sb("mod_mag", [B, 2, D])
        bc4 = sb("bc4", [B, 5, D])
        mod_bc = sb("mod_bc", [P, B, 5, D])

        st1 = sb("st1", [P, 2, NT, 6])
        mv1 = sb("mv1", [P, 2, NT, 2])
        ve1 = sb("ve1", [P, 2, NT])
        rs1 = sb("rs1", [P, 2, NT])
        z = sb("z", [P, 2, NT, D])
        hT = sb("hT", [P, 2, L])
        v_sb = sb("v_sb", [P, 2, NT, D + 1])
        qk_sq = sb("qk_sq", [P, NT * 2, D])
        o_sq = sb("o_sq", [P, NT, D])
        ssq = sb("ssq", [P, 2, NT * 2])
        msq = sb("msq", [P, 2, NT * 2])
        rqk = sb("rqk", [P, 2, NT * 2])
        qk_sb = sb("qk_sb", [P, 2, NT, 2, D])
        o_sb = sb("o_sb", [P, 2, NT, D])
        ra = sb("ra", [P, 2, NT, 2, D])
        rb = sb("rb", [P, 2, NT, 2, D])
        qkf = sb("qkf", [P, 2, NT, 2, D])
        qfT = sb("qfT", [P, 2, L])
        kv = sb("kv", [P, 2, D + H])
        den = sb("den", [P, 2, NT, H])
        rden = sb("rden", [P, 2, NT, H])
        attn = sb("attn", [P, 2, NT, D])
        attnT = sb("attnT", [P, 2, L])
        oss = sb("oss", [P, 2, NT])
        oms = sb("oms", [P, 2, NT])
        ors = sb("ors", [P, 2, NT])
        og = sb("og", [P, NT, D])
        st2 = sb("st2", [P, NT, 6])
        mv2 = sb("mv2", [P, 2, NT, 2])
        ve2 = sb("ve2", [P, 2, NT])
        rs2 = sb("rs2", [P, 2, NT])
        h2c = sb("h2c", [P, NT, D])
        rec = sb("rec", [P, 2, NT, TOPK, REC])
        h2T = sb("h2T", [P, 2, L])
        lg = sb("lg", [P, NT, NE])
        top = sb("top", [P, NT, 8])
        topi = sb("topi", [P, NT, 8], U32)
        topf = sb("topf", [P, NT, TOPK])
        gap = sb("gap", [P, NT, TOPK])
        onehot = sb("onehot", [P, NT, TOPK, NE])
        sel16 = sb("sel16", [P, NT, NE], BF16)
        selsum = sb("selsum", [P, NE])
        carry = sb("carry", [P, NE])
        carry16 = sb("carry16", [P, NE], BF16)
        pos = sb("pos", [P, NT, NE])
        posk = sb("posk", [P, NT, TOPK, NE])
        slot = sb("slot", [P, 2, NT, TOPK], U32)
        pad = sb("pad", [P, REC])
        cnt_i = sb("cnt_i", [1, NE], I32)
        cnt_p = sb("cnt_p", [1, NE], I32)
        nt_i = sb("nt_i", [1, NE], I32)
        nt_f = sb("nt_f", [1, NE])
        nt_one = sb("nt_one", [1, NE])
        nt_cum = sb("nt_cum", [1, NE])
        past = sb("past", [1, TILES, NE])
        pastn = sb("pastn", [1, TILES, NE])
        ex_f = sb("ex_f", [1, TILES])
        before = sb("before", [1, TILES])
        ahead = sb("ahead", [1, TILES])
        row_f = sb("row_f", [1, TILES])
        tile_tab = sb("tile_tab", [1, 2, TILES], I32)

        xt = sb("xt", [P, RING, REC])
        xT = sb("xT", [P, 2, P])
        gact = sb("gact", [P, 2, FF])
        hid = sb("hid", [P, 2, FF])
        hidT = sb("hidT", [P, 2, FF])
        yrow = sb("yrow", [P, RING, D])
        ydest = sb("ydest", [P, RING, 1], U32)

        yk = qk_sb[:].rearrange("p b t q d -> p b (t q) d").rearrange("p b (k t) d -> p b k t d", k=TOPK)
        ysum = attn
        st3 = sb("st3", [P, 2, NT, 6])
        mv3 = sb("mv3", [P, 2, NT, 2])
        ve3 = sb("ve3", [P, 2, NT])
        rs3 = sb("rs3", [P, 2, NT])
        fin = z
        res = sb("res", [P, 2, NT, D])

        bank = [pb(f"bank{i}") for i in range(6)]
        qk_ps = ctx.enter_context(nc.psum_tensor("qk_ps", [P, NT, 2, D], F32))
        ta_ps, tb_ps, v_ps, n_ps, m_ps, w_ps = bank
        VK, DEN = 0, 160
        LG, RK, CNT = 0, 64, 128

        s = {n: sem(n) for n in (
            "ld_x0 ld_x1 ld_x2 ld_x3 ld_cst ld_vec ld_cond ld_mod ld_qkv ld_out ld_wr ld_dest ld_gu ld_down "
            "scond_ok const_ok half_ok up_ok gswap_ok rope_ok modcol_ps modcol_ok mod4_ps mod4_ok sgn_ok mag_ok "
            "bc4_ok modbc_ps modbc_ok clamp_ok vone_ok "
            "st1_ok mv1_ok ve1_ok rs1_ok z_ok zT_ps hT_ok qkv_ps v_ok ssq_ok msq_ok rqk_ok ra_ok rot_ok qkf_ok "
            "vk_ps qT_ps qfT_ok kv_ok res_ps den_ok rden_ok attn_ok aT_ps attnT_ok o_ps oss_ok oms_ok ors_ok og_ok "
            "x2_ok st2_ok mv2_ok ve2_ok rs2_ok h2c_ok h2_ok dup_ok h2T_ps h2T_ok lg_ps lg_ok top_ok topi_ok topf_ok gap_ok wt_ok "
            "onehot_ok sel_ok selsum_ok carry_ok carry16_ok rank_ps pos_ok posk_ok slot_ok pad_ok pad_dest_ok "
            "scat0 scat1 cnt_ps cnt_ok nt1 nt2 nt3 nt4 nt5 past_ok pastn_ok ex_ok before_ok ahead_ok row_ok tab_ok pads_out "
            "dest_ok xT_ps xT_ok gu_ps gact_ok hid_ok hidT_ps hidT_ok y_ps yrow_ok ydest_ok y_seen qk_ok o_ok modrow4_ps modrow4_ok "
            "ysum_ok st3_ok mv3_ok ve3_ok rs3_ok fin_ok res_ok").split()}
        ld_tile = [sem(f"ld_tile{q}") for q in range(RING)]
        y_out = [sem(f"y_out{q}") for q in range(RING)]
        stored = [sem(f"stored{h}") for h in range(2)]
        ld_y = [sem(f"ld_y{b}") for b in range(B)]
        block = ctx.enter_context(nc.Block())

        ident = cst[:, C_ID:C_ID + P]

        xT_bank, g_bank, hT_bank, y_bank = (ta_ps, tb_ps), (v_ps, n_ps), (m_ps, w_ps), (qk_ps[:, 0:2], qk_ps[:, 2:4])

        def tile_of(turn, c):
            return turn * RING + c, c % RING, c % 2, turn + c // RING

        def steps(engine, stages):
            def step(turn, n):
                for k, stage in stages:
                    if not isinstance(turn, int) or 0 <= n - k < TILES:
                        stage(turn, n - k)
            for n in range(STAGES - 1 + RING):
                step(0, n)
            with engine.Fori(1, TURNS) as turn:
                for v in range(RING):
                    step(turn, STAGES - 1 + v)
            for n in range(TILES, TILES + STAGES - 1):
                step(0, n)

        def used_before(engine, sem, value):
            if not isinstance(value, int) or value > 0:
                engine.wait_ge(sem, value)

        @block.sync
        def _(sp):
            sp.dma_start(x_sb[:, 0:NT, :], x_v[:, 0:NT, :]).then_inc(s["ld_x0"], 16)
            sp.dma_start(cst[:], consts).then_inc(s["ld_cst"], 16)
            sp.dma_start(wqkv_sb[:], wqkv).then_inc(s["ld_qkv"], 16)
            for b in range(1, B):
                sp.dma_start(x_sb[:, b * NT:(b + 1) * NT, :], x_v[:, b * NT:(b + 1) * NT, :]).then_inc(s[f"ld_x{b}"], 16)
            sp.dma_start(wout_sb[:], wout).then_inc(s["ld_out"], 16)
            sp.dma_start(wr_sb[:], wrouter).then_inc(s["ld_wr"], 16)
            sp.dma_start(dest_sb[:], dests).then_inc(s["ld_dest"], 16)
            sp.dma_start(wgu_sb[:], wgu).then_inc(s["ld_gu"], 16)
            sp.dma_start(wd_sb[:], wdown).then_inc(s["ld_down"], 16)

            sp.wait_ge(s["pad_dest_ok"], 1)
            sp.dma_start(sorted_rows[DEAD_ROW:DEAD_ROW + P, :], pad[:]).then_inc(s["pads_out"], 16)
            sp.wait_ge(s["cnt_ok"], 1)
            for e in range(NE):
                n = sp.value_load(cnt_i[0:1, e:e + 1], min_val=0, max_val=TOKENS)
                sp.dma_start(sorted_rows[bass.ds(n + e * REGION, P), :], pad[:]).then_inc(s["pads_out"], 16)
            sp.wait_ge(s["pads_out"], 16 * (NE + 1))
            sp.wait_ge(s["scat0"], 16 * NT * TOPK * 2)
            sp.wait_ge(s["scat1"], 16 * NT * TOPK * 2)
            sp.wait_ge(s["tab_ok"], 1)

            def load_tile(turn, c):
                j, q, _, _ = tile_of(turn, c)
                row = sp.value_load(tile_tab[0:1, 1, bass.ds(j, 1)], min_val=0, max_val=DEAD_ROW)
                used_before(sp, s["xT_ps"], j - RING + 1)
                used_before(sp, s["hid_ok"], j - RING + 1)
                used_before(sp, s["ydest_ok"], j - RING + 1)
                sp.dma_start(xt[:, q, :], sorted_rows[bass.ds(row, P), :]).then_inc(ld_tile[q], 16)

            steps(sp, [(0, load_tile)])

            for q in range(RING):
                sp.wait_ge(y_out[q], 16 * len(range(q, TILES, RING)))
            for b in range(B):
                if b >= 2:
                    sp.wait_ge(s["ysum_ok"], b - 1)
                for k in range(TOPK):
                    sp.dma_start(yk[:, b % 2, k], rows_v[:, k, b * NT:(b + 1) * NT, :]).then_inc(ld_y[b], 16)
            for b in range(B):
                sp.wait_ge(s["res_ok"], b + 1)
                sp.dma_start(out_v[:, b * NT:(b + 1) * NT, :], res[:, b % 2]).then_inc(stored[b % 2], 16)
            for h in range(2):
                sp.wait_ge(stored[h], 16 * B // 2)

        @block.scalar
        def _(act):
            act.dma_start(cond_sb[:], cond).then_inc(s["ld_cond"], 16)
            act.dma_start(wmod_sb[:], wmod).then_inc(s["ld_mod"], 16)
            act.dma_start(vec_row[:], vecs.to_broadcast([P, V_ALL])).then_inc(s["ld_vec"], 16)
            act.wait_ge(s["ld_cond"], 16)
            nc.scalar.activation(scond[:], cond_sb[:], ACT.Silu).then_inc(s["scond_ok"], 1)
            act.wait_ge(s["mod4_ps"], 1)
            nc.scalar.copy(mod4[:, 0:512], n_ps[0:B, :])
            nc.scalar.copy(mod4[:, 512:6 * D], w_ps[0:B, 0:256]).then_inc(s["mod4_ok"], 1)

            def norm_out(b):
                act.wait_ge(s["zT_ps"], b + 1)
                act.wait_ge(s["modcol_ok"], 1)
                if b >= 2:
                    act.wait_ge(s["qkv_ps"], b - 1)
                nc.scalar.activation(hT[:, b % 2], ta_ps[:], ACT.Identity, bias=sa_col[:, b:b + 1],
                                     scale=ca_col[:, b:b + 1]).then_inc(s["hT_ok"], 1)
                act.wait_ge(s["qkv_ps"], b + 1)
                act.wait_ge(s["vone_ok"], 1)
                if b >= 2:
                    act.wait_ge(s["vk_ps"], b - 1)
                nc.scalar.copy(v_sb[:, b % 2, :, 0:D], v_ps[:].rearrange("p (t d) -> p t d", d=D)).then_inc(s["v_ok"], 1)
                if b >= 2:
                    act.wait_ge(s["ra_ok"], 3 * (b - 1))
                nc.scalar.copy(qk_sb[:, b % 2], qk_ps[:]).then_inc(s["qk_ok"], 1)
                act.wait_ge(s["qk_ok"], b + 1)
                if b >= 1:
                    act.wait_ge(s["ssq_ok"], b)
                if b >= 2:
                    act.wait_ge(s["msq_ok"], b - 1)
                for i in range(NT):
                    for j in range(2):
                        last = nc.scalar.activation(qk_sq[:, 2 * i + j], qk_sb[:, b % 2, i, j, :], ACT.Square,
                                                    accum_out=ssq[:, b % 2, 2 * i + j:2 * i + j + 1])
                last.then_inc(s["ssq_ok"], 1)

            norm_out(0)
            for b in range(B):
                act.wait_ge(s["modbc_ps"], b + 1)
                nc.scalar.copy(mod_bc[:, b, 0:4], (n_ps, w_ps)[b % 2][:].rearrange("p (r d) -> p r d", d=D)).then_inc(s["modbc_ok"], 1)
            act.wait_ge(s["modrow4_ps"], 1)
            nc.scalar.copy(mod_bc[:, :, 4], tb_ps[:].rearrange("p (b d) -> p b d", d=D)).then_inc(s["modrow4_ok"], 1)

            for b in range(B + 1):
                if b < B:
                    act.wait_ge(s["qT_ps"], b + 1)
                    if b >= 2:
                        act.wait_ge(s["res_ps"], b - 1)
                    nc.scalar.copy(qfT[:, b % 2], ta_ps[:]).then_inc(s["qfT_ok"], 1)
                if b >= 1:
                    p = b - 1
                    act.wait_ge(s["h2_ok"], b)
                    if p >= 2:
                        act.wait_ge(s[f"scat{p % 2}"], 16 * NT * TOPK * (p // 2))
                    nc.scalar.copy(rec[:, p % 2, :, 1, 0:D], rec[:, p % 2, :, 0, 0:D]).then_inc(s["dup_ok"], 1)
                    act.wait_ge(s["h2T_ps"], b)
                    if p >= 2:
                        act.wait_ge(s["lg_ps"], p - 1)
                    nc.scalar.copy(h2T[:, p % 2], tb_ps[:]).then_inc(s["h2T_ok"], 1)
                if b + 1 < B:
                    norm_out(b + 1)
                if b >= 1:
                    act.wait_ge(s["gap_ok"], 2 * b)
                    nc.scalar.activation(rec[:, p % 2, :, :, D], gap[:], ACT.Sigmoid).then_inc(s["wt_ok"], 1)
                if b < B:
                    act.wait_ge(s["aT_ps"], b + 1)
                    if b >= 2:
                        act.wait_ge(s["o_ps"], b - 1)
                    nc.scalar.copy(attnT[:, b % 2], tb_ps[:]).then_inc(s["attnT_ok"], 1)
                    act.wait_ge(s["o_ps"], b + 1)
                    if b >= 2:
                        act.wait_ge(s["og_ok"], b - 1)
                    nc.scalar.copy(o_sb[:, b % 2].rearrange("p t d -> p (t d)"), n_ps[:]).then_inc(s["o_ok"], 1)
                    act.wait_ge(s["o_ok"], b + 1)
                    if b >= 1:
                        act.wait_ge(s["oss_ok"], b)
                    if b >= 2:
                        act.wait_ge(s["oms_ok"], b - 1)
                    for i in range(NT):
                        last = nc.scalar.activation(o_sq[:, i], o_sb[:, b % 2, i], ACT.Square,
                                                    accum_out=oss[:, b % 2, i:i + 1])
                    last.then_inc(s["oss_ok"], 1)

            def x_back(turn, c):
                j, _, h, _ = tile_of(turn, c)
                act.wait_ge(s["xT_ps"], j + 1)
                used_before(act, s["gu_ps"], j - 1)
                nc.scalar.copy(xT[:, h, :], xT_bank[h][:, 0:P]).then_inc(s["xT_ok"], 1)

            def gate(turn, c):
                j, _, h, _ = tile_of(turn, c)
                act.wait_ge(s["gu_ps"], j + 1)
                used_before(act, s["hid_ok"], j - 1)
                nc.scalar.activation(gact[:, h, :], g_bank[h][:, 0:FF], ACT.Silu).then_inc(s["gact_ok"], 1)

            def hid_back(turn, c):
                j, _, h, _ = tile_of(turn, c)
                act.wait_ge(s["hidT_ps"], j + 1)
                used_before(act, s["y_ps"], j - 1)
                nc.scalar.copy(hidT[:, h, :], hT_bank[h][:, 0:FF]).then_inc(s["hidT_ok"], 1)

            def y_back(turn, c):
                j, q, h, before = tile_of(turn, c)
                act.wait_ge(s["y_ps"], j + 1)
                used_before(act, y_out[q], before * 16)
                nc.scalar.copy(yrow[:, q, :], y_bank[h][:, 0, 0]).then_inc(s["yrow_ok"], 1)

            steps(act, [(0, x_back), (1, gate), (3, y_back), (2, hid_back)])

        @block.gpsimd
        def _(pool):
            nc.gpsimd.memset(neg_half[:], -0.5).then_inc(s["half_ok"], 1)
            nc.gpsimd.memset(v_sb[:, :, :, D:D + 1], 1.0).then_inc(s["vone_ok"], 1)
            nc.gpsimd.memset(pad[:], 0.0).then_inc(s["pad_ok"], 1)
            pool.wait_ge(s["pad_ok"], 1)
            nc.gpsimd.memset(pad[:, D + 1:D + 2], float(SKIP)).then_inc(s["pad_dest_ok"], 1)
            pool.wait_ge(s["half_ok"], 1)

            def inv_sqrt(dst, src, n, ready, done):
                nc.gpsimd.tensor_tensor(dst, src, neg_half[:, 0:n], ALU.pow).then_inc(done, 1)

            def in_norm(b):
                pool.wait_ge(s["ve1_ok"], b + 1)
                if b >= 2:
                    pool.wait_ge(s["z_ok"], b - 1)
                inv_sqrt(rs1[:, b % 2], ve1[:, b % 2], NT, None, s["rs1_ok"])

            def qk_norm(b):
                pool.wait_ge(s["ssq_ok"], b + 1)
                nc.gpsimd.tensor_scalar(msq[:, b % 2], ssq[:, b % 2], 1.0 / D, RMS_EPS, ALU.mult,
                                        ALU.add).then_inc(s["msq_ok"], 1)
                pool.wait_ge(s["msq_ok"], b + 1)
                if b >= 2:
                    pool.wait_ge(s["qkf_ok"], b - 1)
                inv_sqrt(rqk[:, b % 2], msq[:, b % 2], NT * 2, None, s["rqk_ok"])

            in_norm(0)
            qk_norm(0)
            for b in range(B + 1):
                if b >= 1:
                    pool.wait_ge(s["ve2_ok"], b)
                    inv_sqrt(rs2[:, (b - 1) % 2], ve2[:, (b - 1) % 2], NT, None, s["rs2_ok"])
                if b + 1 < B:
                    in_norm(b + 1)
                    qk_norm(b + 1)
                if b < B:
                    pool.wait_ge(s["oss_ok"], b + 1)
                    nc.gpsimd.tensor_scalar(oms[:, b % 2], oss[:, b % 2], 1.0 / D, RMS_EPS, ALU.mult,
                                            ALU.add).then_inc(s["oms_ok"], 1)
                    pool.wait_ge(s["oms_ok"], b + 1)
                    if b >= 2:
                        pool.wait_ge(s["x2_ok"], b - 1)
                    inv_sqrt(ors[:, b % 2], oms[:, b % 2], NT, None, s["ors_ok"])
                if b >= 1:
                    p = b - 1
                    pool.wait_ge(s["slot_ok"], b)
                    pool.wait_ge(s["dup_ok"], b)
                    pool.wait_ge(s["wt_ok"], b)
                    pool.wait_ge(s["dest_ok"], b)
                    for i in range(NT):
                        for k in range(TOPK):
                            nc.gpsimd.indirect_dma_start(
                                out=sorted_rows, out_offset=bass.IndirectOffsetOnAxis(ap=slot[:, p % 2, i, k:k + 1], axis=0),
                                in_=rec[:, p % 2, i, k, :], in_offset=None).then_inc(s[f"scat{p % 2}"], 16)

            last_row = pool.to_reg(TOPK * TOKENS - 1)

            def scatter_back(turn, c):
                j, q, _, _ = tile_of(turn, c)
                pool.wait_ge(s["yrow_ok"], j + 1)
                pool.wait_ge(s["ydest_ok"], j + 1)
                pool.sem_inc(s["y_seen"], 1)
                nc.gpsimd.indirect_dma_start(
                    out=expert_rows, out_offset=bass.IndirectOffsetOnAxis(ap=ydest[:, q, :], axis=0),
                    in_=yrow[:, q, :], in_offset=None, bounds_check=last_row,
                    oob_is_err=False).then_inc(y_out[q], 16)

            steps(pool, [(3, scatter_back)])
            for b in range(B):
                pool.wait_ge(s["ve3_ok"], b + 1)
                if b >= 2:
                    pool.wait_ge(s["res_ok"], b - 1)
                inv_sqrt(rs3[:, b % 2], ve3[:, b % 2], NT, None, s["rs3_ok"])

        @block.vector
        def _(dve):
            v = nc.vector

            def in_norm(b):
                t0 = b * NT
                dve.wait_ge(s[f"ld_x{b}"], 16)
                for i in range(NT):
                    last = v.bn_stats(st1[:, b % 2, i], x_sb[:, t0 + i, :])
                last.then_inc(s["st1_ok"], 1)
                dve.wait_ge(s["st1_ok"], b + 1)
                for i in range(NT):
                    last = v.bn_aggr(mv1[:, b % 2, i], st1[:, b % 2, i])
                last.then_inc(s["mv1_ok"], 1)
                dve.wait_ge(s["mv1_ok"], b + 1)
                v.tensor_scalar_add(ve1[:, b % 2], mv1[:, b % 2, :, 1], LN_EPS).then_inc(s["ve1_ok"], 1)
                dve.wait_ge(s["rs1_ok"], b + 1)
                if b >= 2:
                    dve.wait_ge(s["zT_ps"], b - 1)
                for i in range(NT):
                    last = v.tensor_scalar(z[:, b % 2, i], x_sb[:, t0 + i, :], mv1[:, b % 2, i, 0:1], rs1[:, b % 2, i:i + 1],
                                           ALU.subtract, ALU.mult)
                last.then_inc(s["z_ok"], 1)

            def rotate(b):
                dve.wait_ge(s["qk_ok"], b + 1)
                pairs = lambda ap: ap.rearrange("p (m two) -> p m two", two=2)
                r_a = ra[:, b % 2].rearrange("p t q d -> p (t q d)")
                r_b = rb[:, b % 2].rearrange("p t q d -> p (t q d)")
                qk = qk_sb[:, b % 2].rearrange("p t q d -> p (t q d)")
                rc = rope_c[:].rearrange("p t q d -> p (t q d)")
                rs = rope_s[:].rearrange("p t q d -> p (t q d)")
                v.tensor_tensor(r_a, qk, rc, ALU.mult).then_inc(s["ra_ok"], 1)
                v.tensor_tensor(pairs(r_b)[:, :, 0], pairs(qk)[:, :, 1], pairs(rs)[:, :, 0], ALU.mult).then_inc(s["ra_ok"], 1)
                v.tensor_tensor(pairs(r_b)[:, :, 1], pairs(qk)[:, :, 0], pairs(rs)[:, :, 1], ALU.mult).then_inc(s["ra_ok"], 1)
                dve.wait_ge(s["ra_ok"], 3 * (b + 1))
                v.tensor_tensor(r_a, r_a, r_b, ALU.add).then_inc(s["rot_ok"], 1)
                dve.wait_ge(s["rot_ok"], b + 1)
                dve.wait_ge(s["rqk_ok"], b + 1)
                if b >= 2:
                    dve.wait_ge(s["vk_ps"], b - 1)
                    dve.wait_ge(s["qT_ps"], b - 1)
                v.scalar_tensor_tensor(
                    out=qkf[:, b % 2].rearrange("p t q d -> p (t q) d"), in0=ra[:, b % 2].rearrange("p t q d -> p (t q) d"),
                    scalar=0.0, in1=rqk[:, b % 2].unsqueeze(2).to_broadcast([P, NT * 2, D]),
                    op0=ALU.max, op1=ALU.mult).then_inc(s["qkf_ok"], 1)

            def summary(b):
                dve.wait_ge(s["vk_ps"], b + 1)
                if b >= 2:
                    dve.wait_ge(s["res_ps"], b - 1)
                v.tensor_tensor(kv[:, b % 2, 0:D], m_ps[:, VK:VK + D], cst[:, C_BLK:C_BLK + D], ALU.mult)
                v.tensor_scalar(kv[:, b % 2, D:D + H], cst[:, C_HEAD:C_HEAD + H], m_ps[:, VK + D:VK + D + 1], None,
                                ALU.mult).then_inc(s["kv_ok"], 1)

            def divide(b):
                dve.wait_ge(s["res_ps"], b + 1)
                v.tensor_scalar_add(den[:, b % 2], m_ps[:, DEN:DEN + NT * H].rearrange("p (t h) -> p t h", h=H),
                                    LIN_EPS).then_inc(s["den_ok"], 1)
                dve.wait_ge(s["den_ok"], b + 1)
                v.reciprocal(rden[:, b % 2], den[:, b % 2]).then_inc(s["rden_ok"], 1)
                dve.wait_ge(s["rden_ok"], b + 1)
                if b >= 2:
                    dve.wait_ge(s["aT_ps"], b - 1)
                v.tensor_tensor(attn[:, b % 2].rearrange("p t (h e) -> p (t h) e", e=DH),
                                n_ps[:].rearrange("p (m e) -> p m e", e=DH),
                                rden[:, b % 2].rearrange("p t h -> p (t h)").unsqueeze(2).to_broadcast([P, NT * H, DH]),
                                ALU.mult).then_inc(s["attn_ok"], 1)

            def residual(b):
                t0 = b * NT
                dve.wait_ge(s["o_ok"], b + 1)
                dve.wait_ge(s["modbc_ok"], b + 1)
                v.tensor_tensor(og[:], o_sb[:, b % 2],
                                mod_bc[:, b, 0:1].to_broadcast([P, NT, D]), ALU.mult).then_inc(s["og_ok"], 1)
                dve.wait_ge(s["og_ok"], b + 1)
                dve.wait_ge(s["ors_ok"], b + 1)
                for i in range(NT):
                    last = v.scalar_tensor_tensor(out=x2[:, t0 + i, :], in0=og[:, i, :], scalar=ors[:, b % 2, i:i + 1],
                                                  in1=x_sb[:, t0 + i, :], op0=ALU.mult, op1=ALU.add)
                last.then_inc(s["x2_ok"], 1)
                dve.wait_ge(s["x2_ok"], b + 1)
                for i in range(NT):
                    last = v.bn_stats(st2[:, i], x2[:, t0 + i, :])
                last.then_inc(s["st2_ok"], 1)
                dve.wait_ge(s["st2_ok"], b + 1)
                for i in range(NT):
                    last = v.bn_aggr(mv2[:, b % 2, i], st2[:, i])
                last.then_inc(s["mv2_ok"], 1)
                dve.wait_ge(s["mv2_ok"], b + 1)
                v.tensor_scalar_add(ve2[:, b % 2], mv2[:, b % 2, :, 1], LN_EPS).then_inc(s["ve2_ok"], 1)
                for i in range(NT):
                    last = v.scalar_tensor_tensor(out=h2c[:, i], in0=x2[:, t0 + i, :], scalar=mv2[:, b % 2, i, 0:1],
                                                  in1=mod_bc[:, b, 1], op0=ALU.subtract, op1=ALU.mult)
                last.then_inc(s["h2c_ok"], 1)
                dve.wait_ge(s["h2c_ok"], b + 1)
                dve.wait_ge(s["rs2_ok"], b + 1)
                if b >= 2:
                    dve.wait_ge(s[f"scat{b % 2}"], 16 * NT * TOPK * (b // 2))
                for i in range(NT):
                    last = v.scalar_tensor_tensor(out=rec[:, b % 2, i, 0, 0:D], in0=h2c[:, i], scalar=rs2[:, b % 2, i:i + 1],
                                                  in1=mod_bc[:, b, 2], op0=ALU.mult, op1=ALU.add)
                last.then_inc(s["h2_ok"], 1)

            def choose(b):
                dve.wait_ge(s["lg_ps"], b + 1)
                v.tensor_copy(lg[:], w_ps[:, LG:LG + NT * NE].rearrange("p (t e) -> p t e", e=NE)).then_inc(s["lg_ok"], 1)
                dve.wait_ge(s["lg_ok"], b + 1)
                for i in range(NT):
                    last = v.max(top[:, i], lg[:, i])
                last.then_inc(s["top_ok"], 1)
                dve.wait_ge(s["top_ok"], b + 1)
                for i in range(NT):
                    last = v.max_index(topi[:, i], top[:, i], lg[:, i])
                last.then_inc(s["topi_ok"], 1)
                if b >= 1:
                    dve.wait_ge(s["wt_ok"], b)
                v.tensor_tensor(gap[:, :, 0], top[:, :, 0], top[:, :, 1], ALU.subtract).then_inc(s["gap_ok"], 1)
                v.tensor_tensor(gap[:, :, 1], top[:, :, 1], top[:, :, 0], ALU.subtract).then_inc(s["gap_ok"], 1)
                dve.wait_ge(s["topi_ok"], b + 1)
                v.tensor_copy(topf[:], topi[:, :, 0:TOPK]).then_inc(s["topf_ok"], 1)
                dve.wait_ge(s["topf_ok"], b + 1)
                for k in range(TOPK):
                    last = v.tensor_tensor(onehot[:, :, k, :],
                                           cst[:, C_EXP:C_EXP + NE].unsqueeze(1).to_broadcast([P, NT, NE]),
                                           topf[:, :, k:k + 1].to_broadcast([P, NT, NE]), ALU.is_equal)
                last.then_inc(s["onehot_ok"], 1)
                dve.wait_ge(s["onehot_ok"], b + 1)
                v.tensor_tensor(sel16[:], onehot[:, :, 0], onehot[:, :, 1], ALU.add).then_inc(s["sel_ok"], 1)

            def place(b):
                dve.wait_ge(s["rank_ps"], b + 1)
                v.tensor_tensor(pos[:], w_ps[:, RK:RK + NT * NE].rearrange("p (t e) -> p t e", e=NE),
                                cst[:, C_BASE:C_BASE + NE].unsqueeze(1).to_broadcast([P, NT, NE]), ALU.add).then_inc(s["pos_ok"], 1)
                v.tensor_reduce(selsum[:], sel16[:].rearrange("p t e -> p e t"), AX.X, ALU.add).then_inc(s["selsum_ok"], 1)
                dve.wait_ge(s["pos_ok"], b + 1)
                for k in range(TOPK):
                    last = v.tensor_tensor(posk[:, :, k, :], onehot[:, :, k, :], pos[:], ALU.mult)
                last.then_inc(s["posk_ok"], 1)
                dve.wait_ge(s["selsum_ok"], b + 1)
                v.tensor_tensor(carry[:], carry[:], selsum[:], ALU.add).then_inc(s["carry_ok"], 1)
                dve.wait_ge(s["posk_ok"], b + 1)
                if b >= 2:
                    dve.wait_ge(s[f"scat{b % 2}"], 16 * NT * TOPK * (b // 2))
                with nc.allow_low_precision(reason="row numbers, whole and below 2**24"):
                    v.tensor_reduce(slot[:, b % 2], posk[:], AX.X, ALU.add).then_inc(s["slot_ok"], 1)
                dve.wait_ge(s["carry_ok"], b + 2)
                v.tensor_copy(carry16[:], carry[:]).then_inc(s["carry16_ok"], 1)
                v.tensor_copy(rec[:, b % 2, :, :, D + 1], dest_sb[:, b * NT:(b + 1) * NT, :]).then_inc(s["dest_ok"], 1)

            v.memset(ones[:], 1.0).then_inc(s["const_ok"], 1)
            v.memset(ones16[:], 1.0).then_inc(s["const_ok"], 1)
            v.memset(carry[:], 0.0).then_inc(s["carry_ok"], 1)
            v.memset(carry16[:], 0.0).then_inc(s["carry16_ok"], 1)
            v.memset(nt_one[:], 1.0).then_inc(s["const_ok"], 1)
            in_norm(0)
            dve.wait_ge(s["modcol_ps"], 1)
            v.tensor_copy(sa_col[:], m_ps[:, 0:B])
            v.tensor_scalar_add(ca_col[:], m_ps[:, B:2 * B], 1.0).then_inc(s["modcol_ok"], 1)
            dve.wait_ge(s["ld_vec"], 16)
            dve.wait_ge(s["ld_cst"], 16)
            gqk = vec_row[:, V_GQ:V_GQ + 2 * D].rearrange("p (m two) -> p m two", two=2)
            gsw = gswap[:].rearrange("p q (m two) -> p (q m) two", two=2)
            v.tensor_copy(gsw[:, :, 0], gqk[:, :, 1])
            v.tensor_copy(gsw[:, :, 1], gqk[:, :, 0]).then_inc(s["gswap_ok"], 1)
            for i in range(NT):
                v.tensor_tensor(rope_c[:, i], vec_row[:, V_GQ:V_GQ + 2 * D].rearrange("p (q d) -> p q d", d=D),
                                cst[:, C_COS + i * D:C_COS + (i + 1) * D].unsqueeze(1).to_broadcast([P, 2, D]), ALU.mult)
            dve.wait_ge(s["gswap_ok"], 1)
            for i in range(NT):
                last = v.tensor_tensor(rope_s[:, i], gswap[:],
                                       cst[:, C_SIN + i * D:C_SIN + (i + 1) * D].unsqueeze(1).to_broadcast([P, 2, D]), ALU.mult)
            last.then_inc(s["rope_ok"], 1)
            v.tensor_copy(up16[:], cst[:, C_UP:C_UP + P]).then_inc(s["up_ok"], 1)
            dve.wait_ge(s["mod4_ok"], 1)
            gates = mod4[:].rearrange("b (r d) -> b r d", d=D)[:, 2:6:3]
            v.tensor_scalar(mod_sgn[:], gates, 0.0, 0.5, ALU.is_ge, ALU.subtract).then_inc(s["sgn_ok"], 1)
            v.scalar_tensor_tensor(out=mod_mag[:], in0=gates, scalar=-1.0, in1=gates, op0=ALU.mult,
                                   op1=ALU.max).then_inc(s["mag_ok"], 1)
            dve.wait_ge(s["mag_ok"], 1)
            v.tensor_scalar(mod_mag[:], mod_mag[:], 0.25, 2.0, ALU.max, ALU.mult).then_inc(s["mag_ok"], 1)
            dve.wait_ge(s["sgn_ok"], 1)
            dve.wait_ge(s["mag_ok"], 2)
            v.tensor_tensor(mod_mag[:], mod_sgn[:], mod_mag[:], ALU.mult).then_inc(s["clamp_ok"], 1)
            v.tensor_scalar_add(bc4[:, 1], mod4[:, 4 * D:5 * D], 1.0)
            v.tensor_copy(bc4[:, 2], mod4[:, 3 * D:4 * D])
            dve.wait_ge(s["clamp_ok"], 1)
            v.tensor_tensor(bc4[:, 0], mod_mag[:, 0], vec_row[0:B, V_GOUT:V_GOUT + D], ALU.mult)
            v.tensor_tensor(bc4[:, 3], mod_mag[:, 1], vec_row[0:B, V_GAMMA:V_GAMMA + D], ALU.mult)
            v.tensor_tensor(bc4[:, 4], mod_mag[:, 1], vec_row[0:B, V_BETA:V_BETA + D], ALU.mult).then_inc(s["bc4_ok"], 1)
            dve.wait_ge(s["rope_ok"], 1)

            for b in range(B + 1):
                if b < B:
                    rotate(b)
                if b >= 1:
                    residual(b - 1)
                if b < B:
                    summary(b)
                if b + 1 < B:
                    in_norm(b + 1)
                if b >= 1:
                    if b == 1:
                        dve.wait_ge(s["ld_dest"], 16)
                    choose(b - 1)
                if b < B:
                    divide(b)
                if b >= 1:
                    place(b - 1)

            dve.wait_ge(s["cnt_ps"], 1)
            v.tensor_copy(cnt_i[:], w_ps[0:1, CNT:CNT + NE]).then_inc(s["cnt_ok"], 1)
            v.tensor_scalar_add(cnt_p[:], w_ps[0:1, CNT:CNT + NE], float(P - 1)).then_inc(s["nt1"], 1)
            dve.wait_ge(s["nt1"], 1)
            v.tensor_single_scalar(nt_i[:], cnt_p[:], 7, ALU.arith_shift_right).then_inc(s["nt2"], 1)
            dve.wait_ge(s["nt2"], 1)
            v.tensor_copy(nt_f[:], nt_i[:]).then_inc(s["nt3"], 1)
            dve.wait_ge(s["nt3"], 1)
            v.tensor_tensor_scan(nt_cum[:], nt_one[:], nt_f[:], 0.0, ALU.mult, ALU.add).then_inc(s["nt4"], 1)
            dve.wait_ge(s["nt4"], 1)
            tiles = cst[0:1, C_TILE:C_TILE + TILES * NE].rearrange("p (j e) -> p j e", e=NE)
            v.tensor_tensor(past[:], tiles, nt_cum[:].unsqueeze(1).to_broadcast([1, TILES, NE]), ALU.is_ge).then_inc(s["past_ok"], 1)
            dve.wait_ge(s["past_ok"], 1)
            v.tensor_tensor(pastn[:], past[:], nt_f[:].unsqueeze(1).to_broadcast([1, TILES, NE]), ALU.mult).then_inc(s["pastn_ok"], 1)
            v.tensor_reduce(ex_f[:], past[:], AX.X, ALU.add).then_inc(s["ex_ok"], 1)
            dve.wait_ge(s["pastn_ok"], 1)
            v.tensor_reduce(before[:], pastn[:], AX.X, ALU.add).then_inc(s["before_ok"], 1)
            dve.wait_ge(s["ex_ok"], 1)
            v.tensor_scalar(tile_tab[:, 0], ex_f[:], float(NE - 1), None, ALU.min)
            dve.wait_ge(s["before_ok"], 1)
            v.tensor_tensor(ahead[:], tiles[:, :, 0], before[:], ALU.subtract).then_inc(s["ahead_ok"], 1)
            v.tensor_scalar(row_f[:], ex_f[:], float(REGION), None, ALU.mult).then_inc(s["row_ok"], 1)
            dve.wait_ge(s["ahead_ok"], 1)
            dve.wait_ge(s["row_ok"], 1)
            v.scalar_tensor_tensor(out=row_f[:], in0=ahead[:], scalar=float(P), in1=row_f[:], op0=ALU.mult,
                                   op1=ALU.add).then_inc(s["row_ok"], 1)
            dve.wait_ge(s["row_ok"], 2)
            v.tensor_scalar(tile_tab[:, 1], row_f[:], float(DEAD_ROW), None, ALU.min).then_inc(s["tab_ok"], 1)

            def destinations(turn, c):
                _, q, _, before = tile_of(turn, c)
                dve.wait_ge(ld_tile[q], before * 16 + 16)
                used_before(dve, y_out[q], before * 16)
                v.tensor_copy(ydest[:, q], xt[:, q, D + 1:D + 2]).then_inc(s["ydest_ok"], 1)

            def hidden(turn, c):
                j, q, h, _ = tile_of(turn, c)
                dve.wait_ge(s["gact_ok"], j + 1)
                used_before(dve, s["hidT_ps"], j - 1)
                v.scalar_tensor_tensor(out=hid[:, h, :], in0=gact[:, h, :], scalar=xt[:, q, D:D + 1],
                                       in1=g_bank[h][:, FF:2 * FF], op0=ALU.mult, op1=ALU.mult).then_inc(s["hid_ok"], 1)

            steps(dve, [(0, destinations), (1, hidden)])

            for b in range(B):
                t0 = b * NT
                dve.wait_ge(ld_y[b], 32)
                v.tensor_tensor(ysum[:, b % 2], yk[:, b % 2, 0], yk[:, b % 2, 1], ALU.add).then_inc(s["ysum_ok"], 1)
                dve.wait_ge(s["ysum_ok"], b + 1)
                for i in range(NT):
                    last = v.bn_stats(st3[:, b % 2, i], ysum[:, b % 2, i])
                last.then_inc(s["st3_ok"], 1)
                dve.wait_ge(s["st3_ok"], b + 1)
                for i in range(NT):
                    last = v.bn_aggr(mv3[:, b % 2, i], st3[:, b % 2, i])
                last.then_inc(s["mv3_ok"], 1)
                dve.wait_ge(s["mv3_ok"], b + 1)
                v.tensor_scalar_add(ve3[:, b % 2], mv3[:, b % 2, :, 1], LN_EPS).then_inc(s["ve3_ok"], 1)
                v.tensor_tensor(x2[:, t0:t0 + NT, :], x2[:, t0:t0 + NT, :],
                                mod_bc[:, b, 4:5].to_broadcast([P, NT, D]), ALU.add)
                for i in range(NT):
                    last = v.scalar_tensor_tensor(out=fin[:, b % 2, i], in0=ysum[:, b % 2, i], scalar=mv3[:, b % 2, i, 0:1],
                                                  in1=mod_bc[:, b, 3], op0=ALU.subtract, op1=ALU.mult)
                last.then_inc(s["fin_ok"], 1)
                dve.wait_ge(s["fin_ok"], b + 1)
                dve.wait_ge(s["rs3_ok"], b + 1)
                if b >= 2:
                    dve.wait_ge(stored[b % 2], 16 * (b // 2))
                for i in range(NT):
                    last = v.scalar_tensor_tensor(out=res[:, b % 2, i], in0=fin[:, b % 2, i], scalar=rs3[:, b % 2, i:i + 1],
                                                  in1=x2[:, t0 + i, :], op0=ALU.mult, op1=ALU.add)
                last.then_inc(s["res_ok"], 1)

        @block.tensor
        def _(pe):
            mm = nc.tensor.matmul
            pe.wait_ge(s["ld_mod"], 16)
            pe.wait_ge(s["scond_ok"], 1)
            mm(m_ps[:, 0:B], wmod_sb[:, 0:D], scond[:], start=True, stop=True)
            mm(m_ps[:, B:2 * B], wmod_sb[:, D:2 * D], scond[:], start=True, stop=True).then_inc(s["modcol_ps"], 1)
            mm(n_ps[0:B, :], scond[:], wmod_sb[:, 0:512], start=True, stop=True)
            mm(w_ps[0:B, 0:256], scond[:], wmod_sb[:, 512:6 * D], start=True, stop=True).then_inc(s["mod4_ps"], 1)

            def project(b):
                pe.wait_ge(s["ld_cst"], 16)
                pe.wait_ge(s["z_ok"], b + 1)
                if b >= 1:
                    pe.wait_ge(s["qfT_ok"], b)
                for i in range(NT):
                    last = nc.tensor.transpose(ta_ps[:, i * P:(i + 1) * P], z[:, b % 2, i], ident)
                last.then_inc(s["zT_ps"], 1)
                pe.wait_ge(s["hT_ok"], b + 1)
                pe.wait_ge(s["ld_qkv"], 16)
                pe.wait_ge(s["ld_vec"], 16)
                pe.wait_ge(s["const_ok"], 3)
                if b >= 1:
                    pe.wait_ge(s["qk_ok"], b)
                    pe.wait_ge(s["v_ok"], b)
                for i in range(NT):
                    hi = hT[:, b % 2, i * P:(i + 1) * P]
                    qk = qk_ps[:, i].rearrange("p q d -> p (q d)")
                    vv = v_ps[:, i * D:(i + 1) * D]
                    mm(qk, hi, wqkv_sb[:, 0:2 * D], start=True, stop=False)
                    mm(qk, ones[0:1, :], vec_row[0:1, 0:2 * D], start=False, stop=True)
                    mm(vv, hi, wqkv_sb[:, 2 * D:3 * D], start=True, stop=False)
                    last = mm(vv, ones[0:1, :], vec_row[0:1, 2 * D:3 * D], start=False, stop=True)
                last.then_inc(s["qkv_ps"], 1)

            def modulation_rows():
                pe.wait_ge(s["bc4_ok"], 1)
                rows = bc4[:].rearrange("b r d -> b (r d)")
                for b in range(B):
                    one = cst[0:B, C_SEL + b * P:C_SEL + (b + 1) * P]
                    if b >= 2:
                        pe.wait_ge(s["modbc_ok"], b - 1)
                    mm((n_ps, w_ps)[b % 2][:], one, rows[:, 0:512], start=True, stop=True).then_inc(s["modbc_ps"], 1)
                for b in range(B):
                    one = cst[0:B, C_SEL + b * P:C_SEL + (b + 1) * P]
                    last = mm(tb_ps[:, b * P:(b + 1) * P], one, rows[:, 512:5 * D], start=True, stop=True)
                last.then_inc(s["modrow4_ps"], 1)

            project(0)
            modulation_rows()
            pe.wait_ge(s["modbc_ok"], B)
            pe.wait_ge(s["modrow4_ok"], 1)
            for b in range(B + 1):
                if b < B:
                    if b >= 1:
                        pe.wait_ge(s["den_ok"], b)
                    pe.wait_ge(s["qkf_ok"], b + 1)
                    pe.wait_ge(s["v_ok"], b + 1)
                    for i in range(NT):
                        last = mm(m_ps[:, VK:VK + D + 1], qkf[:, b % 2, i, 1], v_sb[:, b % 2, i], start=(i == 0), stop=(i == NT - 1))
                    last.then_inc(s["vk_ps"], 1)
                    pe.wait_ge(s["hT_ok"], b + 1)
                    for i in range(NT):
                        last = nc.tensor.transpose(ta_ps[:, i * P:(i + 1) * P], qkf[:, b % 2, i, 0], ident)
                    last.then_inc(s["qT_ps"], 1)
                if b >= 1:
                    p = b - 1
                    pe.wait_ge(s["h2_ok"], b)
                    pe.wait_ge(s["attnT_ok"], b)
                    for i in range(NT):
                        last = nc.tensor.transpose(tb_ps[:, i * P:(i + 1) * P], rec[:, p % 2, i, 0, 0:D], ident)
                    last.then_inc(s["h2T_ps"], 1)
                if b < B:
                    pe.wait_ge(s["kv_ok"], b + 1)
                    pe.wait_ge(s["qfT_ok"], b + 1)
                    if b >= 1:
                        pe.wait_ge(s["o_ok"], b)
                    for i in range(NT):
                        qi = qfT[:, b % 2, i * P:(i + 1) * P]
                        mm(n_ps[:, i * D:(i + 1) * D], qi, kv[:, b % 2, 0:D], start=True, stop=True)
                        last = mm(m_ps[:, DEN + i * H:DEN + (i + 1) * H], qi, kv[:, b % 2, D:D + H], start=True, stop=True)
                    last.then_inc(s["res_ps"], 1)
                if b >= 1:
                    pe.wait_ge(s["h2T_ok"], b)
                    pe.wait_ge(s["ld_wr"], 16)
                    if p >= 1:
                        pe.wait_ge(s["pos_ok"], p)
                    for i in range(NT):
                        last = mm(w_ps[:, LG + i * NE:LG + (i + 1) * NE], h2T[:, p % 2, i * P:(i + 1) * P], wr_sb[:], start=True, stop=True)
                    last.then_inc(s["lg_ps"], 1)
                if b + 1 < B:
                    project(b + 1)
                if b < B:
                    pe.wait_ge(s["attn_ok"], b + 1)
                    if b >= 1:
                        pe.wait_ge(s["h2T_ok"], b)
                    for i in range(NT):
                        last = nc.tensor.transpose(tb_ps[:, i * P:(i + 1) * P], attn[:, b % 2, i], ident)
                    last.then_inc(s["aT_ps"], 1)
                    pe.wait_ge(s["attnT_ok"], b + 1)
                    pe.wait_ge(s["ld_out"], 16)
                    for i in range(NT):
                        oi = n_ps[:, i * D:(i + 1) * D]
                        mm(oi, attnT[:, b % 2, i * P:(i + 1) * P], wout_sb[:], start=True, stop=False)
                        last = mm(oi, ones[0:1, :], vec_row[0:1, V_BOUT:V_BOUT + D], start=False, stop=True)
                    last.then_inc(s["o_ps"], 1)
                if b >= 1:
                    pe.wait_ge(s["sel_ok"], b)
                    pe.wait_ge(s["up_ok"], 1)
                    pe.wait_ge(s["carry16_ok"], b)
                    rk = w_ps[:, RK:RK + NT * NE].rearrange("p (t e) -> p t e", e=NE)
                    mm(rk, up16[:], sel16[:], start=True, stop=False)
                    for d in range(1, NT):
                        mm(rk[:, d:], ones16[:], sel16[:, 0:NT - d], start=False, stop=False)
                    mm(rk, ones16[:], carry16[:].unsqueeze(1).to_broadcast([P, NT, NE]), start=False, stop=True).then_inc(s["rank_ps"], 1)
            pe.wait_ge(s["carry16_ok"], B + 1)
            mm(w_ps[:, CNT:CNT + NE], ones16[:], carry16[:], start=True, stop=True).then_inc(s["cnt_ps"], 1)

            pe.wait_ge(s["tab_ok"], 1)
            pe.wait_ge(s["ld_gu"], 16)
            pe.wait_ge(s["ld_down"], 16)

            def x_turn(turn, c):
                j, q, h, before = tile_of(turn, c)
                pe.wait_ge(ld_tile[q], before * 16 + 16)
                used_before(pe, s["xT_ok"], j - 1)
                nc.tensor.transpose(xT_bank[h][:, 0:P], xt[:, q, 0:D], ident).then_inc(s["xT_ps"], 1)

            def gate_up(turn, c):
                j, _, h, _ = tile_of(turn, c)
                e = pe.value_load(tile_tab[0:1, 0, bass.ds(j, 1)], min_val=0, max_val=NE - 1)
                pe.wait_ge(s["xT_ok"], j + 1)
                used_before(pe, s["hid_ok"], j - 1)
                mm(g_bank[h][:], xT[:, h, :], wgu_sb[:, bass.ds(e, 1), :], start=True, stop=True).then_inc(s["gu_ps"], 1)

            def hid_turn(turn, c):
                j, _, h, _ = tile_of(turn, c)
                pe.wait_ge(s["hid_ok"], j + 1)
                used_before(pe, s["hidT_ok"], j - 1)
                for f in range(FB):
                    last = nc.tensor.transpose(hT_bank[h][:, f * P:(f + 1) * P], hid[:, h, f * P:(f + 1) * P], ident)
                last.then_inc(s["hidT_ps"], 1)

            def down(turn, c):
                j, _, h, _ = tile_of(turn, c)
                e = pe.value_load(tile_tab[0:1, 0, bass.ds(j, 1)], min_val=0, max_val=NE - 1)
                pe.wait_ge(s["hidT_ok"], j + 1)
                used_before(pe, s["yrow_ok"], j - 1)
                for f in range(FB):
                    last = mm(y_bank[h][:, 0, 0], hidT[:, h, f * P:(f + 1) * P], wd_sb[:, bass.ds(e, 1), f, :],
                              start=(f == 0), stop=(f == FB - 1))
                last.then_inc(s["y_ps"], 1)

            steps(pe, [(0, x_turn), (1, gate_up), (3, down), (2, hid_turn)])


def _shape_constants():
    import numpy as np
    c = np.zeros((P, C_ALL), np.float32)
    r = np.arange(P)
    c[:, C_ID:C_ID + P] = np.eye(P)
    c[:, C_BLK:C_BLK + D] = r[:, None] // DH == r[None, :] // DH
    c[:, C_HEAD:C_HEAD + H] = r[:, None] // DH == np.arange(H)[None, :]
    c[:, C_UP:C_UP + P] = r[:, None] < r[None, :]
    c[:, C_EXP:C_EXP + NE] = np.arange(NE)
    c[:, C_BASE:C_BASE + NE] = np.arange(NE) * REGION
    inv = (np.float32(1.0) / np.float32(THETA) ** (np.arange(0, DH, 2, dtype=np.float32) / np.float32(DH))).astype(np.float32)
    ang = np.outer(np.arange(L, dtype=np.float32), inv).astype(np.float32)
    cos = np.tile(np.repeat(np.cos(ang), 2, axis=1), (1, H))
    sin = np.tile(np.repeat(np.sin(ang), 2, axis=1), (1, H))
    sin[:, 0::2] *= -1
    for i in range(NT):
        c[:, C_COS + i * D:C_COS + (i + 1) * D] = cos[i * P:(i + 1) * P]
        c[:, C_SIN + i * D:C_SIN + (i + 1) * D] = sin[i * P:(i + 1) * P]
    for b in range(B):
        c[b, C_SEL + b * P:C_SEL + (b + 1) * P] = 1
    c[0, C_TILE:] = np.repeat(np.arange(TILES), NE)
    t = np.arange(TOKENS, dtype=np.float32).reshape(TT, P).T
    dests = np.stack([t + k * TOKENS for k in range(TOPK)], axis=-1).astype(np.float32)
    return c, dests


def kernel(**inputs):
    import numpy as np
    import concourse.bacc as bacc
    from concourse.bass_utils import run_bass_kernel_spmd

    a = {k[3:]: np.asarray(v) for k, v in inputs.items()}
    consts, dests = _shape_constants()
    gate, up, down = a["ffn_w_gate"], a["ffn_w_up"], a["ffn_w_down"]
    arrays = {
        "x": a["attn_x"].reshape(TOKENS, D),
        "wqkv": a["attn_Wqkv"].T,
        "wout": a["attn_Wout"].T,
        "wrouter": a["ffn_w_router"].T,
        "wgu": np.concatenate([gate, up], axis=1).transpose(2, 0, 1),
        "wdown": down.reshape(NE, D, FB, P).transpose(3, 0, 2, 1),
        "wmod": a["wmod"],
        "cond": a["c"].T,
        "vecs": np.concatenate([a["attn_bqkv"], a["attn_bout"], a["attn_gq"], a["attn_gk"], a["attn_gout"],
                                a["ffn_ln_gamma"], a["ffn_ln_beta"]])[None, :],
        "consts": consts,
        "dests": dests,
    }
    arrays = {k: np.ascontiguousarray(v) for k, v in arrays.items()}
    nc = bacc.Bacc("TRN2", target_bir_lowering=False, num_devices=1)
    aps = {k: nc.dram_tensor(k, v.shape, mybir.dt.from_np(v.dtype), kind="ExternalInput").ap() for k, v in arrays.items()}
    out = nc.dram_tensor("out", (TOKENS, D), mybir.dt.float32, kind="ExternalOutput").ap()
    adaln_block(nc, out=out, **aps)
    r = run_bass_kernel_spmd(nc, [arrays], core_ids=[0])
    return r.results[0]["out"].reshape(B, L, D)
```

```python
import concourse.bass as bass
from concourse import mybir
from contextlib import ExitStack

P = 128
B, L, D = 4, 512, 128
NT = L // P
TOKENS = B * L
TT = TOKENS // P
H, DH = 16, 8
NE, FF, TOPK = 8, 256, 2
FB = FF // P
RMS_EPS = 1.1920929e-07
LIN_EPS = 1e-06
LN_EPS = 1e-05
THETA = 10000.0

REGION = TOKENS + P
DEAD_ROW = NE * REGION
TILES = TOPK * TT + NE - 1
STAGES = 4
RING = 12
Y_RING = 8
GROUP = 4
TAB = -(-TILES // GROUP) * GROUP
REC = D + 2
W_ALL = 2 * FF + FB * D
W_RING = 3
W_POOL = 5
SKIP = 1 << 20

LOW = 32
SEL = LOW + B

C_ID = 0
C_BLK = C_ID + P
C_HEAD = C_BLK + D
C_UP = C_HEAD + H
C_EXP = C_UP + P
C_BASE = C_EXP + NE
C_COS = C_BASE + NE
C_SIN = C_COS + NT * DH
C_ALL = C_SIN + NT * DH
R_SEL = 0
R_TILE = R_SEL + B * P
R_ALL = R_TILE + TAB * NE

V_BQKV, V_BOUT, V_GQ, V_GK, V_GOUT, V_GAMMA, V_BETA, V_ALL = 0, 384, 512, 640, 768, 896, 1024, 1152
W_QKV, W_OUT, W_ROUTER, W_ATT = 0, 3 * D, 4 * D, 4 * D + NE


def adaln_block(nc, x, watt, wexp, wmod, cond, vecs, consts, rows, dests, out):
    F32 = mybir.dt.float32
    F32R = mybir.dt.float32r
    BF16 = mybir.dt.bfloat16
    I32 = mybir.dt.int32
    U32 = mybir.dt.uint32
    ALU = mybir.AluOpType
    ACT = mybir.ActivationFunctionType
    AX = mybir.AxisListType

    sorted_rows = nc.dram_tensor("sorted_rows", [DEAD_ROW + P, REC], F32).ap()
    expert_rows = nc.dram_tensor("expert_rows", [TOPK * TOKENS, D], F32).ap()
    x_v = x.rearrange("(t p) d -> p t d", p=P)
    out_v = out.rearrange("(t p) d -> p t d", p=P)
    rows_v = expert_rows.rearrange("(k t p) d -> p k t d", k=TOPK, p=P)

    ctx = ExitStack()
    with ctx:
        def sb(name, shape, dt=F32):
            return ctx.enter_context(nc.sbuf_tensor(name, shape, dt))

        def sem(name):
            return ctx.enter_context(nc.semaphore(name))

        x_sb = sb("x_sb", [P, TT, D])
        cst = sb("cst", [P, C_ALL])
        row_sb = sb("row_sb", [SEL, R_ALL])
        dest_sb = sb("dest_sb", [P, TT, TOPK], I32)
        gqk = sb("gqk", [P, 2 * D])
        vec_sb = sb("vec_sb", [SEL, 3 * D])
        bias_in = sb("bias_in", [LOW + 1, 4 * D])
        bias_parts = sb("bias_parts", [LOW + 1, 4 * D], F32R)
        ones_r = sb("ones_r", [LOW + 1, P], F32R)
        watt_sb = sb("watt_sb", [P, W_ATT])
        wq_hi = sb("wq_hi", [P, 3 * D], F32R)
        wq_lo = sb("wq_lo", [P, 3 * D], F32R)
        wmod_sb = sb("wmod_sb", [P, 6 * D])
        cond_sb = sb("cond_sb", [P, B])
        scond = sb("scond", [P, SEL])
        ones16 = sb("ones16", [P, P], BF16)
        up16 = sb("up16", [P, P], BF16)
        neg_half = sb("neg_half", [P, NT])
        half_pair = sb("half_pair", [P, NT, 2])
        rope_c = sb("rope_c", [P, NT, 2 * D])
        rope_s = sb("rope_s", [P, NT, 2 * D])
        mcol = sb("mcol", [P, 2, 2, B])
        mod4 = sb("mod4", [SEL, 4, D])
        mod_sgn = sb("mod_sgn", [SEL, 2, D])
        mod_mag = sb("mod_mag", [SEL, 2, D])
        mod_row = sb("mod_row", [SEL, 5, D])
        row_parts = sb("row_parts", [SEL, 5, D], F32R)
        sel_r = sb("sel_r", [SEL, B, P], F32R)
        mod_bc = sb("mod_bc", [P, B, 4, D])
        beta_bc = sb("beta_bc", [P, B, D])

        st1 = sb("st1", [P, B, NT, 6])
        mv1 = sb("mv1", [P, B, NT, 2])
        ve1 = sb("ve1", [P, B, NT])
        rs1 = sb("rs1", [P, B, NT])
        nm1 = sb("nm1", [P, B, NT])
        z = sb("z", [P, 2, NT, D])
        h_f = sb("h_f", [P, L])
        hT_hi = sb("hT_hi", [P, 2, L], F32R)
        hT_lo = sb("hT_lo", [P, 2, L], F32R)
        v_sb = sb("v_sb", [P, 2, NT, D + 1])
        qk_sb = sb("qk_sb", [P, 2, NT, 2, D])
        sq_junk = sb("sq_junk", [P, NT * 2, D], BF16)
        ssq = sb("ssq", [P, B, NT, 2])
        msq = sb("msq", [P, B, NT, 2])
        rqk = sb("rqk", [P, B, NT, 2])
        ra = sb("ra", [P, 2, NT, 2, D])
        rb = sb("rb", [P, NT, 2, D])
        kf = sb("kf", [P, 2, NT, D])
        qfT = sb("qfT", [P, 2, L])
        kv = sb("kv", [P, 2, D + H])
        den = sb("den", [P, B, NT, H])
        rden = sb("rden", [P, B, NT, H])
        attn = sb("attn", [P, 2, NT, D])
        attnT = sb("attnT", [P, 2, L])
        o_sb = sb("o_sb", [P, 2, NT, D])
        o_junk = sb("o_junk", [P, NT, D], BF16)
        oss = sb("oss", [P, B, NT])
        oms = sb("oms", [P, B, NT])
        ors = sb("ors", [P, B, NT])
        og = sb("og", [P, NT, D])
        st2 = sb("st2", [P, B, NT, 6])
        mv2 = sb("mv2", [P, B, NT, 2])
        ve2 = sb("ve2", [P, B, NT])
        rs2 = sb("rs2", [P, B, NT])
        nm2 = sb("nm2", [P, B, NT])
        z2 = sb("z2", [P, 2, NT, D])
        h2c = sb("h2c", [P, NT, D])
        rec = sb("rec", [P, 2, NT, TOPK, REC])
        h2T = sb("h2T", [P, 2, L])
        lg = sb("lg", [P, NT, NE])
        top = sb("top", [P, NT, 8])
        topi = sb("topi", [P, NT, 8], U32)
        topf = sb("topf", [P, NT, TOPK])
        gap = sb("gap", [P, NT, TOPK])
        tanh_gap = sb("tanh_gap", [P, NT, TOPK])
        onehot = sb("onehot", [P, NT, TOPK, NE])
        sel16 = sb("sel16", [P, NT, NE], BF16)
        selsum = sb("selsum", [P, NE])
        carry = sb("carry", [P, NE])
        carry16 = sb("carry16", [P, NE], BF16)
        pos = sb("pos", [P, NT, NE])
        posk = sb("posk", [P, NT, TOPK, NE])
        slot = sb("slot", [P, 2, NT, TOPK], U32)
        pad = sb("pad", [P, REC])

        cnt_i = sb("cnt_i", [1, NE], I32)
        cnt_p = sb("cnt_p", [1, NE], I32)
        nt_i = sb("nt_i", [1, NE], I32)
        nt_f = sb("nt_f", [1, NE])
        nt_one = sb("nt_one", [1, NE])
        nt_cum = sb("nt_cum", [1, NE])
        past = sb("past", [1, TAB, NE])
        pastn = sb("pastn", [1, TAB, NE])
        ex_f = sb("ex_f", [1, TAB])
        before = sb("before", [1, TAB])
        ahead = sb("ahead", [1, TAB])
        row_f = sb("row_f", [1, TAB])
        tile_tab = sb("tile_tab", [1, 2, TAB], I32)

        w_in = sb("w_in", [P, W_RING, W_ALL])
        w_high = sb("w_high", [P, NE, W_ALL], F32R)
        w_low = sb("w_low", [P, NE, W_ALL], F32R)
        st3 = sb("st3", [P, B, NT, 6])
        mv3 = sb("mv3", [P, B, NT, 2])
        ve3 = sb("ve3", [P, B, NT])
        rs3 = sb("rs3", [P, B, NT])
        nm3 = sb("nm3", [P, B, NT])
        xt = rec[:].rearrange("p b t k c -> p (b t k) c")[:, 0:RING]
        xT = hT_lo[:, 0].rearrange("p (h n t) -> p h n t", h=2, n=2)
        hidT = hT_hi[:].rearrange("p h (n f) -> p h n f", n=2)
        yrow = attnT[:].rearrange("p h (i d) -> p (h i) d", d=D)
        gact = og[:].rearrange("p (h i) d -> p h (i d)", h=2)
        hid = h2c[:].rearrange("p (h i) d -> p h (i d)", h=2)
        yk = [big[:, h].rearrange("p (k t) q d -> p k (t q) d", k=TOPK) for big in (qk_sb, ra) for h in range(2)]
        ysum = attn
        z3 = z
        fin = z2
        res = [big[:, h] for big in (o_sb, kf) for h in range(2)]

        ta_ps, tb_ps, v_ps, n_ps, m_ps, w_ps = [ctx.enter_context(nc.psum_tensor(f"bank{i}", [P, 512], F32)) for i in range(6)]
        qk_ps = ctx.enter_context(nc.psum_tensor("qk_ps", [P, NT, 2, D], F32))
        VK, DEN = 0, 160
        LG, RK, CNT = 0, 64, 128
        xT_bank, g_bank, hT_bank, y_bank = (ta_ps, tb_ps), (v_ps, n_ps), (m_ps, w_ps), (qk_ps[:, 0:2], qk_ps[:, 2:4])

        s = {n: sem(n) for n in (
            "ld_x0 ld_x1 ld_x2 ld_x3 ld_cst ld_gqk ld_vec ld_bias ld_cond ld_mod ld_att ld_rows ld_dest "
            "bias_zero bias_hi bias_ok onesr_ok wq_hi_ok wq_ok scond0 scond_ok sel_r_ok ones_ok up_ok exp_ok rope_ok vone_ok "
            "modcol_ps mcol_ok mod4_ps mod4_ok row_step row_parts_ok modbc_ps modbc_ok beta_ps beta_ok "
            "moments1 ve1_ok rs1_ok nm1_ok z_ok zT_ps hf_ok hT_hi_ok hT_ok qkv_ps v_ok qk_ok ssq_ok msq_ok rqk_ok "
            "ra_ok rot_ok kf_ok qT_ps qfT_ok vk_ps kv_ok res_ps den_ok rden_ok attn_ok aT_ps attnT_ok o_ps o_ok "
            "oss_ok oms_ok ors_ok og_ok x2_ok moments2 ve2_ok rs2_ok nm2_ok z2_ok h2T_ps h2T_ok h2c_ok h2_ok dup_ok "
            "lg_ps choose_step gap_ok tanh_ok sel_ok selsum_ok carry_ok carry16_ok rank_ps "
            "pos_ok posk_ok slot_ok pad_ok pad_dest_ok scat0 scat1 "
            "cnt_ps cnt_ok nt_ok table_step tab_ok pads_out w_hi w_lo w_hi2 w_lo2 "
            "xT_ps xT_hi xT_ok gu_ps gact_ok hid_ok hidT_ps hidT_hi hidT_ok y_ps yrow_ok "
            "xb_ok ysum_ok moments3 ve3_ok rs3_ok nm3_ok z3_ok fin_ok res_ok").split()}
        ld_w = [sem(f"ld_w{q}") for q in range(W_RING)]
        ld_tile = [sem(f"ld_tile{q}") for q in range(RING)]
        y_out = [sem(f"y_out{q}") for q in range(Y_RING)]
        ld_y = [sem(f"ld_y{b}") for b in range(B)]
        stored = sem("stored")
        block = ctx.enter_context(nc.Block())

        ident = cst[:, C_ID:C_ID + P]

        def pipeline(count, stages):
            for n in range(count + max(k for k, _ in stages)):
                for k, stage in stages:
                    if 0 <= n - k < count:
                        stage(n - k)

        def followed(stage, then, item=0):
            def both(b):
                stage(b)
                if b == item:
                    then()
            return both

        def table_values(engine, entries, max_val):
            _, values = nc.values_load_multi_w_load_instructions(
                entries, engines=[engine], min_val=0, max_val=max_val,
                skip_runtime_bounds_check_because="the entries are within this range by the arithmetic that makes them")
            return values

        @block.sync
        def _(sp):
            sp.dma_start(x_sb[:, 0:NT, :], x_v[:, 0:NT, :]).then_inc(s["ld_x0"], 16)
            sp.dma_start(cst[:], consts).then_inc(s["ld_cst"], 16)
            sp.dma_start(gqk[:], vecs[:, V_GQ:V_GQ + 2 * D].to_broadcast([P, 2 * D])).then_inc(s["ld_gqk"], 16)
            sp.dma_start(watt_sb[:], watt).then_inc(s["ld_att"], 16)
            for b in range(1, B):
                sp.dma_start(x_sb[:, b * NT:(b + 1) * NT, :], x_v[:, b * NT:(b + 1) * NT, :]).then_inc(s[f"ld_x{b}"], 16)
            sp.dma_start(dest_sb[:], dests).then_inc(s["ld_dest"], 16)
            for e in range(NE):
                if e >= W_RING:
                    sp.wait_ge(s["w_lo"], e - W_RING + 1)
                sp.dma_start(w_in[:, e % W_RING], wexp[:, e]).then_inc(ld_w[e % W_RING], 16)

            sp.wait_ge(s["pad_dest_ok"], 1)
            sp.dma_start(sorted_rows[DEAD_ROW:DEAD_ROW + P, :], pad[:]).then_inc(s["pads_out"], 16)
            sp.wait_ge(s["cnt_ok"], 1)
            for e in range(NE):
                if e % GROUP == 0:
                    counts = table_values(mybir.EngineType.SP, cnt_i[0:1, e:e + GROUP], TOKENS)
                sp.dma_start(sorted_rows[bass.ds(counts[e % GROUP] + e * REGION, P), :], pad[:]).then_inc(s["pads_out"], 16)
            sp.wait_ge(s["tab_ok"], 1)
            sp.wait_ge(s["pads_out"], 16 * (NE + 1))
            sp.wait_ge(s["scat0"], 16 * NT * TOPK * 2)
            sp.wait_ge(s["scat1"], 16 * NT * TOPK * 2)
            for j in range(TILES):
                q = j % RING
                if j % GROUP == 0:
                    first_rows = table_values(mybir.EngineType.SP, tile_tab[0:1, 1, j:j + GROUP], DEAD_ROW)
                if j >= RING:
                    last = j - RING
                    sp.wait_ge(s["xT_ps"], last + 1)
                    sp.wait_ge(s["hid_ok"], last + 1)
                    sp.wait_ge(y_out[last % Y_RING], 16 * (last // Y_RING + 1))
                sp.dma_start(xt[:, q, :], sorted_rows[bass.ds(first_rows[j % GROUP], P), :]).then_inc(ld_tile[q], 16)

            for q in range(Y_RING):
                sp.wait_ge(y_out[q], 16 * len(range(q, TILES, Y_RING)))
            for b in range(B):
                for k in range(TOPK):
                    sp.dma_start(yk[b][:, k], rows_v[:, k, b * NT:(b + 1) * NT, :]).then_inc(ld_y[b], 16)
            for b in range(B):
                sp.wait_ge(s["res_ok"], b + 1)
                sp.dma_start(out_v[:, b * NT:(b + 1) * NT, :], res[b]).then_inc(stored, 16)
            sp.wait_ge(stored, 16 * B)

        @block.scalar
        def _(act):
            act.dma_start(cond_sb[:], cond).then_inc(s["ld_cond"], 16)
            act.dma_start(wmod_sb[:], wmod).then_inc(s["ld_mod"], 16)
            act.wait_ge(s["bias_zero"], 1)
            for first in (0, LOW):
                act.dma_start(bias_in[first:first + 1, :], vecs[:, V_BQKV:V_BQKV + 4 * D]).then_inc(s["ld_bias"], 16)
            act.dma_start(vec_sb[:], vecs[:, V_GOUT:V_ALL].to_broadcast([SEL, 3 * D])).then_inc(s["ld_vec"], 16)
            act.dma_start(row_sb[:], rows).then_inc(s["ld_rows"], 16)
            act.wait_ge(s["ld_cond"], 16)
            act.wait_ge(s["scond0"], 1)
            nc.scalar.activation(scond[:, 0:B], cond_sb[:], ACT.Silu)
            nc.scalar.activation(scond[:, LOW:LOW + B], cond_sb[:], ACT.Silu).then_inc(s["scond_ok"], 1)
            act.wait_ge(s["ld_att"], 16)
            nc.scalar.copy(wq_hi[:], watt_sb[:, W_QKV:W_QKV + 3 * D]).then_inc(s["wq_hi_ok"], 1)
            act.wait_ge(s["mod4_ps"], 1)
            nc.scalar.copy(mod4[:].rearrange("b r d -> b (r d)"), n_ps[0:SEL, :]).then_inc(s["mod4_ok"], 1)

            def norm(b):
                act.wait_ge(s["nm1_ok"], b + 1)
                if b >= 2:
                    act.wait_ge(s["zT_ps"], b - 1)
                for i in range(NT):
                    last = nc.scalar.activation(z[:, b % 2, i], x_sb[:, b * NT + i, :], ACT.Identity,
                                                bias=nm1[:, b, i:i + 1], scale=rs1[:, b, i:i + 1])
                last.then_inc(s["z_ok"], 1)

            def modulate(b):
                act.wait_ge(s["zT_ps"], b + 1)
                act.wait_ge(s["mcol_ok"], 2)
                if b >= 1:
                    act.wait_ge(s["hT_ok"], b)
                nc.scalar.activation(h_f[:], ta_ps[:], ACT.Identity, bias=mcol[:, 0, 0, b:b + 1],
                                     scale=mcol[:, 0, 1, b:b + 1]).then_inc(s["hf_ok"], 1)
                act.wait_ge(s["hf_ok"], b + 1)
                if b >= 2:
                    act.wait_ge(s["qkv_ps"], 2 * (b - 1))
                nc.scalar.copy(hT_hi[:, b % 2], h_f[:]).then_inc(s["hT_hi_ok"], 1)

            def qk_back(half):
                def stage(b):
                    act.wait_ge(s["qkv_ps"], 2 * b + half + 1)
                    if b >= 2:
                        act.wait_ge(s["ra_ok"], 2 * (b - 2) + half + 1)
                        act.wait_ge(s["ssq_ok"], 2 * (b - 2) + half + 1)
                    t = slice(2 * half, 2 * half + 2)
                    nc.scalar.copy(qk_sb[:, b % 2, t], qk_ps[:, t]).then_inc(s["qk_ok"], 1)
                return stage

            def squares(half):
                def stage(b):
                    act.wait_ge(s["qk_ok"], 2 * b + half + 1)
                    if b >= 1:
                        act.wait_ge(s["ssq_ok"], 2 * b)
                    for i in (2 * half, 2 * half + 1):
                        for j in range(2):
                            last = nc.scalar.activation(sq_junk[:, 2 * i + j], qk_sb[:, b % 2, i, j, :], ACT.Square,
                                                        accum_out=ssq[:, b, i, j:j + 1])
                    last.then_inc(s["ssq_ok"], 1)
                return stage

            def v_back(b):
                act.wait_ge(s["qkv_ps"], 2 * b + 2)
                act.wait_ge(s["vone_ok"], 1)
                if b >= 2:
                    act.wait_ge(s["vk_ps"], b - 1)
                nc.scalar.copy(v_sb[:, b % 2, :, 0:D], v_ps[:].rearrange("p (t d) -> p t d", d=D)).then_inc(s["v_ok"], 1)

            def keys(b):
                act.wait_ge(s["rot_ok"], 2 * b + 2)
                act.wait_ge(s["rqk_ok"], b + 1)
                if b >= 2:
                    act.wait_ge(s["vk_ps"], b - 1)
                for i in range(NT):
                    last = nc.scalar.activation(kf[:, b % 2, i], ra[:, b % 2, i, 1, :], ACT.Relu, scale=rqk[:, b, i, 1:2])
                last.then_inc(s["kf_ok"], 1)

            def queries(b):
                act.wait_ge(s["qT_ps"], b + 1)
                if b >= 2:
                    act.wait_ge(s["res_ps"], b - 1)
                nc.scalar.activation(qfT[:, b % 2], ta_ps[:], ACT.Relu).then_inc(s["qfT_ok"], 1)

            def attn_back(b):
                act.wait_ge(s["aT_ps"], b + 1)
                if b >= 2:
                    act.wait_ge(s["o_ps"], b - 1)
                nc.scalar.copy(attnT[:, b % 2], tb_ps[:]).then_inc(s["attnT_ok"], 1)

            def out_back(b):
                act.wait_ge(s["o_ps"], b + 1)
                if b >= 2:
                    act.wait_ge(s["og_ok"], b - 1)
                nc.scalar.copy(o_sb[:, b % 2].rearrange("p t d -> p (t d)"), n_ps[:]).then_inc(s["o_ok"], 1)

            def out_squares(b):
                act.wait_ge(s["o_ok"], b + 1)
                if b >= 1:
                    act.wait_ge(s["oss_ok"], b)
                for i in range(NT):
                    last = nc.scalar.activation(o_junk[:, i], o_sb[:, b % 2, i], ACT.Square, accum_out=oss[:, b, i:i + 1])
                last.then_inc(s["oss_ok"], 1)

            def norm2(b):
                act.wait_ge(s["nm2_ok"], b + 1)
                if b >= 2:
                    act.wait_ge(s["h2T_ps"], b - 1)
                    act.wait_ge(s["h2c_ok"], b - 1)
                for i in range(NT):
                    last = nc.scalar.activation(z2[:, b % 2, i], x_sb[:, b * NT + i, :], ACT.Identity,
                                                bias=nm2[:, b, i:i + 1], scale=rs2[:, b, i:i + 1])
                last.then_inc(s["z2_ok"], 1)

            def modulate2(b):
                act.wait_ge(s["h2T_ps"], b + 1)
                if b >= 2:
                    act.wait_ge(s["lg_ps"], b - 1)
                nc.scalar.activation(h2T[:, b % 2], tb_ps[:], ACT.Identity, bias=mcol[:, 1, 0, b:b + 1],
                                     scale=mcol[:, 1, 1, b:b + 1]).then_inc(s["h2T_ok"], 1)

            def repeat_row(b):
                act.wait_ge(s["h2_ok"], b + 1)
                nc.scalar.copy(rec[:, b % 2, :, 1, 0:D], rec[:, b % 2, :, 0, 0:D]).then_inc(s["dup_ok"], 1)

            def router_tanh(b):
                act.wait_ge(s["gap_ok"], 2 * b + 2)
                nc.scalar.activation(tanh_gap[:], gap[:], ACT.Tanh, scale=0.5).then_inc(s["tanh_ok"], 1)

            def modulation_rows():
                for b, ps in enumerate((w_ps, n_ps, tb_ps, m_ps)):
                    act.wait_ge(s["modbc_ps"], b + 1)
                    nc.scalar.copy(mod_bc[:, b], ps[:].rearrange("p (r d) -> p r d", d=D)).then_inc(s["modbc_ok"], 1)

            pipeline(B, [(4, attn_back), (2, norm), (3, v_back), (5, repeat_row), (3, keys), (4, out_back), (4, out_squares),
                         (3, queries), (5, router_tanh), (2, followed(modulate, modulation_rows)), (2, qk_back(0)),
                         (2, squares(0)), (4, norm2), (2, qk_back(1)), (4, modulate2), (2, squares(1))])
            for e in range(W_POOL, NE):
                act.wait_ge(ld_w[e % W_RING], 16 * (e // W_RING + 1))
                nc.scalar.copy(w_high[:, e], w_in[:, e % W_RING]).then_inc(s["w_hi2"], 1)
            act.wait_ge(s["beta_ps"], 1)
            nc.scalar.copy(beta_bc[:].rearrange("p b d -> p (b d)"), tb_ps[:]).then_inc(s["beta_ok"], 1)

            def x_high(j):
                act.wait_ge(s["xT_ps"], j + 1)
                if j >= 2:
                    act.wait_ge(s["gu_ps"], j - 1)
                nc.scalar.copy(xT[:, j % 2, 0, :], xT_bank[j % 2][:, 0:P]).then_inc(s["xT_hi"], 1)

            def gate(j):
                act.wait_ge(s["gu_ps"], j + 1)
                if j >= 2:
                    act.wait_ge(s["hid_ok"], j - 1)
                nc.scalar.activation(gact[:, j % 2, :], g_bank[j % 2][:, 0:FF], ACT.Silu).then_inc(s["gact_ok"], 1)

            def hid_high(j):
                act.wait_ge(s["hidT_ps"], j + 1)
                if j >= 2:
                    act.wait_ge(s["y_ps"], j - 1)
                nc.scalar.copy(hidT[:, j % 2, 0, :], hT_bank[j % 2][:, 0:FF]).then_inc(s["hidT_hi"], 1)

            def y_back(j):
                act.wait_ge(s["y_ps"], j + 1)
                if j >= Y_RING:
                    act.wait_ge(y_out[j % Y_RING], 16 * (j // Y_RING))
                nc.scalar.copy(yrow[:, j % Y_RING, :], y_bank[j % 2][:, 0, 0]).then_inc(s["yrow_ok"], 1)

            pipeline(TILES, [(STAGES, y_back), (0, x_high), (1, gate), (2, hid_high)])

            for b in range(B):
                act.wait_ge(s["ysum_ok"], b + 1)
                act.wait_ge(s["nm3_ok"], b + 1)
                if b >= 2:
                    act.wait_ge(s["fin_ok"], b - 1)
                for i in range(NT):
                    last = nc.scalar.activation(z3[:, b % 2, i], ysum[:, b % 2, i], ACT.Identity,
                                                bias=nm3[:, b, i:i + 1], scale=rs3[:, b, i:i + 1])
                last.then_inc(s["z3_ok"], 1)

        @block.gpsimd
        def _(pool):
            g = nc.gpsimd
            g.memset(bias_in[:], 0.0).then_inc(s["bias_zero"], 1)
            g.memset(scond[:], 0.0).then_inc(s["scond0"], 1)
            g.memset(neg_half[:], -0.5).then_inc(s["exp_ok"], 1)
            g.memset(half_pair[:, :, 0:1], 0.5).then_inc(s["exp_ok"], 1)
            g.memset(half_pair[:, :, 1:2], -0.5).then_inc(s["exp_ok"], 1)
            g.memset(v_sb[:, :, :, D:D + 1], 1.0).then_inc(s["vone_ok"], 1)
            g.memset(pad[:], 0.0).then_inc(s["pad_ok"], 1)
            pool.wait_ge(s["pad_ok"], 1)
            g.memset(pad[:, D + 1:D + 2].bitcast(I32), SKIP).then_inc(s["pad_dest_ok"], 1)
            pool.wait_ge(s["exp_ok"], 3)

            def scale_and_shift(b, ve, rs, nm, ve_ok, rs_ok, nm_ok):
                pool.wait_ge(ve_ok, b + 1)
                g.tensor_tensor(rs[:, b], ve[:, b], neg_half[:], ALU.pow).then_inc(rs_ok, 1)
                pool.wait_ge(rs_ok, b + 1)
                g.tensor_tensor(nm[:, b], nm[:, b], rs[:, b], ALU.mult).then_inc(nm_ok, 1)

            def norm_scale(b):
                scale_and_shift(b, ve1, rs1, nm1, s["ve1_ok"], s["rs1_ok"], s["nm1_ok"])

            def norm2_scale(b):
                scale_and_shift(b, ve2, rs2, nm2, s["ve2_ok"], s["rs2_ok"], s["nm2_ok"])

            def qk_scale(b):
                pool.wait_ge(s["ssq_ok"], 2 * b + 2)
                g.tensor_scalar(msq[:, b], ssq[:, b], 1.0 / D, RMS_EPS, ALU.mult, ALU.add).then_inc(s["msq_ok"], 1)
                pool.wait_ge(s["msq_ok"], b + 1)
                g.tensor_tensor(rqk[:, b], msq[:, b], half_pair[:], ALU.pow).then_inc(s["rqk_ok"], 1)

            def out_scale(b):
                pool.wait_ge(s["oss_ok"], b + 1)
                g.tensor_scalar(oms[:, b], oss[:, b], 1.0 / D, RMS_EPS, ALU.mult, ALU.add).then_inc(s["oms_ok"], 1)
                pool.wait_ge(s["oms_ok"], b + 1)
                g.tensor_tensor(ors[:, b], oms[:, b], neg_half[:], ALU.pow).then_inc(s["ors_ok"], 1)

            def scatter(i, k):
                def stage(b):
                    pool.wait_ge(s["slot_ok"], b + 1)
                    pool.wait_ge(s["dup_ok"], b + 1)
                    g.indirect_dma_start(
                        out=sorted_rows, out_offset=bass.IndirectOffsetOnAxis(ap=slot[:, b % 2, i, k:k + 1], axis=0),
                        in_=rec[:, b % 2, i, k, :], in_offset=None).then_inc(s[f"scat{b % 2}"], 16)
                return stage

            pool.wait_ge(s["ld_gqk"], 16)
            pool.wait_ge(s["ld_cst"], 16)
            heads = lambda ap: ap.rearrange("p (m e) -> p m e", e=DH)
            gains = heads(gqk[:])
            pairs = lambda ap: ap.rearrange("p m (c two) -> p m c two", two=2)
            for i in range(NT):
                cos = cst[:, C_COS + i * DH:C_COS + (i + 1) * DH].unsqueeze(1).to_broadcast([P, 2 * H, DH])
                g.tensor_tensor(heads(rope_c[:, i]), gains, cos, ALU.mult).then_inc(s["rope_ok"], 1)
            norm_scale(0)
            for i in range(NT):
                sin = pairs(cst[:, C_SIN + i * DH:C_SIN + (i + 1) * DH].unsqueeze(1).to_broadcast([P, 2 * H, DH]))
                for c in range(2):
                    g.tensor_tensor(pairs(heads(rope_s[:, i]))[:, :, :, c], pairs(gains)[:, :, :, 1 - c], sin[:, :, :, c],
                                    ALU.mult).then_inc(s["rope_ok"], 1)

            def split_weights(e):
                pool.wait_ge(ld_w[e % W_RING], 16 * (e // W_RING + 1))
                g.tensor_copy(w_high[:, e], w_in[:, e % W_RING]).then_inc(s["w_hi"], 1)
                pool.wait_ge(s["w_hi"], e + 1)
                g.tensor_tensor(w_low[:, e], w_in[:, e % W_RING], w_high[:, e].bitcast(F32), ALU.subtract).then_inc(s["w_lo"], 1)

            def norm_scale_later(b):
                if b > 0:
                    norm_scale(b)

            def scatters(tiles):
                return [(5 if n >= 2 else 4, scatter(n // TOPK, n % TOPK)) for n in tiles]

            def split(first, count):
                return lambda: [split_weights(e) for e in range(first, first + count)]

            pipeline(B, scatters(range(2, 7)) + [(2, followed(qk_scale, split(2, 2)))] + scatters([7])
                     + [(3, followed(out_scale, split(4, 1))), (0, followed(norm_scale_later, split(0, 2), 1))]
                     + scatters([0, 1]) + [(3, norm2_scale)])

            for j in range(TILES):
                q = j % RING
                pool.wait_ge(s["yrow_ok"], j + 1)
                g.indirect_dma_start(
                    out=expert_rows, out_offset=bass.IndirectOffsetOnAxis(ap=xt[:, q, D + 1:D + 2].bitcast(U32), axis=0),
                    in_=yrow[:, j % Y_RING, :], in_offset=None, bounds_check=TOPK * TOKENS - 1,
                    oob_is_err=False).then_inc(y_out[j % Y_RING], 16)
            for b in range(B):
                scale_and_shift(b, ve3, rs3, nm3, s["ve3_ok"], s["rs3_ok"], s["nm3_ok"])

        @block.vector
        def _(dve):
            v = nc.vector

            def layer_stats(b, src, st, mv, nm, ve, moments_ok, ve_ok):
                for i in range(NT):
                    last = v.bn_stats(st[:, b, i], src(i))
                last.then_inc(moments_ok, 1)
                dve.wait_ge(moments_ok, 2 * b + 1)
                for i in range(NT):
                    last = v.bn_aggr(mv[:, b, i], st[:, b, i])
                last.then_inc(moments_ok, 1)
                dve.wait_ge(moments_ok, 2 * b + 2)
                v.tensor_single_scalar(nm[:, b], mv[:, b, :, 0], -1.0, ALU.mult)
                v.tensor_scalar_add(ve[:, b], mv[:, b, :, 1], LN_EPS).then_inc(ve_ok, 1)

            def all_stats(b):
                dve.wait_ge(s[f"ld_x{b}"], 16)
                layer_stats(b, lambda i: x_sb[:, b * NT + i, :], st1, mv1, nm1, ve1, s["moments1"], s["ve1_ok"])

            def first_stats():
                all_stats(0)

            def stats(b):
                if b > 0:
                    all_stats(b)

            def stats2(b):
                dve.wait_ge(s["x2_ok"], b + 1)
                layer_stats(b, lambda i: x_sb[:, b * NT + i, :], st2, mv2, nm2, ve2, s["moments2"], s["ve2_ok"])

            def low_part(b):
                dve.wait_ge(s["hT_hi_ok"], b + 1)
                if b >= 2:
                    dve.wait_ge(s["qkv_ps"], 2 * (b - 1))
                v.tensor_tensor(hT_lo[:, b % 2], h_f[:], hT_hi[:, b % 2].bitcast(F32), ALU.subtract).then_inc(s["hT_ok"], 1)

            def rotate(half):
                def stage(b):
                    t = slice(2 * half, 2 * half + 2)
                    n = 2 * b + half + 1
                    flat = lambda ap: ap.rearrange("p t q d -> p (t q d)")
                    pairs = lambda ap: ap.rearrange("p (m two) -> p m two", two=2)
                    r_a, r_b, qk = flat(ra[:, b % 2, t]), flat(rb[:, t]), flat(qk_sb[:, b % 2, t])
                    rc, rs = (rope[:, t].rearrange("p t d -> p (t d)") for rope in (rope_c, rope_s))
                    dve.wait_ge(s["qk_ok"], n)
                    dve.wait_ge(s["rope_ok"], 3 * NT)
                    if b >= 2:
                        dve.wait_ge(s["kf_ok"], b - 1)
                        dve.wait_ge(s["qT_ps"], b - 1)
                    v.tensor_tensor(r_a, qk, rc, ALU.mult)
                    v.tensor_tensor(pairs(r_b)[:, :, 0], pairs(qk)[:, :, 1], pairs(rs)[:, :, 0], ALU.mult)
                    v.tensor_tensor(pairs(r_b)[:, :, 1], pairs(qk)[:, :, 0], pairs(rs)[:, :, 1], ALU.mult).then_inc(s["ra_ok"], 1)
                    dve.wait_ge(s["ra_ok"], n)
                    v.tensor_tensor(r_a, r_a, r_b, ALU.add).then_inc(s["rot_ok"], 1)
                return stage

            def summary(b):
                dve.wait_ge(s["vk_ps"], b + 1)
                if b >= 2:
                    dve.wait_ge(s["res_ps"], b - 1)
                v.tensor_tensor(kv[:, b % 2, 0:D], m_ps[:, VK:VK + D], cst[:, C_BLK:C_BLK + D], ALU.mult)
                v.tensor_scalar(kv[:, b % 2, D:D + H], cst[:, C_HEAD:C_HEAD + H], m_ps[:, VK + D:VK + D + 1], None,
                                ALU.mult).then_inc(s["kv_ok"], 1)

            def divide(b):
                dve.wait_ge(s["res_ps"], b + 1)
                dve.wait_ge(s["rqk_ok"], b + 1)
                v.scalar_tensor_tensor(out=den[:, b], in0=rqk[:, b, :, 0:1].to_broadcast([P, NT, H]), scalar=LIN_EPS,
                                       in1=m_ps[:, DEN:DEN + NT * H].rearrange("p (t h) -> p t h", h=H), op0=ALU.mult,
                                       op1=ALU.add).then_inc(s["den_ok"], 1)
                dve.wait_ge(s["den_ok"], b + 1)
                v.reciprocal(rden[:, b], den[:, b]).then_inc(s["rden_ok"], 1)
                dve.wait_ge(s["rden_ok"], b + 1)
                if b >= 2:
                    dve.wait_ge(s["aT_ps"], b - 1)
                v.tensor_tensor(attn[:, b % 2].rearrange("p t (h e) -> p (t h) e", e=DH),
                                n_ps[:].rearrange("p (m e) -> p m e", e=DH),
                                rden[:, b].rearrange("p t h -> p (t h)").unsqueeze(2).to_broadcast([P, NT * H, DH]),
                                ALU.mult).then_inc(s["attn_ok"], 1)

            def gate_out(b):
                dve.wait_ge(s["o_ok"], b + 1)
                dve.wait_ge(s["modbc_ok"], B)
                v.tensor_tensor(og[:], o_sb[:, b % 2],
                                mod_bc[:, b, 0:1].to_broadcast([P, NT, D]), ALU.mult).then_inc(s["og_ok"], 1)

            def residual(b):
                dve.wait_ge(s["og_ok"], b + 1)
                dve.wait_ge(s["ors_ok"], b + 1)
                for i in range(NT):
                    t = b * NT + i
                    last = v.scalar_tensor_tensor(out=x_sb[:, t, :], in0=og[:, i, :], scalar=ors[:, b, i:i + 1],
                                                  in1=x_sb[:, t, :], op0=ALU.mult, op1=ALU.add)
                last.then_inc(s["x2_ok"], 1)

            def record_rows(b):
                dve.wait_ge(s["z2_ok"], b + 1)
                v.tensor_tensor(h2c[:], z2[:, b % 2], mod_bc[:, b, 1:2].to_broadcast([P, NT, D]), ALU.mult).then_inc(s["h2c_ok"], 1)
                dve.wait_ge(s["h2c_ok"], b + 1)
                if b >= 2:
                    dve.wait_ge(s[f"scat{b % 2}"], 16 * NT * TOPK * (b // 2))
                v.tensor_tensor(rec[:, b % 2, :, 0, 0:D], h2c[:], mod_bc[:, b, 2:3].to_broadcast([P, NT, D]),
                                ALU.add).then_inc(s["h2_ok"], 1)

            def choose(b):
                dve.wait_ge(s["lg_ps"], b + 1)
                v.tensor_copy(lg[:], w_ps[:, LG:LG + NT * NE].rearrange("p (t e) -> p t e", e=NE)).then_inc(s["choose_step"], 1)
                dve.wait_ge(s["choose_step"], 5 * b + 1)
                for i in range(NT):
                    last = v.max(top[:, i], lg[:, i])
                last.then_inc(s["choose_step"], 1)
                dve.wait_ge(s["choose_step"], 5 * b + 2)
                for i in range(NT):
                    last = v.max_index(topi[:, i], top[:, i], lg[:, i])
                last.then_inc(s["choose_step"], 1)
                if b >= 1:
                    dve.wait_ge(s["tanh_ok"], b)
                v.tensor_tensor(gap[:, :, 0], top[:, :, 0], top[:, :, 1], ALU.subtract).then_inc(s["gap_ok"], 1)
                v.tensor_tensor(gap[:, :, 1], top[:, :, 1], top[:, :, 0], ALU.subtract).then_inc(s["gap_ok"], 1)
                dve.wait_ge(s["choose_step"], 5 * b + 3)
                v.tensor_copy(topf[:], topi[:, :, 0:TOPK]).then_inc(s["choose_step"], 1)
                dve.wait_ge(s["choose_step"], 5 * b + 4)
                for k in range(TOPK):
                    last = v.tensor_tensor(onehot[:, :, k, :],
                                           cst[:, C_EXP:C_EXP + NE].unsqueeze(1).to_broadcast([P, NT, NE]),
                                           topf[:, :, k:k + 1].to_broadcast([P, NT, NE]), ALU.is_equal)
                last.then_inc(s["choose_step"], 1)
                dve.wait_ge(s["choose_step"], 5 * b + 5)
                if b >= 1:
                    dve.wait_ge(s["rank_ps"], b)
                v.tensor_tensor(sel16[:], onehot[:, :, 0], onehot[:, :, 1], ALU.add).then_inc(s["sel_ok"], 1)

            def place(b):
                dve.wait_ge(s["rank_ps"], b + 1)
                v.tensor_tensor(pos[:], w_ps[:, RK:RK + NT * NE].rearrange("p (t e) -> p t e", e=NE),
                                cst[:, C_BASE:C_BASE + NE].unsqueeze(1).to_broadcast([P, NT, NE]), ALU.add).then_inc(s["pos_ok"], 1)
                v.tensor_reduce(selsum[:], sel16[:].rearrange("p t e -> p e t"), AX.X, ALU.add).then_inc(s["selsum_ok"], 1)
                if b >= 2:
                    dve.wait_ge(s[f"scat{b % 2}"], 16 * NT * TOPK * (b // 2))
                if b == 0:
                    dve.wait_ge(s["ld_dest"], 16)
                dve.wait_ge(s["tanh_ok"], b + 1)
                v.tensor_scalar(rec[:, b % 2, :, :, D], tanh_gap[:], 0.5, 0.5, ALU.mult, ALU.add)
                v.tensor_copy(rec[:, b % 2, :, :, D + 1].bitcast(I32), dest_sb[:, b * NT:(b + 1) * NT, :])
                dve.wait_ge(s["pos_ok"], b + 1)
                for k in range(TOPK):
                    last = v.tensor_tensor(posk[:, :, k, :], onehot[:, :, k, :], pos[:], ALU.mult)
                last.then_inc(s["posk_ok"], 1)
                dve.wait_ge(s["selsum_ok"], b + 1)
                v.tensor_tensor(carry[:], carry[:], selsum[:], ALU.add).then_inc(s["carry_ok"], 1)
                dve.wait_ge(s["posk_ok"], b + 1)
                with nc.allow_low_precision(reason="row numbers, whole and below 2**24"):
                    v.tensor_reduce(slot[:, b % 2], posk[:], AX.X, ALU.add).then_inc(s["slot_ok"], 1)
                dve.wait_ge(s["carry_ok"], b + 2)
                v.tensor_copy(carry16[:], carry[:]).then_inc(s["carry16_ok"], 1)

            v.memset(ones16[:], 1.0).then_inc(s["ones_ok"], 1)
            dve.wait_ge(s["ones_ok"], 1)
            v.tensor_copy(ones_r[:], ones16[0:LOW + 1]).then_inc(s["onesr_ok"], 1)
            v.memset(carry[:], 0.0).then_inc(s["carry_ok"], 1)
            v.memset(carry16[:], 0.0).then_inc(s["carry16_ok"], 1)
            v.memset(nt_one[:], 1.0).then_inc(s["ones_ok"], 1)
            first_stats()
            dve.wait_ge(s["modcol_ps"], 1)
            cols = m_ps[:, 0:4 * B].rearrange("p (n c b) -> p n c b", n=2, c=2)
            v.tensor_copy(mcol[:, :, 0], cols[:, :, 0]).then_inc(s["mcol_ok"], 1)
            v.tensor_scalar_add(mcol[:, :, 1], cols[:, :, 1], 1.0).then_inc(s["mcol_ok"], 1)
            dve.wait_ge(s["wq_hi_ok"], 1)
            v.tensor_tensor(wq_lo[:], watt_sb[:, W_QKV:W_QKV + 3 * D], wq_hi[:].bitcast(F32), ALU.subtract).then_inc(s["wq_ok"], 1)
            dve.wait_ge(s["ld_bias"], 32)
            v.tensor_copy(bias_parts[:], bias_in[:]).then_inc(s["bias_hi"], 1)
            dve.wait_ge(s["bias_hi"], 1)
            v.tensor_tensor(bias_parts[LOW:LOW + 1], bias_in[LOW:LOW + 1], bias_parts[LOW:LOW + 1].bitcast(F32),
                            ALU.subtract).then_inc(s["bias_ok"], 1)
            dve.wait_ge(s["ld_rows"], 16)
            v.tensor_copy(sel_r[:].rearrange("r b p -> r (b p)"), row_sb[:, R_SEL:R_SEL + B * P]).then_inc(s["sel_r_ok"], 1)

            def modulation_rows():
                dve.wait_ge(s["mod4_ok"], 1)
                gates = mod4[:, 0:4:3]
                v.tensor_scalar(mod_sgn[:], gates, 0.0, 0.5, ALU.is_ge, ALU.subtract).then_inc(s["row_step"], 1)
                v.scalar_tensor_tensor(out=mod_mag[:], in0=gates, scalar=-1.0, in1=gates, op0=ALU.mult,
                                       op1=ALU.max).then_inc(s["row_step"], 1)
                v.tensor_scalar_add(mod_row[:, 1], mod4[:, 2], 1.0)
                v.tensor_copy(mod_row[:, 2], mod4[:, 1])
                dve.wait_ge(s["row_step"], 2)
                v.tensor_scalar(mod_mag[:], mod_mag[:], 0.25, 2.0, ALU.max, ALU.mult).then_inc(s["row_step"], 1)
                dve.wait_ge(s["row_step"], 3)
                v.tensor_tensor(mod_mag[:], mod_sgn[:], mod_mag[:], ALU.mult).then_inc(s["row_step"], 1)
                dve.wait_ge(s["row_step"], 4)
                dve.wait_ge(s["ld_vec"], 16)
                v.tensor_tensor(mod_row[:, 0], mod_mag[:, 0], vec_sb[:, 0:D], ALU.mult)
                v.tensor_tensor(mod_row[:, 3:5], mod_mag[:, 1:2].to_broadcast([SEL, 2, D]),
                                vec_sb[:, D:3 * D].rearrange("b (r d) -> b r d", d=D), ALU.mult).then_inc(s["row_step"], 1)
                dve.wait_ge(s["row_step"], 5)
                v.tensor_copy(row_parts[:], mod_row[:]).then_inc(s["row_step"], 1)
                dve.wait_ge(s["row_step"], 6)
                v.tensor_tensor(row_parts[LOW:SEL], mod_row[LOW:SEL], row_parts[LOW:SEL].bitcast(F32),
                                ALU.subtract).then_inc(s["row_parts_ok"], 1)
                v.tensor_copy(up16[:], cst[:, C_UP:C_UP + P]).then_inc(s["up_ok"], 1)

            modulation_rows()
            pipeline(B, [(5, place), (3, summary), (4, residual), (2, low_part), (4, stats2), (0, stats), (3, divide),
                         (2, rotate(0)), (2, rotate(1)), (4, record_rows), (4, choose), (3, gate_out)])

            dve.wait_ge(s["cnt_ps"], 1)
            v.tensor_copy(cnt_i[:], w_ps[0:1, CNT:CNT + NE]).then_inc(s["cnt_ok"], 1)
            v.tensor_scalar_add(cnt_p[:], w_ps[0:1, CNT:CNT + NE], float(P - 1)).then_inc(s["nt_ok"], 1)
            dve.wait_ge(s["nt_ok"], 1)
            v.tensor_single_scalar(nt_i[:], cnt_p[:], 7, ALU.arith_shift_right).then_inc(s["nt_ok"], 1)
            dve.wait_ge(s["nt_ok"], 2)
            v.tensor_copy(nt_f[:], nt_i[:]).then_inc(s["nt_ok"], 1)
            dve.wait_ge(s["nt_ok"], 3)
            v.tensor_tensor_scan(nt_cum[:], nt_one[:], nt_f[:], 0.0, ALU.mult, ALU.add).then_inc(s["nt_ok"], 1)
            dve.wait_ge(s["nt_ok"], 4)
            tiles = row_sb[0:1, R_TILE:R_TILE + TAB * NE].rearrange("p (j e) -> p j e", e=NE)
            v.tensor_tensor(past[:], tiles, nt_cum[:].unsqueeze(1).to_broadcast([1, TAB, NE]), ALU.is_ge).then_inc(s["table_step"], 1)
            dve.wait_ge(s["table_step"], 1)
            v.tensor_tensor(pastn[:], past[:], nt_f[:].unsqueeze(1).to_broadcast([1, TAB, NE]), ALU.mult).then_inc(s["table_step"], 1)
            v.tensor_reduce(ex_f[:], past[:], AX.X, ALU.add).then_inc(s["table_step"], 1)
            dve.wait_ge(s["table_step"], 2)
            v.tensor_reduce(before[:], pastn[:], AX.X, ALU.add).then_inc(s["table_step"], 1)
            dve.wait_ge(s["table_step"], 3)
            v.tensor_scalar(tile_tab[:, 0], ex_f[:], float(NE - 1), None, ALU.min)
            v.tensor_scalar(row_f[:], ex_f[:], float(REGION), None, ALU.mult).then_inc(s["table_step"], 1)
            dve.wait_ge(s["table_step"], 4)
            v.tensor_tensor(ahead[:], tiles[:, :, 0], before[:], ALU.subtract).then_inc(s["table_step"], 1)
            dve.wait_ge(s["table_step"], 6)
            dve.wait_ge(s["table_step"], 5)
            v.scalar_tensor_tensor(out=row_f[:], in0=ahead[:], scalar=float(P), in1=row_f[:], op0=ALU.mult,
                                   op1=ALU.add).then_inc(s["table_step"], 1)
            dve.wait_ge(s["table_step"], 7)
            v.tensor_scalar(tile_tab[:, 1], row_f[:], float(DEAD_ROW), None, ALU.min).then_inc(s["tab_ok"], 1)

            for n, e in enumerate(range(W_POOL, NE)):
                dve.wait_ge(s["w_hi2"], n + 1)
                v.tensor_tensor(w_low[:, e], w_in[:, e % W_RING], w_high[:, e].bitcast(F32), ALU.subtract).then_inc(s["w_lo2"], 1)

            dve.wait_ge(s["beta_ok"], 1)
            for b in range(B):
                rows_b = x_sb[:, b * NT:(b + 1) * NT, :]
                last = v.tensor_tensor(rows_b, rows_b, beta_bc[:, b:b + 1].to_broadcast([P, NT, D]), ALU.add)
            last.then_inc(s["xb_ok"], 1)

            def x_low(j):
                dve.wait_ge(s["xT_hi"], j + 1)
                v.tensor_tensor(xT[:, j % 2, 1, :], xT_bank[j % 2][:, 0:P], xT[:, j % 2, 0, :].bitcast(F32),
                                ALU.subtract).then_inc(s["xT_ok"], 1)

            def hidden(j):
                dve.wait_ge(s["gact_ok"], j + 1)
                if j >= 2:
                    dve.wait_ge(s["hidT_ps"], j - 1)
                v.scalar_tensor_tensor(out=hid[:, j % 2, :], in0=gact[:, j % 2, :], scalar=xt[:, j % RING, D:D + 1],
                                       in1=g_bank[j % 2][:, FF:2 * FF], op0=ALU.mult, op1=ALU.mult).then_inc(s["hid_ok"], 1)

            def hid_low(j):
                dve.wait_ge(s["hidT_hi"], j + 1)
                v.tensor_tensor(hidT[:, j % 2, 1, :], hT_bank[j % 2][:, 0:FF], hidT[:, j % 2, 0, :].bitcast(F32),
                                ALU.subtract).then_inc(s["hidT_ok"], 1)

            pipeline(TILES, [(0, x_low), (1, hidden), (2, hid_low)])

            def sum_stats(b):
                dve.wait_ge(ld_y[b], 32)
                if b >= 2:
                    dve.wait_ge(s["z3_ok"], b - 1)
                v.tensor_tensor(ysum[:, b % 2], yk[b][:, 0], yk[b][:, 1], ALU.add).then_inc(s["ysum_ok"], 1)
                dve.wait_ge(s["ysum_ok"], b + 1)
                layer_stats(b, lambda i: ysum[:, b % 2, i], st3, mv3, nm3, ve3, s["moments3"], s["ve3_ok"])

            def finish(b):
                dve.wait_ge(s["z3_ok"], b + 1)
                v.tensor_tensor(fin[:, b % 2], z3[:, b % 2], mod_bc[:, b, 3:4].to_broadcast([P, NT, D]),
                                ALU.mult).then_inc(s["fin_ok"], 1)
                dve.wait_ge(s["fin_ok"], b + 1)
                dve.wait_ge(s["xb_ok"], 1)
                v.tensor_tensor(res[b], fin[:, b % 2], x_sb[:, b * NT:(b + 1) * NT, :], ALU.add).then_inc(s["res_ok"], 1)

            pipeline(B, [(0, sum_stats), (1, finish)])

        @block.tensor
        def _(pe):
            mm = nc.tensor.matmul
            turn = nc.tensor.transpose
            pe.wait_ge(s["ld_mod"], 16)
            pe.wait_ge(s["scond_ok"], 1)
            for n, r in enumerate((0, 1, 3, 4)):
                last = mm(m_ps[:, n * B:(n + 1) * B], wmod_sb[:, r * D:(r + 1) * D], scond[:, 0:B], start=True, stop=True)
            last.then_inc(s["modcol_ps"], 1)
            mm(n_ps[0:SEL, :], scond[:], wmod_sb[:, 2 * D:6 * D], start=True, stop=True).then_inc(s["mod4_ps"], 1)

            def turn_z(b):
                pe.wait_ge(s["ld_cst"], 16)
                pe.wait_ge(s["z_ok"], b + 1)
                if b >= 1:
                    pe.wait_ge(s["qfT_ok"], b)
                for i in range(NT):
                    last = turn(ta_ps[:, i * P:(i + 1) * P], z[:, b % 2, i], ident)
                last.then_inc(s["zT_ps"], 1)

            def modulation_rows():
                pe.wait_ge(s["row_parts_ok"], 1)
                pe.wait_ge(s["sel_r_ok"], 1)
                rows4 = row_parts[:, 0:4].rearrange("b r d -> b (r d)")
                pe.wait_ge(s["mcol_ok"], 2)
                pe.wait_ge(s["mod4_ok"], 1)
                for b, ps in enumerate((w_ps, n_ps, tb_ps, m_ps)):
                    mm(ps[:], sel_r[:, b], rows4, start=True, stop=True).then_inc(s["modbc_ps"], 1)

            def project(half):
                def stage(b):
                    pe.wait_ge(s["hT_ok"], b + 1)
                    pe.wait_ge(s["wq_ok"], 1)
                    pe.wait_ge(s["bias_ok"], 1)
                    pe.wait_ge(s["onesr_ok"], 1)
                    if b >= 1:
                        pe.wait_ge(s["qk_ok"], 2 * (b - 1) + half + 1)
                        pe.wait_ge(s["v_ok"], b)
                    for i in (2 * half, 2 * half + 1):
                        hi, lo = (part[:, b % 2, i * P:(i + 1) * P] for part in (hT_hi, hT_lo))
                        for dst, c in ((qk_ps[:, i].rearrange("p q d -> p (q d)"), slice(0, 2 * D)),
                                       (v_ps[:, i * D:(i + 1) * D], slice(2 * D, 3 * D))):
                            mm(dst, ones_r[:], bias_parts[:, c], start=True, stop=False)
                            mm(dst, hi, wq_hi[:, c], start=False, stop=False)
                            mm(dst, hi, wq_lo[:, c], start=False, stop=False)
                            last = mm(dst, lo, wq_hi[:, c], start=False, stop=True)
                    last.then_inc(s["qkv_ps"], 1)
                return stage

            def turn_q(b):
                pe.wait_ge(s["rot_ok"], 2 * b + 2)
                pe.wait_ge(s["hf_ok"], b + 1)
                for i in range(NT):
                    last = turn(ta_ps[:, i * P:(i + 1) * P], ra[:, b % 2, i, 0], ident)
                last.then_inc(s["qT_ps"], 1)

            def keys_values(b):
                pe.wait_ge(s["kf_ok"], b + 1)
                pe.wait_ge(s["v_ok"], b + 1)
                if b == 0:
                    pe.wait_ge(s["modbc_ok"], B)
                else:
                    pe.wait_ge(s["den_ok"], b)
                for i in range(NT):
                    last = mm(m_ps[:, VK:VK + D + 1], kf[:, b % 2, i], v_sb[:, b % 2, i], start=(i == 0), stop=(i == NT - 1))
                last.then_inc(s["vk_ps"], 1)

            def attend(b):
                pe.wait_ge(s["kv_ok"], b + 1)
                pe.wait_ge(s["qfT_ok"], b + 1)
                if b >= 1:
                    pe.wait_ge(s["o_ok"], b)
                for i in range(NT):
                    qi = qfT[:, b % 2, i * P:(i + 1) * P]
                    mm(n_ps[:, i * D:(i + 1) * D], qi, kv[:, b % 2, 0:D], start=True, stop=True)
                    last = mm(m_ps[:, DEN + i * H:DEN + (i + 1) * H], qi, kv[:, b % 2, D:D + H], start=True, stop=True)
                last.then_inc(s["res_ps"], 1)

            def turn_attn(b):
                pe.wait_ge(s["attn_ok"], b + 1)
                if b == 0:
                    pe.wait_ge(s["modbc_ok"], 3)
                else:
                    pe.wait_ge(s["h2T_ok"], b)
                for i in range(NT):
                    last = turn(tb_ps[:, i * P:(i + 1) * P], attn[:, b % 2, i], ident)
                last.then_inc(s["aT_ps"], 1)

            def project_out(b):
                pe.wait_ge(s["attnT_ok"], b + 1)
                for i in range(NT):
                    oi = n_ps[:, i * D:(i + 1) * D]
                    mm(oi, ones_r[:], bias_parts[:, 3 * D:4 * D], start=True, stop=False)
                    last = mm(oi, attnT[:, b % 2, i * P:(i + 1) * P], watt_sb[:, W_OUT:W_OUT + D], start=False, stop=True)
                last.then_inc(s["o_ps"], 1)

            def turn_z2(b):
                pe.wait_ge(s["z2_ok"], b + 1)
                pe.wait_ge(s["attnT_ok"], b + 1)
                for i in range(NT):
                    last = turn(tb_ps[:, i * P:(i + 1) * P], z2[:, b % 2, i], ident)
                last.then_inc(s["h2T_ps"], 1)

            def route(b):
                pe.wait_ge(s["h2T_ok"], b + 1)
                if b >= 1:
                    pe.wait_ge(s["pos_ok"], b)
                for i in range(NT):
                    last = mm(w_ps[:, LG + i * NE:LG + (i + 1) * NE], h2T[:, b % 2, i * P:(i + 1) * P],
                              watt_sb[:, W_ROUTER:W_ROUTER + NE], start=True, stop=True)
                last.then_inc(s["lg_ps"], 1)

            def rank(b):
                pe.wait_ge(s["sel_ok"], b + 1)
                pe.wait_ge(s["up_ok"], 1)
                pe.wait_ge(s["ones_ok"], 1)
                pe.wait_ge(s["carry16_ok"], b + 1)
                rk = w_ps[:, RK:RK + NT * NE].rearrange("p (t e) -> p t e", e=NE)
                mm(rk, up16[:], sel16[:], start=True, stop=False)
                for d in range(1, NT):
                    mm(rk[:, d:], ones16[:], sel16[:, 0:NT - d], start=False, stop=False)
                mm(rk, ones16[:], carry16[:].unsqueeze(1).to_broadcast([P, NT, NE]), start=False, stop=True).then_inc(s["rank_ps"], 1)

            pipeline(B, [(2, followed(turn_z, modulation_rows)), (3, attend), (2, project(0)), (2, project(1)), (4, turn_z2),
                         (3, turn_attn), (4, route), (3, project_out), (2, turn_q), (4, rank), (2, keys_values)])
            pe.wait_ge(s["h2T_ok"], B)
            pe.wait_ge(s["attnT_ok"], B)
            for b in range(B):
                last = mm(tb_ps[:, b * P:(b + 1) * P], sel_r[:, b], row_parts[:, 4], start=True, stop=True)
            last.then_inc(s["beta_ps"], 1)
            pe.wait_ge(s["carry16_ok"], B + 1)
            mm(w_ps[:, CNT:CNT + NE], ones16[:], carry16[:], start=True, stop=True).then_inc(s["cnt_ps"], 1)

            pe.wait_ge(s["tab_ok"], 1)
            pe.wait_ge(s["beta_ok"], 1)
            pe.wait_ge(s["w_lo"], W_POOL)
            pe.wait_ge(s["w_lo2"], NE - W_POOL)

            def x_turn(j):
                pe.wait_ge(ld_tile[j % RING], 16 * (j // RING) + 16)
                if j >= 2:
                    pe.wait_ge(s["xT_ok"], j - 1)
                turn(xT_bank[j % 2][:, 0:P], xt[:, j % RING, 0:D], ident).then_inc(s["xT_ps"], 1)

            def gate_up(j):
                if j % GROUP == 0:
                    experts.extend(table_values(mybir.EngineType.PE, tile_tab[0:1, 0, j:j + GROUP], NE - 1))
                e = bass.ds(experts[j], 1)
                pe.wait_ge(s["xT_ok"], j + 1)
                if j >= 2:
                    pe.wait_ge(s["hid_ok"], j - 1)
                for n, (part, w) in enumerate(((0, w_high), (0, w_low), (1, w_high))):
                    last = mm(g_bank[j % 2][:], xT[:, j % 2, part, :], w[:, e, 0:2 * FF], start=(n == 0), stop=(n == 2))
                last.then_inc(s["gu_ps"], 1)

            def hid_turn(j):
                pe.wait_ge(s["hid_ok"], j + 1)
                if j >= 2:
                    pe.wait_ge(s["hidT_ok"], j - 1)
                for f in range(FB):
                    last = turn(hT_bank[j % 2][:, f * P:(f + 1) * P], hid[:, j % 2, f * P:(f + 1) * P], ident)
                last.then_inc(s["hidT_ps"], 1)

            def down(j):
                e = bass.ds(experts[j], 1)
                pe.wait_ge(s["hidT_ok"], j + 1)
                if j >= 2:
                    pe.wait_ge(s["yrow_ok"], j - 1)
                for f in range(FB):
                    for n, (part, w) in enumerate(((0, w_high), (0, w_low), (1, w_high))):
                        last = mm(y_bank[j % 2][:, 0, 0], hidT[:, j % 2, part, f * P:(f + 1) * P],
                                  w[:, e, 2 * FF + f * D:2 * FF + (f + 1) * D],
                                  start=(f == 0 and n == 0), stop=(f == FB - 1 and n == 2))
                last.then_inc(s["y_ps"], 1)

            experts = []
            pipeline(TILES, [(0, x_turn), (1, gate_up), (2, hid_turn), (3, down)])


def _shape_constants():
    import numpy as np
    c = np.zeros((P, C_ALL), np.float32)
    r = np.arange(P)
    c[:, C_ID:C_ID + P] = np.eye(P)
    c[:, C_BLK:C_BLK + D] = r[:, None] // DH == r[None, :] // DH
    c[:, C_HEAD:C_HEAD + H] = r[:, None] // DH == np.arange(H)[None, :]
    c[:, C_UP:C_UP + P] = r[:, None] < r[None, :]
    c[:, C_EXP:C_EXP + NE] = np.arange(NE)
    c[:, C_BASE:C_BASE + NE] = np.arange(NE) * REGION
    inv = (np.float32(1.0) / np.float32(THETA) ** (np.arange(0, DH, 2, dtype=np.float32) / np.float32(DH))).astype(np.float32)
    ang = np.outer(np.arange(L, dtype=np.float32), inv).astype(np.float32)
    cos = np.repeat(np.cos(ang), 2, axis=1)
    sin = np.repeat(np.sin(ang), 2, axis=1)
    sin[:, 0::2] *= -1
    for i in range(NT):
        c[:, C_COS + i * DH:C_COS + (i + 1) * DH] = cos[i * P:(i + 1) * P]
        c[:, C_SIN + i * DH:C_SIN + (i + 1) * DH] = sin[i * P:(i + 1) * P]
    rows = np.zeros((SEL, R_ALL), np.float32)
    for b in range(B):
        for row in (b, LOW + b):
            rows[row, R_SEL + b * P:R_SEL + (b + 1) * P] = 1
    rows[0, R_TILE:] = np.repeat(np.arange(TAB), NE)
    t = np.arange(TOKENS, dtype=np.int32).reshape(TT, P).T
    dests = np.stack([t + k * TOKENS for k in range(TOPK)], axis=-1)
    return c, rows, dests


def kernel(**inputs):
    import numpy as np
    import concourse.bacc as bacc
    from concourse.bass_utils import run_bass_kernel_spmd

    a = {k[3:]: np.asarray(v) for k, v in inputs.items()}
    consts, rows, dests = _shape_constants()
    gate, up, down = a["ffn_w_gate"], a["ffn_w_up"], a["ffn_w_down"]
    arrays = {
        "x": a["attn_x"].reshape(TOKENS, D),
        "watt": np.concatenate([a["attn_Wqkv"].T, a["attn_Wout"].T, a["ffn_w_router"].T], axis=1),
        "wexp": np.concatenate([gate.transpose(2, 0, 1), up.transpose(2, 0, 1),
                                down.reshape(NE, D, FB, P).transpose(3, 0, 2, 1).reshape(P, NE, FB * D)], axis=2),
        "wmod": a["wmod"],
        "cond": a["c"].T,
        "vecs": np.concatenate([a["attn_bqkv"], a["attn_bout"], a["attn_gq"], a["attn_gk"], a["attn_gout"],
                                a["ffn_ln_gamma"], a["ffn_ln_beta"]])[None, :],
        "consts": consts,
        "rows": rows,
        "dests": dests,
    }
    arrays = {k: np.ascontiguousarray(v) for k, v in arrays.items()}
    nc = bacc.Bacc("TRN2", target_bir_lowering=False, num_devices=1)
    aps = {k: nc.dram_tensor(k, v.shape, mybir.dt.from_np(v.dtype), kind="ExternalInput").ap() for k, v in arrays.items()}
    out = nc.dram_tensor("out", (TOKENS, D), mybir.dt.float32, kind="ExternalOutput").ap()
    adaln_block(nc, out=out, **aps)
    r = run_bass_kernel_spmd(nc, [arrays], core_ids=[0])
    return r.results[0]["out"].reshape(B, L, D)
```

```python
import concourse.bass as bass
from concourse import mybir
from contextlib import ExitStack

P = 128
B, L, D = 4, 512, 128
NT = L // P
TOKENS = B * L
TT = TOKENS // P
H, DH = 16, 8
NE, FF, TOPK = 8, 256, 2
FB = FF // P
RMS_EPS = 1.1920929e-07
LIN_EPS = 1e-06
LN_EPS = 1e-05
THETA = 10000.0

REGION = TOKENS + P
DEAD_ROW = NE * REGION
TILES = TOPK * TT + NE - 1
STAGES = 4
RING = 12
Y_RING = 8
GROUP = 4
TAB = -(-TILES // GROUP) * GROUP
REC = D + 2
W_BLOCKS = 3 * FB
W_RING = 3
W_POOL = 7
SKIP = 1 << 20

QKV = 3 * D
LOW = 32
SEL = LOW + B

C_ID = 0
C_BLK = C_ID + P
C_HEAD = C_BLK + D
C_UP = C_HEAD + H
C_EXP = C_UP + P
C_BASE = C_EXP + NE
C_COS = C_BASE + NE
C_SIN = C_COS + NT * DH
C_ALL = C_SIN + NT * DH
R_SEL = 0
R_TILE = R_SEL + B * P
R_ALL = R_TILE + TAB * NE

V_BQKV, V_BOUT, V_GQ, V_GK, V_GOUT, V_GAMMA, V_BETA, V_ALL = 0, 384, 512, 640, 768, 896, 1024, 1152
W_QKV, W_OUT, W_ROUTER, W_ATT = 0, 3 * D, 4 * D, 4 * D + NE


def adaln_block(nc, x, watt, wexp, wmod, cond, vecs, consts, rows, dests, out):
    F32 = mybir.dt.float32
    F32R = mybir.dt.float32r
    BF16 = mybir.dt.bfloat16
    I32 = mybir.dt.int32
    U32 = mybir.dt.uint32
    ALU = mybir.AluOpType
    ACT = mybir.ActivationFunctionType
    AX = mybir.AxisListType

    sorted_rows = nc.dram_tensor("sorted_rows", [DEAD_ROW + P, REC], F32).ap()
    expert_rows = nc.dram_tensor("expert_rows", [TOPK * TOKENS, D], F32).ap()
    x_v = x.rearrange("(t p) d -> p t d", p=P)
    out_v = out.rearrange("(t p) d -> p t d", p=P)
    rows_v = expert_rows.rearrange("(k t p) d -> p k t d", k=TOPK, p=P)

    ctx = ExitStack()
    with ctx:
        def sb(name, shape, dt=F32):
            return ctx.enter_context(nc.sbuf_tensor(name, shape, dt))

        def sem(name):
            return ctx.enter_context(nc.semaphore(name))

        x_sb = sb("x_sb", [P, TT, D])
        cst = sb("cst", [P, C_ALL])
        row_sb = sb("row_sb", [SEL, R_ALL])
        dest_sb = sb("dest_sb", [P, TT, TOPK], I32)
        gqk = sb("gqk", [P, 2 * D])
        vec_sb = sb("vec_sb", [SEL, 3 * D])
        bias_in = sb("bias_in", [LOW + 1, 4 * D])
        bias_parts = sb("bias_parts", [LOW + 1, 4 * D], F32R)
        ones_r = sb("ones_r", [LOW + 1, P], F32R)
        watt_sb = sb("watt_sb", [P, W_ATT])
        wq_hi = sb("wq_hi", [P, 3 * D], F32R)
        wq_lo = sb("wq_lo", [P, 3 * D], F32R)
        wmod_sb = sb("wmod_sb", [P, 6 * D])
        cond_sb = sb("cond_sb", [P, B])
        warm = sb("warm", [1, 1])
        scond = sb("scond", [P, SEL])
        ones16 = sb("ones16", [P, P], BF16)
        up16 = sb("up16", [P, P], BF16)
        neg_half = sb("neg_half", [P, NT])
        half_pair = sb("half_pair", [P, NT, 2])
        rope_c = sb("rope_c", [P, NT, 2 * D])
        rope_s = sb("rope_s", [P, NT, 2 * D])
        mcol = sb("mcol", [P, 2, 2, B])
        mod4 = sb("mod4", [SEL, 4, D])
        mod_sgn = sb("mod_sgn", [SEL, 2, D])
        mod_mag = sb("mod_mag", [SEL, 2, D])
        mod_row = sb("mod_row", [SEL, 5, D])
        row_parts = sb("row_parts", [SEL, 5, D], F32R)
        sel_r = sb("sel_r", [SEL, B, P], F32R)
        mod_bc = sb("mod_bc", [P, B, 4, D])
        beta_bc = sb("beta_bc", [P, B, D])

        st1 = sb("st1", [P, B, NT, 6])
        mv1 = sb("mv1", [P, B, NT, 2])
        ve1 = sb("ve1", [P, B, NT])
        rs1 = sb("rs1", [P, B, NT])
        z = sb("z", [P, 2, NT, D])
        h_f = sb("h_f", [P, L])
        hT_hi = sb("hT_hi", [P, 2, L], F32R)
        hT_lo = sb("hT_lo", [P, 2, L], F32R)
        qkv_sb = sb("qkv_sb", [P, 2, NT, QKV + 1])
        sq_junk = sb("sq_junk", [P, NT * 2, D], BF16)
        ssq = sb("ssq", [P, B, NT, 2])
        msq = sb("msq", [P, B, NT, 2])
        rqk = sb("rqk", [P, B, NT, 2])
        ra = sb("ra", [P, 2, NT, 2, D])
        rb = sb("rb", [P, NT, 2, D])
        kf = sb("kf", [P, 2, NT, D])
        qfT = sb("qfT", [P, 2, L])
        kv = sb("kv", [P, 2, D + H])
        den = sb("den", [P, B, NT, H])
        rden = sb("rden", [P, B, NT, H])
        attn = sb("attn", [P, 2, NT, D])
        attnT = sb("attnT", [P, 2, L])
        o_sb = sb("o_sb", [P, 2, NT, D])
        o_junk = sb("o_junk", [P, NT, D], BF16)
        oss = sb("oss", [P, B, NT])
        oms = sb("oms", [P, B, NT])
        ors = sb("ors", [P, B, NT])
        og = sb("og", [P, NT, D])
        st2 = sb("st2", [P, B, NT, 6])
        mv2 = sb("mv2", [P, B, NT, 2])
        ve2 = sb("ve2", [P, B, NT])
        rs2 = sb("rs2", [P, B, NT])
        z2 = sb("z2", [P, 2, NT, D])
        h2c = sb("h2c", [P, NT, D])
        rec = sb("rec", [P, 2, NT, TOPK, REC])
        h2T = sb("h2T", [P, 2, L])
        top = sb("top", [P, NT, 8])
        topi = sb("topi", [P, NT, 8], U32)
        gap = sb("gap", [P, NT])
        tanh_gap = sb("tanh_gap", [P, NT])
        onehot = sb("onehot", [P, NT, TOPK, NE])
        sel16 = sb("sel16", [P, NT, NE], BF16)
        selsum = sb("selsum", [P, NE])
        carry = sb("carry", [P, NE])
        carry16 = sb("carry16", [P, NE], BF16)
        pos = sb("pos", [P, NT, NE])
        posk = sb("posk", [P, NT, TOPK, NE])
        slot = sb("slot", [P, 2, NT, TOPK], U32)
        pad = sb("pad", [P, REC])

        cnt_i = sb("cnt_i", [1, NE], I32)
        cnt_p = sb("cnt_p", [1, NE], I32)
        nt_i = sb("nt_i", [1, NE], I32)
        nt_f = sb("nt_f", [1, NE])
        nt_one = sb("nt_one", [1, NE])
        nt_cum = sb("nt_cum", [1, NE])
        past = sb("past", [1, TAB, NE])
        pastn = sb("pastn", [1, TAB, NE])
        ex_f = sb("ex_f", [1, TAB])
        before = sb("before", [1, TAB])
        ahead = sb("ahead", [1, TAB])
        row_f = sb("row_f", [1, TAB])
        tile_tab = sb("tile_tab", [1, 2, TAB], I32)

        w_in = sb("w_in", [P, W_RING, W_BLOCKS, D])
        w_parts = sb("w_parts", [P, NE, W_BLOCKS, 2, D], F32R)
        st3 = sb("st3", [P, B, NT, 6])
        mv3 = sb("mv3", [P, B, NT, 2])
        ve3 = sb("ve3", [P, B, NT])
        rs3 = sb("rs3", [P, B, NT])
        nm3 = sb("nm3", [P, B, NT])
        xt = rec[:].rearrange("p b t k c -> p (b t k) c")[:, 0:RING]
        xT = hT_lo[:, 0].rearrange("p (h n t) -> p h n t", h=2, n=2)
        hidT = hT_hi[:].rearrange("p h (n f) -> p h n f", n=2)
        yrow = attnT[:].rearrange("p h (i d) -> p (h i) d", d=D)
        gact = og[:].rearrange("p (h i) d -> p h (i d)", h=2)
        hid = h2c[:].rearrange("p (h i) d -> p h (i d)", h=2)
        yk = ([qkv_sb[:, h].rearrange("p t c -> p (t c)")[:, 0:TOPK * NT * D].rearrange("p (k t d) -> p k t d", k=TOPK, d=D)
               for h in range(2)] + [ra[:, h].rearrange("p (k t) q d -> p k (t q) d", k=TOPK) for h in range(2)])
        ysum = [attn[:, 0], attn[:, 1], qfT[:, 0].rearrange("p (t d) -> p t d", d=D), qfT[:, 1].rearrange("p (t d) -> p t d", d=D)]
        z3 = z
        fin = z2
        res = [big[:, h] for big in (o_sb, kf) for h in range(2)]

        ta_ps, tb_ps, n_ps, m_ps, w_ps, *qkv_bank = [
            ctx.enter_context(nc.psum_tensor(name, [P, 512], F32))
            for name in ("ta_ps", "tb_ps", "n_ps", "m_ps", "w_ps", "qkv_ps0", "qkv_ps1", "qkv_ps2")]
        QB = len(qkv_bank)
        VK, DEN = 0, 160
        LG, RK, CNT = 0, 64, 128
        xT_bank, g_bank, hT_bank, y_bank = (ta_ps, tb_ps), (qkv_bank[2], n_ps), (m_ps, w_ps), qkv_bank[0:2]

        s = {n: sem(n) for n in (
            "ld_x0 ld_x1 ld_x2 ld_x3 ld_cst ld_gqk ld_vec ld_bias ld_cond ld_mod ld_att ld_rows ld_dest "
            "bias_zero bias_hi bias_ok onesr_ok wq_hi_ok wq_ok scond0 scond_ok sel_r_ok ones_ok up_ok exp_ok rope_ok vone_ok "
            "modcol_ps mcol_ok mod4_ps mod4_ok row_step row_parts_ok modbc_ps modbc_ok beta_ps beta_ok "
            "moments1 ve1_ok rs1_ok z_ok zT_ps hf_ok hT_hi_ok hT_ok qkv_ps qkv_ok ssq_ok msq_ok rqk_ok "
            "ra_ok rot_ok kf_ok qT_ps qfT_ok vk_ps kv_ok res_ps den_ok rden_ok attn_ok aT_ps attnT_ok o_ps o_ok "
            "oss_ok oms_ok ors_ok og_ok x2_ok moments2 ve2_ok rs2_ok z2_ok h2T_ps h2T_ok h2c_ok h2_ok dup_ok "
            "lg_ps choose_step gap_ok tanh_ok weight_ok sel_ok selsum_ok carry_ok carry16_ok rank_ps "
            "pos_ok posk_ok slot_ok pad_ok pad_dest_ok scat0 scat1 "
            "cnt_ps cnt_ok nt_ok table_step tab_ok pads_out w_hi w_lo w_lo2 "
            "xT_ps xT_hi xT_ok gu_ps gact_ok hid_ok hidT_ps hidT_hi hidT_ok y_ps yrow_ok "
            "xb_ok ysum_ok moments3 mv3_ok ve3_ok rs3_ok nm3_ok z3_ok fin_ok res_ok last_ok").split()}
        ld_w = [sem(f"ld_w{q}") for q in range(W_RING)]
        ld_tile = [sem(f"ld_tile{q}") for q in range(RING)]
        y_out = [sem(f"y_out{q}") for q in range(Y_RING)]
        ld_y = [sem(f"ld_y{b}") for b in range(B)]
        stored = sem("stored")
        block = ctx.enter_context(nc.Block())

        ident = cst[:, C_ID:C_ID + P]

        def pipeline(count, stages):
            for n in range(count + max(k for k, _ in stages)):
                for k, stage in stages:
                    if 0 <= n - k < count:
                        stage(n - k)

        def later(stage, first=1):
            return lambda item: stage(item) if item >= first else None

        def only(item, work):
            return lambda i: work() if i == item else None

        def table_values(engine, entries, max_val):
            _, values = nc.values_load_multi_w_load_instructions(
                entries, engines=[engine], min_val=0, max_val=max_val,
                skip_runtime_bounds_check_because="the entries are within this range by the arithmetic that makes them")
            return values

        @block.sync
        def _(sp):
            sp.dma_start(x_sb[:, 0:NT, :], x_v[:, 0:NT, :]).then_inc(s["ld_x0"], 16)
            sp.dma_start(cst[:], consts).then_inc(s["ld_cst"], 16)
            sp.dma_start(gqk[:], vecs[:, V_GQ:V_GQ + 2 * D].to_broadcast([P, 2 * D])).then_inc(s["ld_gqk"], 16)
            sp.dma_start(watt_sb[:], watt).then_inc(s["ld_att"], 16)
            for b in range(1, B):
                sp.dma_start(x_sb[:, b * NT:(b + 1) * NT, :], x_v[:, b * NT:(b + 1) * NT, :]).then_inc(s[f"ld_x{b}"], 16)
            sp.dma_start(row_sb[:], rows).then_inc(s["ld_rows"], 16)
            sp.dma_start(dest_sb[:], dests).then_inc(s["ld_dest"], 16)
            for e in range(NE):
                if e >= W_RING:
                    sp.wait_ge(s["w_lo"], e - W_RING + 1)
                sp.dma_start(w_in[:, e % W_RING], wexp[:, e]).then_inc(ld_w[e % W_RING], 16)

            sp.wait_ge(s["pad_dest_ok"], 1)
            sp.dma_start(sorted_rows[DEAD_ROW:DEAD_ROW + P, :], pad[:]).then_inc(s["pads_out"], 16)
            sp.wait_ge(s["cnt_ok"], 1)
            for e in range(NE):
                if e % GROUP == 0:
                    counts = table_values(mybir.EngineType.SP, cnt_i[0:1, e:e + GROUP], TOKENS)
                sp.dma_start(sorted_rows[bass.ds(counts[e % GROUP] + e * REGION, P), :], pad[:]).then_inc(s["pads_out"], 16)
            sp.wait_ge(s["tab_ok"], 1)
            sp.wait_ge(s["pads_out"], 16 * (NE + 1))
            sp.wait_ge(s["scat0"], 16 * NT * TOPK * 2)
            sp.wait_ge(s["scat1"], 16 * NT * TOPK * 2)
            for j in range(TILES):
                q = j % RING
                if j % GROUP == 0:
                    first_rows = table_values(mybir.EngineType.SP, tile_tab[0:1, 1, j:j + GROUP], DEAD_ROW)
                if j >= RING:
                    last = j - RING
                    sp.wait_ge(s["xT_ps"], last + 1)
                    sp.wait_ge(s["hid_ok"], last + 1)
                    sp.wait_ge(y_out[last % Y_RING], 16 * (last // Y_RING + 1))
                sp.dma_start(xt[:, q, :], sorted_rows[bass.ds(first_rows[j % GROUP], P), :]).then_inc(ld_tile[q], 16)

            for q in range(Y_RING):
                sp.wait_ge(y_out[q], 16 * len(range(q, TILES, Y_RING)))
            for b in range(B):
                for k in range(TOPK):
                    sp.dma_start(yk[b][:, k], rows_v[:, k, b * NT:(b + 1) * NT, :]).then_inc(ld_y[b], 16)
            for b in range(B):
                sp.wait_ge(*((s["res_ok"], b + 1) if b < B - 1 else (s["last_ok"], 1)))
                sp.dma_start(out_v[:, b * NT:(b + 1) * NT, :], res[b]).then_inc(stored, 16)
            sp.wait_ge(stored, 16 * B)

        @block.scalar
        def _(act):
            act.dma_start(cond_sb[:], cond).then_inc(s["ld_cond"], 16)
            act.dma_start(wmod_sb[:], wmod).then_inc(s["ld_mod"], 16)
            act.wait_ge(s["exp_ok"], 1)
            nc.scalar.activation(warm[:], neg_half[0:1, 0:1], ACT.Silu)
            act.wait_ge(s["scond0"], 1)
            act.wait_ge(s["ld_cond"], 16)
            nc.scalar.activation(scond[:, 0:B], cond_sb[:], ACT.Silu)
            nc.scalar.activation(scond[:, LOW:LOW + B], cond_sb[:], ACT.Silu).then_inc(s["scond_ok"], 1)
            def modulate(b):
                act.wait_ge(s["zT_ps"], b + 1)
                act.wait_ge(s["mcol_ok"], 2)
                if b >= 1:
                    act.wait_ge(s["hT_ok"], b)
                nc.scalar.activation(h_f[:], ta_ps[:], ACT.Identity, bias=mcol[:, 0, 0, b:b + 1],
                                     scale=mcol[:, 0, 1, b:b + 1]).then_inc(s["hf_ok"], 1)
                act.wait_ge(s["hf_ok"], b + 1)
                if b >= 2:
                    act.wait_ge(s["qkv_ps"], NT * (b - 1))
                nc.scalar.copy(hT_hi[:, b % 2], h_f[:]).then_inc(s["hT_hi_ok"], 1)

            def qkv_back(half):
                def stage(b):
                    if b == 0:
                        act.wait_ge(s["vone_ok"], 1)
                    if b >= 2:
                        act.wait_ge(s["ra_ok"], 2 * (b - 2) + half + 1)
                        act.wait_ge(s["ssq_ok"], 2 * (b - 2) + half + 1)
                        act.wait_ge(s["vk_ps"], b - 1)
                    for i in (2 * half, 2 * half + 1):
                        n = b * NT + i
                        act.wait_ge(s["qkv_ps"], n + 1)
                        nc.scalar.copy(qkv_sb[:, b % 2, i, 0:QKV], qkv_bank[n % QB][:, 0:QKV]).then_inc(s["qkv_ok"], 1)
                return stage

            def squares(half):
                def stage(b):
                    act.wait_ge(s["qkv_ok"], b * NT + 2 * half + 2)
                    if b >= 1:
                        act.wait_ge(s["ssq_ok"], 2 * b)
                    for i in (2 * half, 2 * half + 1):
                        for j in range(2):
                            last = nc.scalar.activation(sq_junk[:, 2 * i + j], qkv_sb[:, b % 2, i, j * D:(j + 1) * D], ACT.Square,
                                                        accum_out=ssq[:, b, i, j:j + 1])
                    last.then_inc(s["ssq_ok"], 1)
                return stage

            def queries(b):
                act.wait_ge(s["qT_ps"], b + 1)
                if b >= 2:
                    act.wait_ge(s["res_ps"], b - 1)
                nc.scalar.activation(qfT[:, b % 2], ta_ps[:], ACT.Relu).then_inc(s["qfT_ok"], 1)

            def attn_back(b):
                act.wait_ge(s["aT_ps"], b + 1)
                if b >= 2:
                    act.wait_ge(s["o_ps"], b - 1)
                nc.scalar.copy(attnT[:, b % 2], tb_ps[:]).then_inc(s["attnT_ok"], 1)

            def out_back(b):
                act.wait_ge(s["o_ps"], b + 1)
                if b >= 2:
                    act.wait_ge(s["og_ok"], b - 1)
                nc.scalar.copy(o_sb[:, b % 2].rearrange("p t d -> p (t d)"), n_ps[:]).then_inc(s["o_ok"], 1)

            def out_squares(b):
                act.wait_ge(s["o_ok"], b + 1)
                if b >= 1:
                    act.wait_ge(s["oss_ok"], b)
                for i in range(NT):
                    last = nc.scalar.activation(o_junk[:, i], o_sb[:, b % 2, i], ACT.Square, accum_out=oss[:, b, i:i + 1])
                last.then_inc(s["oss_ok"], 1)

            def modulate2(b):
                act.wait_ge(s["h2T_ps"], b + 1)
                if b >= 2:
                    act.wait_ge(s["lg_ps"], b - 1)
                nc.scalar.activation(h2T[:, b % 2], tb_ps[:], ACT.Identity, bias=mcol[:, 1, 0, b:b + 1],
                                     scale=mcol[:, 1, 1, b:b + 1]).then_inc(s["h2T_ok"], 1)

            def repeat_row(b):
                act.wait_ge(s["h2_ok"], b + 1)
                nc.scalar.copy(rec[:, b % 2, :, 1, 0:D], rec[:, b % 2, :, 0, 0:D]).then_inc(s["dup_ok"], 1)

            def router_tanh(b):
                act.wait_ge(s["gap_ok"], b + 1)
                if b >= 1:
                    act.wait_ge(s["weight_ok"], b)
                nc.scalar.activation(tanh_gap[:], gap[:], ACT.Tanh, scale=0.5).then_inc(s["tanh_ok"], 1)

            def weight_high_parts():
                act.wait_ge(s["ld_att"], 16)
                nc.scalar.copy(wq_hi[:], watt_sb[:, W_QKV:W_QKV + 3 * D]).then_inc(s["wq_hi_ok"], 1)
                act.wait_ge(s["ld_bias"], 32)
                nc.scalar.copy(bias_parts[:], bias_in[:]).then_inc(s["bias_hi"], 1)

            def modulation_copy():
                act.wait_ge(s["mod4_ps"], 1)
                nc.scalar.copy(mod4[:].rearrange("b r d -> b (r d)"), n_ps[0:SEL, :]).then_inc(s["mod4_ok"], 1)

            def modulation_rows():
                for b, ps in enumerate((w_ps, n_ps, tb_ps, w_ps)):
                    act.wait_ge(s["modbc_ps"], b + 1)
                    nc.scalar.copy(mod_bc[:, b], ps[:].rearrange("p (r d) -> p r d", d=D)).then_inc(s["modbc_ok"], 1)

            def high_parts(first, end):
                for e in range(first, end):
                    act.wait_ge(ld_w[e % W_RING], 16 * (e // W_RING + 1))
                    nc.scalar.copy(w_parts[:, e, :, 0], w_in[:, e % W_RING]).then_inc(s["w_hi"], 1)

            weight_high_parts()
            pipeline(B, [(5, only(1, lambda: high_parts(5, W_POOL))), (4, only(0, lambda: high_parts(0, 2))),
                         (6, repeat_row), (6, router_tanh), (3, modulate), (3, only(0, modulation_copy)),
                         (3, qkv_back(0)), (4, attn_back), (3, squares(0)), (5, modulate2), (3, qkv_back(1)),
                         (3, squares(1)), (4, out_back), (3, only(0, modulation_rows)), (4, out_squares),
                         (4, only(0, lambda: high_parts(2, 5))), (3, queries)])
            high_parts(W_POOL, NE)
            act.wait_ge(s["beta_ps"], 1)
            nc.scalar.copy(beta_bc[:].rearrange("p b d -> p (b d)"), tb_ps[:]).then_inc(s["beta_ok"], 1)

            def x_high(j):
                act.wait_ge(s["xT_ps"], j + 1)
                if j >= 2:
                    act.wait_ge(s["gu_ps"], j - 1)
                nc.scalar.copy(xT[:, j % 2, 0, :], xT_bank[j % 2][:, 0:P]).then_inc(s["xT_hi"], 1)

            def gate(j):
                act.wait_ge(s["gu_ps"], j + 1)
                if j >= 2:
                    act.wait_ge(s["hid_ok"], j - 1)
                nc.scalar.activation(gact[:, j % 2, :], g_bank[j % 2][:, 0:FF], ACT.Silu).then_inc(s["gact_ok"], 1)

            def hid_high(j):
                act.wait_ge(s["hidT_ps"], j + 1)
                if j >= 2:
                    act.wait_ge(s["y_ps"], j - 1)
                nc.scalar.copy(hidT[:, j % 2, 0, :], hT_bank[j % 2][:, 0:FF]).then_inc(s["hidT_hi"], 1)

            pipeline(TILES, [(0, x_high), (1, gate), (2, hid_high)])

            for b in range(B):
                act.wait_ge(s["nm3_ok"], b + 1)
                if b >= 2:
                    act.wait_ge(s["fin_ok"], b - 1)
                for i in range(NT):
                    last = nc.scalar.activation(z3[:, b % 2, i], ysum[b][:, i], ACT.Identity,
                                                bias=nm3[:, b, i:i + 1], scale=rs3[:, b, i:i + 1])
                last.then_inc(s["z3_ok"], 1)

        @block.gpsimd
        def _(pool):
            g = nc.gpsimd
            g.memset(neg_half[:], -0.5).then_inc(s["exp_ok"], 1)
            g.memset(scond[:], 0.0).then_inc(s["scond0"], 1)
            g.memset(bias_in[:], 0.0).then_inc(s["bias_zero"], 1)
            pool.wait_ge(s["bias_zero"], 1)
            for first in (0, LOW):
                pool.dma_start(bias_in[first:first + 1, :], vecs[:, V_BQKV:V_BQKV + 4 * D]).then_inc(s["ld_bias"], 16)
            pool.dma_start(vec_sb[:], vecs[:, V_GOUT:V_ALL].to_broadcast([SEL, 3 * D])).then_inc(s["ld_vec"], 16)
            g.memset(half_pair[:, :, 0:1], 0.5).then_inc(s["exp_ok"], 1)
            g.memset(half_pair[:, :, 1:2], -0.5).then_inc(s["exp_ok"], 1)
            g.memset(qkv_sb[:, :, :, QKV:QKV + 1], 1.0).then_inc(s["vone_ok"], 1)
            g.memset(pad[:], 0.0).then_inc(s["pad_ok"], 1)
            pool.wait_ge(s["pad_ok"], 1)
            g.memset(pad[:, D + 1:D + 2].bitcast(I32), SKIP).then_inc(s["pad_dest_ok"], 1)
            pool.wait_ge(s["exp_ok"], 3)

            def norm_scale(b):
                pool.wait_ge(s["ve1_ok"], b + 1)
                g.tensor_tensor(rs1[:, b], ve1[:, b], neg_half[:], ALU.pow).then_inc(s["rs1_ok"], 1)

            def norm2_scale(b):
                pool.wait_ge(s["ve2_ok"], b + 1)
                g.tensor_tensor(rs2[:, b], ve2[:, b], neg_half[:], ALU.pow).then_inc(s["rs2_ok"], 1)

            def qk_scale(half):
                def stage(b):
                    n, t = 2 * b + half + 1, slice(2 * half, 2 * half + 2)
                    pool.wait_ge(s["ssq_ok"], n)
                    g.tensor_scalar(msq[:, b, t], ssq[:, b, t], 1.0 / D, RMS_EPS, ALU.mult, ALU.add).then_inc(s["msq_ok"], 1)
                    pool.wait_ge(s["msq_ok"], n)
                    g.tensor_tensor(rqk[:, b, t], msq[:, b, t], half_pair[:, t], ALU.pow).then_inc(s["rqk_ok"], 1)
                return stage

            def out_scale(b):
                pool.wait_ge(s["oss_ok"], b + 1)
                g.tensor_scalar(oms[:, b], oss[:, b], 1.0 / D, RMS_EPS, ALU.mult, ALU.add).then_inc(s["oms_ok"], 1)
                pool.wait_ge(s["oms_ok"], b + 1)
                g.tensor_tensor(ors[:, b], oms[:, b], neg_half[:], ALU.pow).then_inc(s["ors_ok"], 1)

            def scatter(i, k):
                def stage(b):
                    pool.wait_ge(s["slot_ok"], b + 1)
                    pool.wait_ge(s["dup_ok"], b + 1)
                    g.indirect_dma_start(
                        out=sorted_rows, out_offset=bass.IndirectOffsetOnAxis(ap=slot[:, b % 2, i, k:k + 1], axis=0),
                        in_=rec[:, b % 2, i, k, :], in_offset=None).then_inc(s[f"scat{b % 2}"], 16)
                return stage

            norm_scale(0)
            pool.wait_ge(s["ld_gqk"], 16)
            pool.wait_ge(s["ld_cst"], 16)
            heads = lambda ap: ap.rearrange("p (m e) -> p m e", e=DH)
            gains = heads(gqk[:])
            pairs = lambda ap: ap.rearrange("p m (c two) -> p m c two", two=2)
            for i in range(NT):
                cos = cst[:, C_COS + i * DH:C_COS + (i + 1) * DH].unsqueeze(1).to_broadcast([P, 2 * H, DH])
                g.tensor_tensor(heads(rope_c[:, i]), gains, cos, ALU.mult).then_inc(s["rope_ok"], 1)
            norm_scale(1)
            for i in range(NT):
                sin = pairs(cst[:, C_SIN + i * DH:C_SIN + (i + 1) * DH].unsqueeze(1).to_broadcast([P, 2 * H, DH]))
                for c in range(2):
                    g.tensor_tensor(pairs(heads(rope_s[:, i]))[:, :, :, c], pairs(gains)[:, :, :, 1 - c], sin[:, :, :, c],
                                    ALU.mult).then_inc(s["rope_ok"], 1)

            def split_weights(e):
                pool.wait_ge(s["w_hi"], e + 1)
                g.tensor_tensor(w_parts[:, e, :, 1], w_in[:, e % W_RING], w_parts[:, e, :, 0].bitcast(F32), ALU.subtract).then_inc(s["w_lo"], 1)

            pipeline(B, [(5, only(1, lambda: split_weights(5))), (7, scatter(3, 0)), (1, later(norm_scale, 2)),
                         (5, norm2_scale), (6, scatter(0, 1)), (6, scatter(1, 1)), (3, qk_scale(0)),
                         (6, scatter(0, 0)), (6, scatter(2, 0)), (3, qk_scale(1)),
                         (3, only(0, lambda: split_weights(0))), (3, only(0, lambda: split_weights(1))),
                         (6, scatter(1, 0)), (4, out_scale), (6, scatter(3, 1)), (6, scatter(2, 1)),
                         (4, only(0, lambda: split_weights(2))), (4, only(0, lambda: split_weights(3))),
                         (6, only(0, lambda: split_weights(6))), (4, only(1, lambda: split_weights(4)))])

            for j in range(TILES):
                q = j % RING
                pool.wait_ge(s["yrow_ok"], j + 1)
                g.indirect_dma_start(
                    out=expert_rows, out_offset=bass.IndirectOffsetOnAxis(ap=xt[:, q, D + 1:D + 2].bitcast(U32), axis=0),
                    in_=yrow[:, j % Y_RING, :], in_offset=None, bounds_check=TOPK * TOKENS - 1,
                    oob_is_err=False).then_inc(y_out[j % Y_RING], 16)

            def last_scale(b):
                pool.wait_ge(s["ve3_ok"], b + 1)
                g.tensor_tensor(rs3[:, b], ve3[:, b], neg_half[:], ALU.pow).then_inc(s["rs3_ok"], 1)
                pool.wait_ge(s["rs3_ok"], b + 1)
                g.tensor_tensor(nm3[:, b], nm3[:, b], rs3[:, b], ALU.mult).then_inc(s["nm3_ok"], 1)

            def add_residual(b):
                if b < B - 1:
                    pool.wait_ge(s["fin_ok"], b + 1)
                    pool.wait_ge(s["xb_ok"], 1)
                    g.tensor_tensor(res[b], fin[:, b % 2], x_sb[:, b * NT:(b + 1) * NT, :], ALU.add).then_inc(s["res_ok"], 1)

            pipeline(B, [(0, last_scale), (1, add_residual)])

        @block.vector
        def _(dve):
            v = nc.vector

            def layer_stats(b, st, mv, ve, moments_ok, ve_ok):
                for i in range(NT):
                    last = v.bn_stats(st[:, b, i], x_sb[:, b * NT + i, :])
                last.then_inc(moments_ok, 1)
                dve.wait_ge(moments_ok, 2 * b + 1)
                for i in range(NT):
                    last = v.bn_aggr(mv[:, b, i], st[:, b, i])
                last.then_inc(moments_ok, 1)
                dve.wait_ge(moments_ok, 2 * b + 2)
                v.tensor_scalar_add(ve[:, b], mv[:, b, :, 1], LN_EPS).then_inc(ve_ok, 1)

            def stats(b):
                dve.wait_ge(s[f"ld_x{b}"], 16)
                layer_stats(b, st1, mv1, ve1, s["moments1"], s["ve1_ok"])

            def stats2(b):
                dve.wait_ge(s["x2_ok"], b + 1)
                layer_stats(b, st2, mv2, ve2, s["moments2"], s["ve2_ok"])

            def norm(b):
                dve.wait_ge(s["rs1_ok"], b + 1)
                if b >= 2:
                    dve.wait_ge(s["zT_ps"], b - 1)
                for i in range(NT):
                    v.tensor_scalar(z[:, b % 2, i], x_sb[:, b * NT + i, :], mv1[:, b, i, 0:1], rs1[:, b, i:i + 1],
                                    ALU.subtract, ALU.mult).then_inc(s["z_ok"], 1)

            def low_part(b):
                dve.wait_ge(s["hT_hi_ok"], b + 1)
                if b >= 2:
                    dve.wait_ge(s["qkv_ps"], NT * (b - 1))
                v.tensor_tensor(hT_lo[:, b % 2], h_f[:], hT_hi[:, b % 2].bitcast(F32), ALU.subtract).then_inc(s["hT_ok"], 1)

            def rotate(half):
                def stage(b):
                    t = slice(2 * half, 2 * half + 2)
                    n = 2 * b + half + 1
                    join = lambda ap: ap.rearrange("p t q d -> p t (q d)")
                    pairs = lambda ap: ap.rearrange("p t (m two) -> p t m two", two=2)
                    r_a, r_b, qk = ra[:, b % 2, t], rb[:, t], qkv_sb[:, b % 2, t, 0:2 * D]
                    dve.wait_ge(s["qkv_ok"], b * NT + 2 * half + 2)
                    dve.wait_ge(s["rope_ok"], 3 * NT)
                    if b >= 2:
                        dve.wait_ge(s["kf_ok"], b - 1)
                        dve.wait_ge(s["qT_ps"], b - 1)
                    v.tensor_tensor(join(r_a), qk, rope_c[:, t], ALU.mult)
                    for c in range(2):
                        last = v.tensor_tensor(pairs(join(r_b))[:, :, :, c], pairs(qk)[:, :, :, 1 - c],
                                               pairs(rope_s[:, t])[:, :, :, c], ALU.mult)
                    last.then_inc(s["ra_ok"], 1)
                    dve.wait_ge(s["ra_ok"], n)
                    v.tensor_tensor(r_a, r_a, r_b, ALU.add).then_inc(s["rot_ok"], 1)
                return stage

            def keys(b):
                dve.wait_ge(s["rot_ok"], 2 * b + 2)
                dve.wait_ge(s["rqk_ok"], 2 * b + 2)
                if b >= 2:
                    dve.wait_ge(s["vk_ps"], b - 1)
                v.scalar_tensor_tensor(out=kf[:, b % 2], in0=ra[:, b % 2, :, 1, :], scalar=0.0,
                                       in1=rqk[:, b, :, 1:2].to_broadcast([P, NT, D]), op0=ALU.max,
                                       op1=ALU.mult).then_inc(s["kf_ok"], 1)

            def summary(b):
                dve.wait_ge(s["vk_ps"], b + 1)
                if b >= 2:
                    dve.wait_ge(s["res_ps"], b - 1)
                v.tensor_tensor(kv[:, b % 2, 0:D], m_ps[:, VK:VK + D], cst[:, C_BLK:C_BLK + D], ALU.mult)
                v.tensor_scalar(kv[:, b % 2, D:D + H], cst[:, C_HEAD:C_HEAD + H], m_ps[:, VK + D:VK + D + 1], None,
                                ALU.mult).then_inc(s["kv_ok"], 1)

            def divide(b):
                dve.wait_ge(s["res_ps"], b + 1)
                dve.wait_ge(s["rqk_ok"], 2 * b + 2)
                v.scalar_tensor_tensor(out=den[:, b], in0=rqk[:, b, :, 0:1].to_broadcast([P, NT, H]), scalar=LIN_EPS,
                                       in1=m_ps[:, DEN:DEN + NT * H].rearrange("p (t h) -> p t h", h=H), op0=ALU.mult,
                                       op1=ALU.add).then_inc(s["den_ok"], 1)
                dve.wait_ge(s["den_ok"], b + 1)
                v.reciprocal(rden[:, b], den[:, b]).then_inc(s["rden_ok"], 1)
                dve.wait_ge(s["rden_ok"], b + 1)
                if b >= 2:
                    dve.wait_ge(s["aT_ps"], b - 1)
                v.tensor_tensor(attn[:, b % 2].rearrange("p t (h e) -> p (t h) e", e=DH),
                                n_ps[:].rearrange("p (m e) -> p m e", e=DH),
                                rden[:, b].rearrange("p t h -> p (t h)").unsqueeze(2).to_broadcast([P, NT * H, DH]),
                                ALU.mult).then_inc(s["attn_ok"], 1)

            def gate_out(b):
                dve.wait_ge(s["o_ok"], b + 1)
                dve.wait_ge(s["modbc_ok"], B)
                v.tensor_tensor(og[:], o_sb[:, b % 2],
                                mod_bc[:, b, 0:1].to_broadcast([P, NT, D]), ALU.mult).then_inc(s["og_ok"], 1)

            def residual(b):
                dve.wait_ge(s["og_ok"], b + 1)
                dve.wait_ge(s["ors_ok"], b + 1)
                for i in range(NT):
                    t = b * NT + i
                    last = v.scalar_tensor_tensor(out=x_sb[:, t, :], in0=og[:, i, :], scalar=ors[:, b, i:i + 1],
                                                  in1=x_sb[:, t, :], op0=ALU.mult, op1=ALU.add)
                last.then_inc(s["x2_ok"], 1)

            def norm2(b):
                dve.wait_ge(s["rs2_ok"], b + 1)
                if b >= 2:
                    dve.wait_ge(s["h2T_ps"], b - 1)
                for i in range(NT):
                    v.tensor_scalar(z2[:, b % 2, i], x_sb[:, b * NT + i, :], mv2[:, b, i, 0:1], rs2[:, b, i:i + 1],
                                    ALU.subtract, ALU.mult).then_inc(s["z2_ok"], 1)

            def record_rows(b):
                dve.wait_ge(s["z2_ok"], (b + 1) * NT)
                v.tensor_tensor(h2c[:], z2[:, b % 2], mod_bc[:, b, 1:2].to_broadcast([P, NT, D]), ALU.mult).then_inc(s["h2c_ok"], 1)
                dve.wait_ge(s["h2c_ok"], b + 1)
                if b >= 2:
                    dve.wait_ge(s[f"scat{b % 2}"], 16 * NT * TOPK * (b // 2))
                v.tensor_tensor(rec[:, b % 2, :, 0, 0:D], h2c[:], mod_bc[:, b, 2:3].to_broadcast([P, NT, D]),
                                ALU.add).then_inc(s["h2_ok"], 1)

            def choose(b):
                dve.wait_ge(s["lg_ps"], b + 1)
                if b >= 1:
                    dve.wait_ge(s["tanh_ok"], b)
                    dve.wait_ge(s["rank_ps"], b)
                lg = w_ps[:, LG:LG + NT * NE].rearrange("p (t e) -> p t e", e=NE)
                for i in range(NT):
                    last = v.max(top[:, i], lg[:, i])
                last.then_inc(s["choose_step"], 1)
                dve.wait_ge(s["choose_step"], 3 * b + 1)
                for i in range(NT):
                    last = v.max_index(topi[:, i], top[:, i], lg[:, i])
                last.then_inc(s["choose_step"], 1)
                v.tensor_tensor(gap[:], top[:, :, 0], top[:, :, 1], ALU.subtract).then_inc(s["gap_ok"], 1)
                dve.wait_ge(s["choose_step"], 3 * b + 2)
                for k in range(TOPK):
                    last = v.tensor_tensor(onehot[:, :, k, :],
                                           cst[:, C_EXP:C_EXP + NE].unsqueeze(1).to_broadcast([P, NT, NE]),
                                           topi[:, :, k:k + 1].to_broadcast([P, NT, NE]), ALU.is_equal)
                last.then_inc(s["choose_step"], 1)
                dve.wait_ge(s["choose_step"], 3 * b + 3)
                v.tensor_tensor(sel16[:], onehot[:, :, 0], onehot[:, :, 1], ALU.add).then_inc(s["sel_ok"], 1)

            def place(b):
                dve.wait_ge(s["rank_ps"], b + 1)
                v.tensor_tensor(pos[:], w_ps[:, RK:RK + NT * NE].rearrange("p (t e) -> p t e", e=NE),
                                cst[:, C_BASE:C_BASE + NE].unsqueeze(1).to_broadcast([P, NT, NE]), ALU.add).then_inc(s["pos_ok"], 1)
                v.tensor_reduce(selsum[:], sel16[:].rearrange("p t e -> p e t"), AX.X, ALU.add).then_inc(s["selsum_ok"], 1)
                if b >= 2:
                    dve.wait_ge(s[f"scat{b % 2}"], 16 * NT * TOPK * (b // 2))
                if b == 0:
                    dve.wait_ge(s["ld_dest"], 16)
                dve.wait_ge(s["tanh_ok"], b + 1)
                for k, sign in enumerate((0.5, -0.5)):
                    last = v.tensor_scalar(rec[:, b % 2, :, k, D], tanh_gap[:], sign, 0.5, ALU.mult, ALU.add)
                last.then_inc(s["weight_ok"], 1)
                v.tensor_copy(rec[:, b % 2, :, :, D + 1].bitcast(I32), dest_sb[:, b * NT:(b + 1) * NT, :])
                dve.wait_ge(s["pos_ok"], b + 1)
                v.tensor_tensor(posk[:], onehot[:], pos[:].unsqueeze(2).to_broadcast([P, NT, TOPK, NE]), ALU.mult).then_inc(s["posk_ok"], 1)
                dve.wait_ge(s["selsum_ok"], b + 1)
                v.tensor_tensor(carry[:], carry[:], selsum[:], ALU.add).then_inc(s["carry_ok"], 1)
                dve.wait_ge(s["posk_ok"], b + 1)
                with nc.allow_low_precision(reason="row numbers, whole and below 2**24"):
                    v.tensor_reduce(slot[:, b % 2], posk[:], AX.X, ALU.add).then_inc(s["slot_ok"], 1)
                dve.wait_ge(s["carry_ok"], b + 2)
                v.tensor_copy(carry16[:], carry[:]).then_inc(s["carry16_ok"], 1)

            v.memset(ones16[:], 1.0).then_inc(s["ones_ok"], 1)
            dve.wait_ge(s["ones_ok"], 1)
            v.tensor_copy(ones_r[:], ones16[0:LOW + 1]).then_inc(s["onesr_ok"], 1)
            v.memset(carry[:], 0.0).then_inc(s["carry_ok"], 1)
            v.memset(carry16[:], 0.0).then_inc(s["carry16_ok"], 1)
            v.memset(nt_one[:], 1.0).then_inc(s["ones_ok"], 1)
            stats(0)
            norm(0)
            dve.wait_ge(s["wq_hi_ok"], 1)
            v.tensor_tensor(wq_lo[:], watt_sb[:, W_QKV:W_QKV + 3 * D], wq_hi[:].bitcast(F32), ALU.subtract).then_inc(s["wq_ok"], 1)
            dve.wait_ge(s["bias_hi"], 1)
            v.tensor_tensor(bias_parts[LOW:LOW + 1], bias_in[LOW:LOW + 1], bias_parts[LOW:LOW + 1].bitcast(F32),
                            ALU.subtract).then_inc(s["bias_ok"], 1)
            dve.wait_ge(s["modcol_ps"], 1)
            cols = m_ps[:, 0:4 * B].rearrange("p (n c b) -> p n c b", n=2, c=2)
            v.tensor_copy(mcol[:, :, 0], cols[:, :, 0]).then_inc(s["mcol_ok"], 1)
            v.tensor_scalar_add(mcol[:, :, 1], cols[:, :, 1], 1.0).then_inc(s["mcol_ok"], 1)

            def modulation_rows():
                dve.wait_ge(s["ld_rows"], 16)
                v.tensor_copy(sel_r[:].rearrange("r b p -> r (b p)"), row_sb[:, R_SEL:R_SEL + B * P]).then_inc(s["sel_r_ok"], 1)
                dve.wait_ge(s["mod4_ok"], 1)
                gates = mod4[:, 0:4:3]
                v.tensor_scalar(mod_sgn[:], gates, 0.0, 0.5, ALU.is_ge, ALU.subtract).then_inc(s["row_step"], 1)
                v.scalar_tensor_tensor(out=mod_mag[:], in0=gates, scalar=-1.0, in1=gates, op0=ALU.mult,
                                       op1=ALU.max).then_inc(s["row_step"], 1)
                v.tensor_scalar_add(mod_row[:, 1], mod4[:, 2], 1.0)
                v.tensor_copy(mod_row[:, 2], mod4[:, 1])
                dve.wait_ge(s["row_step"], 2)
                v.tensor_scalar(mod_mag[:], mod_mag[:], 0.25, 2.0, ALU.max, ALU.mult).then_inc(s["row_step"], 1)
                dve.wait_ge(s["row_step"], 3)
                v.tensor_tensor(mod_mag[:], mod_sgn[:], mod_mag[:], ALU.mult).then_inc(s["row_step"], 1)
                dve.wait_ge(s["row_step"], 4)
                dve.wait_ge(s["ld_vec"], 16)
                v.tensor_tensor(mod_row[:, 0], mod_mag[:, 0], vec_sb[:, 0:D], ALU.mult)
                v.tensor_tensor(mod_row[:, 3:5], mod_mag[:, 1:2].to_broadcast([SEL, 2, D]),
                                vec_sb[:, D:3 * D].rearrange("b (r d) -> b r d", d=D), ALU.mult).then_inc(s["row_step"], 1)
                dve.wait_ge(s["row_step"], 5)
                v.tensor_copy(row_parts[:], mod_row[:]).then_inc(s["row_step"], 1)
                dve.wait_ge(s["row_step"], 6)
                v.tensor_tensor(row_parts[LOW:SEL], mod_row[LOW:SEL], row_parts[LOW:SEL].bitcast(F32),
                                ALU.subtract).then_inc(s["row_parts_ok"], 1)
                v.tensor_copy(up16[:], cst[:, C_UP:C_UP + P]).then_inc(s["up_ok"], 1)

            pipeline(B, [(5, gate_out), (4, keys), (6, choose), (5, residual), (4, summary),
                         (3, only(0, modulation_rows)), (5, stats2), (3, low_part), (0, later(stats)),
                         (4, divide), (6, place), (5, norm2), (1, later(norm)), (3, rotate(0)),
                         (5, record_rows), (3, rotate(1))])

            dve.wait_ge(s["cnt_ps"], 1)
            v.tensor_copy(cnt_i[:], w_ps[0:1, CNT:CNT + NE]).then_inc(s["cnt_ok"], 1)
            v.tensor_scalar_add(cnt_p[:], w_ps[0:1, CNT:CNT + NE], float(P - 1)).then_inc(s["nt_ok"], 1)
            dve.wait_ge(s["nt_ok"], 1)
            v.tensor_single_scalar(nt_i[:], cnt_p[:], 7, ALU.arith_shift_right).then_inc(s["nt_ok"], 1)
            dve.wait_ge(s["nt_ok"], 2)
            v.tensor_copy(nt_f[:], nt_i[:]).then_inc(s["nt_ok"], 1)
            dve.wait_ge(s["nt_ok"], 3)
            v.tensor_tensor_scan(nt_cum[:], nt_one[:], nt_f[:], 0.0, ALU.mult, ALU.add).then_inc(s["nt_ok"], 1)
            dve.wait_ge(s["nt_ok"], 4)
            tiles = row_sb[0:1, R_TILE:R_TILE + TAB * NE].rearrange("p (j e) -> p j e", e=NE)
            v.tensor_tensor(past[:], tiles, nt_cum[:].unsqueeze(1).to_broadcast([1, TAB, NE]), ALU.is_ge).then_inc(s["table_step"], 1)
            dve.wait_ge(s["table_step"], 1)
            v.tensor_tensor(pastn[:], past[:], nt_f[:].unsqueeze(1).to_broadcast([1, TAB, NE]), ALU.mult).then_inc(s["table_step"], 1)
            v.tensor_reduce(ex_f[:], past[:], AX.X, ALU.add).then_inc(s["table_step"], 1)
            dve.wait_ge(s["table_step"], 2)
            v.tensor_reduce(before[:], pastn[:], AX.X, ALU.add).then_inc(s["table_step"], 1)
            dve.wait_ge(s["table_step"], 3)
            v.tensor_scalar(tile_tab[:, 0], ex_f[:], float(NE - 1), None, ALU.min)
            v.tensor_scalar(row_f[:], ex_f[:], float(REGION), None, ALU.mult).then_inc(s["table_step"], 1)
            dve.wait_ge(s["table_step"], 4)
            v.tensor_tensor(ahead[:], tiles[:, :, 0], before[:], ALU.subtract).then_inc(s["table_step"], 1)
            dve.wait_ge(s["table_step"], 6)
            dve.wait_ge(s["table_step"], 5)
            v.scalar_tensor_tensor(out=row_f[:], in0=ahead[:], scalar=float(P), in1=row_f[:], op0=ALU.mult,
                                   op1=ALU.add).then_inc(s["table_step"], 1)
            dve.wait_ge(s["table_step"], 7)
            v.tensor_scalar(tile_tab[:, 1], row_f[:], float(DEAD_ROW), None, ALU.min).then_inc(s["tab_ok"], 1)

            for e in range(W_POOL, NE):
                dve.wait_ge(s["w_hi"], e + 1)
                v.tensor_tensor(w_parts[:, e, :, 1], w_in[:, e % W_RING], w_parts[:, e, :, 0].bitcast(F32), ALU.subtract).then_inc(s["w_lo2"], 1)

            dve.wait_ge(s["beta_ok"], 1)
            for b in range(B):
                rows_b = x_sb[:, b * NT:(b + 1) * NT, :]
                last = v.tensor_tensor(rows_b, rows_b, beta_bc[:, b:b + 1].to_broadcast([P, NT, D]), ALU.add)
            last.then_inc(s["xb_ok"], 1)

            def x_low(j):
                dve.wait_ge(s["xT_hi"], j + 1)
                v.tensor_tensor(xT[:, j % 2, 1, :], xT_bank[j % 2][:, 0:P], xT[:, j % 2, 0, :].bitcast(F32),
                                ALU.subtract).then_inc(s["xT_ok"], 1)

            def hidden(j):
                dve.wait_ge(s["gact_ok"], j + 1)
                if j >= 2:
                    dve.wait_ge(s["hidT_ps"], j - 1)
                v.scalar_tensor_tensor(out=hid[:, j % 2, :], in0=gact[:, j % 2, :], scalar=xt[:, j % RING, D:D + 1],
                                       in1=g_bank[j % 2][:, FF:2 * FF], op0=ALU.mult, op1=ALU.mult).then_inc(s["hid_ok"], 1)

            def hid_low(j):
                dve.wait_ge(s["hidT_hi"], j + 1)
                v.tensor_tensor(hidT[:, j % 2, 1, :], hT_bank[j % 2][:, 0:FF], hidT[:, j % 2, 0, :].bitcast(F32),
                                ALU.subtract).then_inc(s["hidT_ok"], 1)

            def y_sum(j):
                dve.wait_ge(s["y_ps"], j + 1)
                if j >= Y_RING:
                    dve.wait_ge(y_out[j % Y_RING], 16 * (j // Y_RING))
                v.tensor_reduce(yrow[:, j % Y_RING, :], y_bank[j % 2][:, 0:2 * D].rearrange("p (c d) -> p d c", c=2), AX.X,
                                ALU.add).then_inc(s["yrow_ok"], 1)

            pipeline(TILES, [(STAGES, y_sum), (0, x_low), (1, hidden), (2, hid_low)])

            def sum_rows(b):
                dve.wait_ge(ld_y[b], 32)
                v.tensor_tensor(ysum[b], yk[b][:, 0], yk[b][:, 1], ALU.add).then_inc(s["ysum_ok"], 1)

            def moments(b):
                dve.wait_ge(s["ysum_ok"], b + 1)
                for i in range(NT):
                    last = v.bn_stats(st3[:, b, i], ysum[b][:, i])
                last.then_inc(s["moments3"], 1)

            def mean_var(b):
                dve.wait_ge(s["moments3"], b + 1)
                for i in range(NT):
                    last = v.bn_aggr(mv3[:, b, i], st3[:, b, i])
                last.then_inc(s["mv3_ok"], 1)

            def finish(b):
                dve.wait_ge(s["z3_ok"], b + 1)
                if b >= 2:
                    dve.wait_ge(s["res_ok"], b - 1)
                v.tensor_tensor(fin[:, b % 2], z3[:, b % 2], mod_bc[:, b, 3:4].to_broadcast([P, NT, D]),
                                ALU.mult).then_inc(s["fin_ok"], 1)

            def var_eps(b):
                dve.wait_ge(s["mv3_ok"], b + 1)
                v.tensor_single_scalar(nm3[:, b], mv3[:, b, :, 0], -1.0, ALU.mult)
                v.tensor_scalar_add(ve3[:, b], mv3[:, b, :, 1], LN_EPS).then_inc(s["ve3_ok"], 1)

            pipeline(B, [(0, sum_rows), (1, mean_var), (1, var_eps), (0, moments), (2, finish)])
            dve.wait_ge(s["fin_ok"], B)
            v.tensor_tensor(res[B - 1], fin[:, (B - 1) % 2], x_sb[:, (B - 1) * NT:B * NT, :], ALU.add).then_inc(s["last_ok"], 1)

        @block.tensor
        def _(pe):
            mm = nc.tensor.matmul
            turn = nc.tensor.transpose
            pe.wait_ge(s["ld_mod"], 16)
            pe.wait_ge(s["scond_ok"], 1)
            for n, r in enumerate((0, 1, 3, 4)):
                last = mm(m_ps[:, n * B:(n + 1) * B], wmod_sb[:, r * D:(r + 1) * D], scond[:, 0:B], start=True, stop=True)
            last.then_inc(s["modcol_ps"], 1)
            mm(n_ps[0:SEL, :], scond[:], wmod_sb[:, 2 * D:6 * D], start=True, stop=True).then_inc(s["mod4_ps"], 1)

            def turn_z(b):
                pe.wait_ge(s["ld_cst"], 16)
                if b >= 1:
                    pe.wait_ge(s["qfT_ok"], b)
                for i in range(NT):
                    pe.wait_ge(s["z_ok"], b * NT + i + 1)
                    last = turn(ta_ps[:, i * P:(i + 1) * P], z[:, b % 2, i], ident)
                last.then_inc(s["zT_ps"], 1)

            def modulation_rows():
                pe.wait_ge(s["row_parts_ok"], 1)
                pe.wait_ge(s["sel_r_ok"], 1)
                rows4 = row_parts[:, 0:4].rearrange("b r d -> b (r d)")
                for b, ps in enumerate((w_ps, n_ps, tb_ps, w_ps)):
                    if ps is w_ps and b > 0:
                        pe.wait_ge(s["modbc_ok"], 1)
                    mm(ps[:], sel_r[:, b], rows4, start=True, stop=True).then_inc(s["modbc_ps"], 1)

            def project(half):
                def stage(b):
                    pe.wait_ge(s["hT_ok"], b + 1)
                    pe.wait_ge(s["wq_ok"], 1)
                    pe.wait_ge(s["bias_ok"], 1)
                    pe.wait_ge(s["onesr_ok"], 1)
                    for i in (2 * half, 2 * half + 1):
                        n = b * NT + i
                        if n >= QB:
                            pe.wait_ge(s["qkv_ok"], n - QB + 1)
                        hi, lo = (part[:, b % 2, i * P:(i + 1) * P] for part in (hT_hi, hT_lo))
                        dst = qkv_bank[n % QB][:, 0:QKV]
                        mm(dst, ones_r[:], bias_parts[:, 0:QKV], start=True, stop=False)
                        mm(dst, hi, wq_hi[:], start=False, stop=False)
                        mm(dst, hi, wq_lo[:], start=False, stop=False)
                        mm(dst, lo, wq_hi[:], start=False, stop=True).then_inc(s["qkv_ps"], 1)
                return stage

            def turn_q(b):
                pe.wait_ge(s["rot_ok"], 2 * b + 2)
                pe.wait_ge(s["hf_ok"], b + 1)
                for i in range(NT):
                    last = turn(ta_ps[:, i * P:(i + 1) * P], ra[:, b % 2, i, 0], ident)
                last.then_inc(s["qT_ps"], 1)

            def keys_values(b):
                pe.wait_ge(s["kf_ok"], b + 1)
                pe.wait_ge(s["qkv_ok"], NT * (b + 1))
                pe.wait_ge(s["mcol_ok"], 2)
                if b >= 1:
                    pe.wait_ge(s["den_ok"], b)
                for i in range(NT):
                    last = mm(m_ps[:, VK:VK + D + 1], kf[:, b % 2, i], qkv_sb[:, b % 2, i, 2 * D:QKV + 1], start=(i == 0), stop=(i == NT - 1))
                last.then_inc(s["vk_ps"], 1)

            def attend(b):
                pe.wait_ge(s["kv_ok"], b + 1)
                pe.wait_ge(s["qfT_ok"], b + 1)
                if b == 0:
                    pe.wait_ge(s["modbc_ok"], 2)
                else:
                    pe.wait_ge(s["o_ok"], b)
                for i in range(NT):
                    qi = qfT[:, b % 2, i * P:(i + 1) * P]
                    mm(n_ps[:, i * D:(i + 1) * D], qi, kv[:, b % 2, 0:D], start=True, stop=True)
                    last = mm(m_ps[:, DEN + i * H:DEN + (i + 1) * H], qi, kv[:, b % 2, D:D + H], start=True, stop=True)
                last.then_inc(s["res_ps"], 1)

            def turn_attn(b):
                pe.wait_ge(s["attn_ok"], b + 1)
                if b == 0:
                    pe.wait_ge(s["modbc_ok"], 3)
                elif b == 1:
                    pe.wait_ge(s["attnT_ok"], 1)
                else:
                    pe.wait_ge(s["h2T_ok"], b - 1)
                for i in range(NT):
                    last = turn(tb_ps[:, i * P:(i + 1) * P], attn[:, b % 2, i], ident)
                last.then_inc(s["aT_ps"], 1)

            def project_out(b):
                pe.wait_ge(s["attnT_ok"], b + 1)
                bias = bias_parts[:, 3 * D:4 * D].unsqueeze(1).to_broadcast([LOW + 1, NT, D])
                mm(n_ps[:], ones_r[:], bias, start=True, stop=False)
                for i in range(NT):
                    oi = n_ps[:, i * D:(i + 1) * D]
                    last = mm(oi, attnT[:, b % 2, i * P:(i + 1) * P], watt_sb[:, W_OUT:W_OUT + D], start=False, stop=(i == NT - 1))
                last.then_inc(s["o_ps"], 1)

            def turn_z2(b):
                pe.wait_ge(s["attnT_ok"], min(b + 2, B))
                for i in range(NT):
                    pe.wait_ge(s["z2_ok"], b * NT + i + 1)
                    last = turn(tb_ps[:, i * P:(i + 1) * P], z2[:, b % 2, i], ident)
                last.then_inc(s["h2T_ps"], 1)

            def route(b):
                pe.wait_ge(s["h2T_ok"], b + 1)
                if b == 0:
                    pe.wait_ge(s["modbc_ok"], B)
                else:
                    pe.wait_ge(s["pos_ok"], b)
                for i in range(NT):
                    last = mm(w_ps[:, LG + i * NE:LG + (i + 1) * NE], h2T[:, b % 2, i * P:(i + 1) * P],
                              watt_sb[:, W_ROUTER:W_ROUTER + NE], start=True, stop=True)
                last.then_inc(s["lg_ps"], 1)

            def rank(b):
                pe.wait_ge(s["sel_ok"], b + 1)
                pe.wait_ge(s["up_ok"], 1)
                pe.wait_ge(s["ones_ok"], 1)
                pe.wait_ge(s["carry16_ok"], b + 1)
                rk = w_ps[:, RK:RK + NT * NE].rearrange("p (t e) -> p t e", e=NE)
                mm(rk, up16[:], sel16[:], start=True, stop=False)
                for d in range(1, NT):
                    mm(rk[:, d:], ones16[:], sel16[:, 0:NT - d], start=False, stop=False)
                mm(rk, ones16[:], carry16[:].unsqueeze(1).to_broadcast([P, NT, NE]), start=False, stop=True).then_inc(s["rank_ps"], 1)

            pipeline(B, [(5, project_out), (6, route), (4, turn_q), (4, keys_values), (6, rank), (3, turn_z),
                         (4, attend), (3, project(0)), (4, turn_attn), (5, turn_z2), (3, project(1)),
                         (3, only(0, modulation_rows))])
            pe.wait_ge(s["h2T_ok"], B)
            pe.wait_ge(s["attnT_ok"], B)
            for b in range(B):
                last = mm(tb_ps[:, b * P:(b + 1) * P], sel_r[:, b], row_parts[:, 4], start=True, stop=True)
            last.then_inc(s["beta_ps"], 1)
            pe.wait_ge(s["carry16_ok"], B + 1)
            mm(w_ps[:, CNT:CNT + NE], ones16[:], carry16[:], start=True, stop=True).then_inc(s["cnt_ps"], 1)

            pe.wait_ge(s["tab_ok"], 1)
            pe.wait_ge(s["beta_ok"], 1)
            pe.wait_ge(s["w_lo"], W_POOL)
            pe.wait_ge(s["w_lo2"], NE - W_POOL)

            def x_turn(j):
                pe.wait_ge(ld_tile[j % RING], 16 * (j // RING) + 16)
                if j >= 2:
                    pe.wait_ge(s["xT_ok"], j - 1)
                turn(xT_bank[j % 2][:, 0:P], xt[:, j % RING, 0:D], ident).then_inc(s["xT_ps"], 1)

            def gate_up(j):
                if j % GROUP == 0:
                    experts.extend(table_values(mybir.EngineType.PE, tile_tab[0:1, 0, j:j + GROUP], NE - 1))
                e = bass.ds(experts[j], 1)
                pe.wait_ge(s["xT_ok"], j + 1)
                if j >= 2:
                    pe.wait_ge(s["hid_ok"], j - 1)
                for n, (part, w_part) in enumerate(((0, 0), (0, 1), (1, 0))):
                    last = mm(g_bank[j % 2][:], xT[:, j % 2, part, :], w_parts[:, e, 0:2 * FB, w_part], start=(n == 0), stop=(n == 2))
                last.then_inc(s["gu_ps"], 1)

            def hid_turn(j):
                pe.wait_ge(s["hid_ok"], j + 1)
                if j >= 2:
                    pe.wait_ge(s["hidT_ok"], j - 1)
                for f in range(FB):
                    last = turn(hT_bank[j % 2][:, f * P:(f + 1) * P], hid[:, j % 2, f * P:(f + 1) * P], ident)
                last.then_inc(s["hidT_ps"], 1)

            def down(j):
                e = bass.ds(experts[j], 1)
                pe.wait_ge(s["hidT_ok"], j + 1)
                if j >= 2:
                    pe.wait_ge(s["yrow_ok"], j - 1)
                y = y_bank[j % 2]
                high, low = (lambda f, part=part: hidT[:, j % 2, part, f * P:(f + 1) * P] for part in range(2))
                mm(y[:, 0:2 * D], high(0), w_parts[:, e, 2 * FB, :], start=True, stop=False)
                for f in range(FB):
                    mm(y[:, 0:D], low(f), w_parts[:, e, 2 * FB + f, 0], start=False, stop=False)
                last = mm(y[:, 0:2 * D], high(1), w_parts[:, e, 2 * FB + 1, :], start=False, stop=True)
                last.then_inc(s["y_ps"], 1)

            experts = []
            pipeline(TILES, [(0, x_turn), (1, gate_up), (2, hid_turn), (3, down)])


def _shape_constants():
    import numpy as np
    c = np.zeros((P, C_ALL), np.float32)
    r = np.arange(P)
    c[:, C_ID:C_ID + P] = np.eye(P)
    c[:, C_BLK:C_BLK + D] = r[:, None] // DH == r[None, :] // DH
    c[:, C_HEAD:C_HEAD + H] = r[:, None] // DH == np.arange(H)[None, :]
    c[:, C_UP:C_UP + P] = r[:, None] < r[None, :]
    c[:, C_EXP:C_EXP + NE] = np.arange(NE)
    c[:, C_BASE:C_BASE + NE] = np.arange(NE) * REGION
    inv = (np.float32(1.0) / np.float32(THETA) ** (np.arange(0, DH, 2, dtype=np.float32) / np.float32(DH))).astype(np.float32)
    ang = np.outer(np.arange(L, dtype=np.float32), inv).astype(np.float32)
    cos = np.repeat(np.cos(ang), 2, axis=1)
    sin = np.repeat(np.sin(ang), 2, axis=1)
    sin[:, 0::2] *= -1
    for i in range(NT):
        c[:, C_COS + i * DH:C_COS + (i + 1) * DH] = cos[i * P:(i + 1) * P]
        c[:, C_SIN + i * DH:C_SIN + (i + 1) * DH] = sin[i * P:(i + 1) * P]
    rows = np.zeros((SEL, R_ALL), np.float32)
    for b in range(B):
        for row in (b, LOW + b):
            rows[row, R_SEL + b * P:R_SEL + (b + 1) * P] = 1
    rows[0, R_TILE:] = np.repeat(np.arange(TAB), NE)
    t = np.arange(TOKENS, dtype=np.int32).reshape(TT, P).T
    dests = np.stack([t + k * TOKENS for k in range(TOPK)], axis=-1)
    return c, rows, dests


def kernel(**inputs):
    import numpy as np
    import concourse.bacc as bacc
    from concourse.bass_utils import run_bass_kernel_spmd

    a = {k[3:]: np.asarray(v) for k, v in inputs.items()}
    consts, rows, dests = _shape_constants()
    gate, up, down = a["ffn_w_gate"], a["ffn_w_up"], a["ffn_w_down"]
    arrays = {
        "x": a["attn_x"].reshape(TOKENS, D),
        "watt": np.concatenate([a["attn_Wqkv"].T, a["attn_Wout"].T, a["ffn_w_router"].T], axis=1),
        "wexp": np.concatenate([gate.transpose(2, 0, 1), up.transpose(2, 0, 1),
                                down.reshape(NE, D, FB, P).transpose(3, 0, 2, 1).reshape(P, NE, FB * D)], axis=2),
        "wmod": a["wmod"],
        "cond": a["c"].T,
        "vecs": np.concatenate([a["attn_bqkv"], a["attn_bout"], a["attn_gq"], a["attn_gk"], a["attn_gout"],
                                a["ffn_ln_gamma"], a["ffn_ln_beta"]])[None, :],
        "consts": consts,
        "rows": rows,
        "dests": dests,
    }
    arrays = {k: np.ascontiguousarray(v) for k, v in arrays.items()}
    nc = bacc.Bacc("TRN2", target_bir_lowering=False, num_devices=1)
    aps = {k: nc.dram_tensor(k, v.shape, mybir.dt.from_np(v.dtype), kind="ExternalInput").ap() for k, v in arrays.items()}
    out = nc.dram_tensor("out", (TOKENS, D), mybir.dt.float32, kind="ExternalOutput").ap()
    adaln_block(nc, out=out, **aps)
    r = run_bass_kernel_spmd(nc, [arrays], core_ids=[0])
    return r.results[0]["out"].reshape(B, L, D)
```
